# Optimizing a Trainium2 kernel written in Bass

```python
import numpy as np
import jax
import jax.numpy as jnp

def _softmax(x, axis=-1):
    return jax.nn.softmax(x, axis=axis)

def _gelu(x):
    return jax.nn.gelu(x, approximate=True)

def _silu(x):
    return jax.nn.silu(x)

def _sigmoid(x):
    return jax.nn.sigmoid(x)

def _layernorm(x, axis=-1, eps=1e-05):
    m = jnp.mean(x, axis=axis, keepdims=True)
    v = jnp.var(x, axis=axis, keepdims=True)
    return (x - m) / jnp.sqrt(v + eps)

def _scatter_add(tgt, idx, src, axis=0):
    return tgt.at[idx].add(src)

def _segment_sum(src, seg, n):
    return jax.ops.segment_sum(src, seg, n)
kernel_name = 'mk_recurrent_d2_jaxref_r8_1ae5a8'

def setup_inputs(seed: int=0):
    np.random.seed(seed)
    _w = jnp.asarray

    def _L0_attn_setup():
        import jax, jax.numpy as jnp
        import numpy as np
        import math
        D_MODEL = 256
        N_HEAD = 16
        D_HEAD = D_MODEL // N_HEAD
        B, T = (4, 256)

        def bitlinear(x, w):
            gamma = jnp.maximum(jnp.mean(jnp.abs(w)), 1e-05)
            w_quant = jnp.clip(jnp.round(w / gamma), -1.0, 1.0)
            w_eff = jax.lax.stop_gradient(w_quant - w) + w
            return jnp.matmul(x, w_eff.T) * gamma
        key = jax.random.key(seed)
        kx, kq, kk, kv, ko = jax.random.split(key, 5)
        s = 0.02
        return {'x': jax.random.normal(kx, (B, T, D_MODEL), dtype=jnp.float32), 'wq': jax.random.normal(kq, (D_MODEL, D_MODEL), dtype=jnp.float32) * s, 'wk': jax.random.normal(kk, (D_MODEL, D_MODEL), dtype=jnp.float32) * s, 'wv': jax.random.normal(kv, (D_MODEL, D_MODEL), dtype=jnp.float32) * s, 'wo': jax.random.normal(ko, (D_MODEL, D_MODEL), dtype=jnp.float32) * s}
    _L0_attn_in = _L0_attn_setup()

    def _L0_ffn_setup():
        import jax, jax.numpy as jnp
        import numpy as np
        EPS = 1e-08

        def _quantize(w):
            gamma = jnp.mean(jnp.abs(w))
            return jnp.clip(jnp.round(w / (gamma + EPS)), -1.0, 1.0)

        def _bitlinear(x, w):
            return jnp.matmul(x, _quantize(w).T)
        key = jax.random.key(seed)
        k1, k2, k3, k4 = jax.random.split(key, 4)
        d, h = (256, 704)
        x = jax.random.normal(k1, (4, 256, d), dtype=jnp.float32)
        w1 = jax.random.normal(k2, (h, d), dtype=jnp.float32)
        w2 = jax.random.normal(k3, (h, d), dtype=jnp.float32)
        w3 = jax.random.normal(k4, (d, h), dtype=jnp.float32)
        return {'x': x, 'w1': w1, 'w2': w2, 'w3': w3}
    _L0_ffn_in = _L0_ffn_setup()

    def _L1_attn_setup():
        import jax, jax.numpy as jnp
        import numpy as np
        H = 256
        NH = 16
        HD = H // NH
        SCALE = 1.0 / np.sqrt(HD)
        key = jax.random.key(seed)
        k1, k2, k3 = jax.random.split(key, 3)
        hidden_states = jax.random.normal(k1, (4, 256, H), dtype=jnp.float32)
        W_attn = jax.random.normal(k2, (H, 3 * H), dtype=jnp.float32) * 0.02
        b_attn = jnp.zeros((3 * H,), dtype=jnp.float32)
        W_proj = jax.random.normal(k3, (H, H), dtype=jnp.float32) * 0.02
        b_proj = jnp.zeros((H,), dtype=jnp.float32)
        return {'hidden_states': hidden_states, 'W_attn': W_attn, 'b_attn': b_attn, 'W_proj': W_proj, 'b_proj': b_proj}
    _L1_attn_in = _L1_attn_setup()

    def _L1_ffn_setup():
        import jax, jax.numpy as jnp
        import numpy as np

        def _sparsify_2to4(h):
            B, S, I = h.shape
            g = h.reshape(B, S, I // 4, 4)
            a = jnp.abs(g)
            _, idx = jax.lax.top_k(a, 2)
            pos = jnp.arange(4)
            mask = (pos == idx[..., 0:1]) | (pos == idx[..., 1:2])
            return (g * mask.astype(g.dtype)).reshape(B, S, I)
        key = jax.random.key(seed)
        k1, k2, k3, k4 = jax.random.split(key, 4)
        B, S, H, I = (4, 256, 256, 1024)
        x = jax.random.normal(k1, (B, S, H), dtype=jnp.float32)
        w_gate = jax.random.normal(k2, (H, I), dtype=jnp.float32) / np.sqrt(H)
        w_up = jax.random.normal(k3, (H, I), dtype=jnp.float32) / np.sqrt(H)
        w_down = jax.random.normal(k4, (I, H), dtype=jnp.float32) / np.sqrt(I)
        return {'x': x, 'w_gate': w_gate, 'w_up': w_up, 'w_down': w_down}
    _L1_ffn_in = _L1_ffn_setup()
    _d = {'L0_attn_x': _L0_attn_in['x'], 'L0_attn_wq': _L0_attn_in['wq'], 'L0_attn_wk': _L0_attn_in['wk'], 'L0_attn_wv': _L0_attn_in['wv'], 'L0_attn_wo': _L0_attn_in['wo'], 'L0_ffn_w1': _L0_ffn_in['w1'], 'L0_ffn_w2': _L0_ffn_in['w2'], 'L0_ffn_w3': _L0_ffn_in['w3'], 'L1_attn_W_attn': _L1_attn_in['W_attn'], 'L1_attn_b_attn': _L1_attn_in['b_attn'], 'L1_attn_W_proj': _L1_attn_in['W_proj'], 'L1_attn_b_proj': _L1_attn_in['b_proj'], 'L1_ffn_w_gate': _L1_ffn_in['w_gate'], 'L1_ffn_w_up': _L1_ffn_in['w_up'], 'L1_ffn_w_down': _L1_ffn_in['w_down']}
    _x0 = _d['L0_attn_x']
    _d['L0_attn_x'] = jax.random.normal(jax.random.fold_in(jax.random.key(seed), 1), (4, 1024, 256), dtype=_x0.dtype)
    del _x0
    return _d

def reference(L0_attn_x, L0_attn_wq, L0_attn_wk, L0_attn_wv, L0_attn_wo, L0_ffn_w1, L0_ffn_w2, L0_ffn_w3, L1_attn_W_attn, L1_attn_b_attn, L1_attn_W_proj, L1_attn_b_proj, L1_ffn_w_gate, L1_ffn_w_up, L1_ffn_w_down):

    def _L0_attn_ref(x, wq, wk, wv, wo):
        import jax, jax.numpy as jnp
        import numpy as np
        import math
        D_MODEL = 256
        N_HEAD = 16
        D_HEAD = D_MODEL // N_HEAD
        B, T = (4, 256)

        def bitlinear(x, w):
            gamma = jnp.maximum(jnp.mean(jnp.abs(w)), 1e-05)
            w_quant = jnp.clip(jnp.round(w / gamma), -1.0, 1.0)
            w_eff = jax.lax.stop_gradient(w_quant - w) + w
            return jnp.matmul(x, w_eff.T) * gamma
        b, t, c = x.shape

        def split_heads(y):
            return y.reshape(b, t, N_HEAD, D_HEAD).transpose(0, 2, 1, 3)
        q = split_heads(bitlinear(x, wq))
        k = split_heads(bitlinear(x, wk))
        v = split_heads(bitlinear(x, wv))
        scale = 1.0 / math.sqrt(D_HEAD)
        scores = jnp.einsum('bhqd,bhkd->bhqk', q, k) * scale
        causal = jnp.tril(jnp.ones((t, t), dtype=bool))
        scores = jnp.where(causal, scores, jnp.finfo(scores.dtype).min)
        attn = jax.nn.softmax(scores, axis=-1)
        out = jnp.einsum('bhqk,bhkd->bhqd', attn, v)
        out = out.transpose(0, 2, 1, 3).reshape(b, t, c)
        return bitlinear(out, wo)

    def _L0_ffn_ref(x, w1, w2, w3):
        import jax, jax.numpy as jnp
        import numpy as np
        EPS = 1e-08

        def _quantize(w):
            gamma = jnp.mean(jnp.abs(w))
            return jnp.clip(jnp.round(w / (gamma + EPS)), -1.0, 1.0)

        def _bitlinear(x, w):
            return jnp.matmul(x, _quantize(w).T)
        x1 = _bitlinear(x, w1)
        x2 = _bitlinear(x, w2)
        hidden = jax.nn.sigmoid(x1) * x2
        return _bitlinear(hidden, w3)

    def _L1_attn_ref(hidden_states, W_attn, b_attn, W_proj, b_proj):
        import jax, jax.numpy as jnp
        import numpy as np
        H = 256
        NH = 16
        HD = H // NH
        SCALE = 1.0 / np.sqrt(HD)
        B, S, _ = hidden_states.shape
        qkv = hidden_states @ W_attn + b_attn
        q, k, v = jnp.split(qkv, 3, axis=-1)

        def split_heads(t):
            return t.reshape(B, S, NH, HD).transpose(0, 2, 1, 3)
        q, k, v = (split_heads(q), split_heads(k), split_heads(v))
        scores = jnp.einsum('bhqd,bhkd->bhqk', q, k) * SCALE
        causal = jnp.tril(jnp.ones((S, S), dtype=bool))
        scores = jnp.where(causal, scores, jnp.finfo(scores.dtype).min)
        attn = jax.nn.softmax(scores, axis=-1)
        out = jnp.einsum('bhqk,bhkd->bhqd', attn, v)
        out = out.transpose(0, 2, 1, 3).reshape(B, S, H)
        out = out @ W_proj + b_proj
        return out

    def _L1_ffn_ref(x, w_gate, w_up, w_down):
        import jax, jax.numpy as jnp
        import numpy as np

        def _sparsify_2to4(h):
            B, S, I = h.shape
            g = h.reshape(B, S, I // 4, 4)
            a = jnp.abs(g)
            _, idx = jax.lax.top_k(a, 2)
            pos = jnp.arange(4)
            mask = (pos == idx[..., 0:1]) | (pos == idx[..., 1:2])
            return (g * mask.astype(g.dtype)).reshape(B, S, I)
        h = jax.nn.silu(jnp.einsum('bsh,hi->bsi', x, w_gate)) * jnp.einsum('bsh,hi->bsi', x, w_up)
        h_sparse = _sparsify_2to4(h)
        return jnp.einsum('bsi,ih->bsh', h_sparse, w_down)
    x = L0_attn_x
    xn = _layernorm(x, axis=-1)
    s = _L0_attn_ref(xn, L0_attn_wq, L0_attn_wk, L0_attn_wv, L0_attn_wo)
    g = _silu(_L0_ffn_ref(xn, L0_ffn_w1, L0_ffn_w2, L0_ffn_w3))
    x = x + s * g
    xn = _layernorm(x, axis=-1)
    s = _L1_attn_ref(xn, L1_attn_W_attn, L1_attn_b_attn, L1_attn_W_proj, L1_attn_b_proj)
    g = _silu(_L1_ffn_ref(xn, L1_ffn_w_gate, L1_ffn_w_up, L1_ffn_w_down))
    x = x + s * g
    return x

_drawn_inputs = setup_inputs


def setup_inputs(seed=0):
    import zlib

    import numpy as np

    out = dict(_drawn_inputs(seed))
    spreads = {'L1_attn_b_attn': (0.0, 0.8), 'L1_attn_b_proj': (0.0, 0.284)}
    factors = {'L1_attn_W_attn': 8.0, 'L1_attn_W_proj': 5.065}
    for name, (base, spread) in spreads.items():
        noise = np.random.default_rng([zlib.crc32(name.encode()), seed]).standard_normal(out[name].shape)
        drawn = base * np.exp(spread * noise) if base else spread * noise
        out[name] = jnp.asarray(drawn.astype(out[name].dtype))
    for name, factor in factors.items():
        out[name] = (out[name] * factor).astype(out[name].dtype)
    return out
```

```python
from contextlib import ExitStack

import concourse.bass as bass
from concourse import mybir

F32 = mybir.dt.float32
F32R = mybir.dt.float32r
BF16 = mybir.dt.bfloat16
ALU = mybir.AluOpType
ACT = mybir.ActivationFunctionType
AX = mybir.AxisListType

P = 128
BANK = 512
B, T, D = 4, 1024, 256
HEADS, DH = 16, 16
KI = D // P
TILES = T // P
HG = 4
GROUPS = HEADS // HG
HC = P // DH
VW = 32
HID = (704, 1024)
EPS_LN = 1e-5
NEG = -1e30
LOWEST = -3e38
SPLITS = 96
MAXROWS = 3
Q_PARTS = (0, 0, 0, 1, 1, 2)
K_PARTS = (0, 1, 2, 0, 1, 0)
C_IDENT, C_TRI, C_MAXMASK = 0, 128, 256
C_END = C_MAXMASK + BANK
S_QB, S_KB, S_VB, S_PB = 0, KI, 2 * KI, 2 * KI + D
S_END = 2 * KI + 2 * D


BASE = 512


def semaphore(nc, known, name):
    if name not in known:
        known[name] = nc.alloc_semaphore(name)
    return known[name]


def split_weights(nc, name, raw_dram, width, high, low):
    with ExitStack() as ctx:
        raw = ctx.enter_context(nc.sbuf_tensor(f"{name}_raw", [P, width], F32))
        loaded = nc.alloc_semaphore(f"{name}_loaded")
        high_done = nc.alloc_semaphore(f"{name}_high_done")
        low_done = nc.alloc_semaphore(f"{name}_low_done")
        block = ctx.enter_context(nc.Block())

        @block.sync
        def _(sp):
            sp.dma_start(raw[:], raw_dram).then_inc(loaded, 16)

        @block.scalar
        def _(act):
            act.wait_ge(loaded, 16)
            nc.scalar.activation(high, raw[:], ACT.Copy).then_inc(high_done, 1)

        @block.vector
        def _(dve):
            dve.wait_ge(high_done, 1)
            nc.vector.tensor_tensor(low, raw[:], high.bitcast(F32), ALU.subtract).then_inc(low_done, 1)
            dve.wait_ge(low_done, 1)


def ternary_weights(nc, name, raw_dram, width, out, pieces, floor, eps, count, gammas):
    with ExitStack() as ctx:
        raw = ctx.enter_context(nc.sbuf_tensor(f"{name}_raw", [P, width], F32))
        loaded = nc.alloc_semaphore(f"{name}_loaded")
        summed = nc.alloc_semaphore(f"{name}_summed")
        totalled = nc.alloc_semaphore(f"{name}_totalled")
        gamma_step = nc.alloc_semaphore(f"{name}_gamma_step")
        above_done = nc.alloc_semaphore(f"{name}_above_done")
        parts_done = nc.alloc_semaphore(f"{name}_parts_done")
        n = len(pieces)
        junk = ctx.enter_context(nc.sbuf_tensor(f"{name}_junk", [P, width], F32))
        sums = ctx.enter_context(nc.sbuf_tensor(f"{name}_sums", [P, n], F32))
        ones = ctx.enter_context(nc.sbuf_tensor(f"{name}_ones", [P, P], F32))
        half = ctx.enter_context(nc.sbuf_tensor(f"{name}_half", [P, 2, n], F32))
        total = ctx.enter_context(nc.psum_tensor(f"{name}_total", [P, BANK], F32))
        block = ctx.enter_context(nc.Block())

        @block.sync
        def _(sp):
            sp.dma_start(raw[:], raw_dram).then_inc(loaded, 16)

        @block.scalar
        def _(act):
            act.wait_ge(loaded, 16)
            for i, (c0, w, _) in enumerate(pieces):
                nc.scalar.activation(junk[:, c0:c0 + w], raw[:, c0:c0 + w], ACT.Abs,
                                     accum_out=sums[:, i:i + 1]).then_inc(summed, 1)

        @block.tensor
        def _(pe):
            pe.wait_ge(summed, n + 1)
            nc.tensor.matmul(total[:, 0:n], ones[:], sums[:], start=True, stop=True).then_inc(totalled, 1)

        @block.vector
        def _(dve):
            nc.vector.memset(ones[:], 1.0).then_inc(summed, 1)
            dve.wait_ge(totalled, 1)
            g0 = pieces[0][2]
            nc.vector.tensor_scalar(gammas[:, g0:g0 + n], total[:, 0:n], 1.0 / count, floor,
                                    ALU.mult, ALU.max).then_inc(gamma_step, 1)
            dve.wait_ge(gamma_step, 1)
            nc.vector.tensor_scalar(half[:, 0], gammas[:, g0:g0 + n], eps, 0.5,
                                    ALU.add, ALU.mult).then_inc(gamma_step, 1)
            nc.vector.tensor_scalar(half[:, 1], gammas[:, g0:g0 + n], eps, -0.5,
                                    ALU.add, ALU.mult).then_inc(gamma_step, 1)
            dve.wait_ge(gamma_step, 3)
            for i, (c0, w, _) in enumerate(pieces):
                nc.vector.tensor_scalar(junk[:, c0:c0 + w], raw[:, c0:c0 + w], half[:, 0, i:i + 1], None,
                                        ALU.is_gt).then_inc(above_done, 1)
            for i, (c0, w, _) in enumerate(pieces):
                dve.wait_ge(above_done, i + 1)
                nc.vector.scalar_tensor_tensor(junk[:, c0:c0 + w], raw[:, c0:c0 + w], half[:, 1, i:i + 1],
                                               junk[:, c0:c0 + w], ALU.is_lt, ALU.subtract).then_inc(above_done, 1)
            dve.wait_ge(above_done, 2 * n)
            nc.vector.tensor_scalar(out, junk[:], -1.0, None, ALU.mult).then_inc(parts_done, 1)


def layer_norm_dve(nc, dve, k, sems, bufs):
    x_loaded, bn_done, stats_done, rstd_done, xn_done, stood_alone, xn_free = sems
    x_in, xn, bn, mv, var_eps, rstd = bufs
    dve.wait_ge(x_loaded, BASE + (k + 1) * 16)
    for i in range(4):
        nc.vector.bn_stats(bn[:, i], x_in[:, i]).then_inc(bn_done, 1)
    for i in range(4):
        if i == 0:
            dve.wait_ge(bn_done, BASE + k * 4 + 4)
            dve.sem_inc(stood_alone, 1)
        nc.vector.bn_aggr(mv[:, i], bn[:, i]).then_inc(stats_done, 1)
    dve.wait_ge(stats_done, BASE + k * 5 + 4)
    nc.vector.tensor_scalar(var_eps[:], mv[:, :, 1], EPS_LN, None, ALU.add).then_inc(stats_done, 1)
    dve.wait_ge(rstd_done, BASE + k + 1)
    dve.wait_ge(xn_free[0], BASE + xn_free[1])
    for i in range(4):
        ins = nc.vector.tensor_scalar(xn[:, i], x_in[:, i], mv[:, i, 0:1], rstd[:, i:i + 1],
                                      ALU.subtract, ALU.mult)
    ins.then_inc(xn_done, 1)


def ffn_pass(nc, known, layer, x_dram, g_dram, w_up_parts, w_down_parts, gammas, consts):
    sparse = layer == 1
    NCH = 4 if sparse else 3
    BLOCKS = B * T // BANK
    BT = BANK // P
    MEMB = [P] * 8 if sparse else [P] * 5 + [HID[0] - 5 * P]
    NW = len(w_up_parts)
    passes = [(0, 0), (0, 1)] + ([(1, 0)] if NW == 2 else [])

    with ExitStack() as ctx:
        def sb(nm, shape, dt):
            return ctx.enter_context(nc.sbuf_tensor(f"f{layer}_{nm}", shape, dt))

        counts = []

        def sem(nm):
            counts.append(semaphore(nc, known, f"ffn_{nm}"))
            return counts[-1]

        x_in = sb("x_in", [P, BT, D], F32)
        xn = sb("xn", [P, BT, D], F32)
        bn = sb("bn", [P, BT, 6], F32)
        mv = sb("mv", [P, BT, 2], F32)
        var_eps = sb("var_eps", [P, BT], F32)
        rstd = sb("rstd", [P, BT], F32)
        minus_half = sb("minus_half", [P, BT], F32)
        xT = [sb(f"xT{i}", [P, KI, BANK], F32R) for i in range(2)]
        act_gate = sb("act_gate", [P, 2, BANK], F32)
        hid = sb("hid", [P, 2, NCH, BANK], F32)
        hT = [sb(f"hT{i}", [P, 2, NCH, BANK], F32R) for i in range(2)]
        sig = sb("sig", [P, 2, BANK], F32)
        g_out = sb("g_out", [P, BT, D], F32)
        if sparse:
            mag = sb("mag", [P, NCH, BANK], F32)
            beats = sb("beats", [P, 6, BANK], BF16)
            votes = sb("votes", [P, 4, BANK], BF16)
            half_votes = sb("half_votes", [P, 4, BANK], BF16)
        ps_up = ctx.enter_context(nc.psum_tensor(f"f{layer}_ps_up", [P, 4, BANK], F32))
        ps_xT = ctx.enter_context(nc.psum_tensor(f"f{layer}_ps_xT", [P, KI, BANK], F32))
        ps_down = ctx.enter_context(nc.psum_tensor(f"f{layer}_ps_down", [P, 2, BANK], F32))

        x_loaded, bn_done, stats_done, rstd_done, xn_done = (
            sem("x_loaded"), sem("bn_done"), sem("stats_done"), sem("rstd_done"), sem("xn_done"))
        half_set, stood_alone = sem("half_set"), sem("stood_alone")
        turned, xT_high, xT_ready = sem("turned"), sem("xT_high"), sem("xT_ready")
        gate_full, up_full, gate_taken, hid_done = sem("gate_full"), sem("up_full"), sem("gate_taken"), sem("hid_done")
        mag_done, beats_done, votes_done, kept = sem("mag_done"), sem("beats_done"), sem("votes_done"), sem("kept")
        high_done, low_done = sem("high_done"), sem("low_done")
        down_done, sig_done, g_done, g_stored = sem("down_done"), sem("sig_done"), sem("g_done"), sem("g_stored")
        block = ctx.enter_context(nc.Block())
        ident = consts[:, C_IDENT:C_IDENT + P]

        def n_par(half, m):
            return (half * NCH + m) % 2

        x_v = x_dram.rearrange("(k i p) d -> k p i d", i=BT, p=P)
        g_v = g_dram.rearrange("(k i p) d -> k p i d", i=BT, p=P)

        def rows(v, k):
            return v[bass.ds(k, 1)].rearrange("o p i d -> p (o i) d")

        @block.sync
        def _(sp):
            for s in counts:
                sp.sem_inc(s, BASE)

            def body(k):
                sp.wait_ge(xn_done, BASE + k)
                sp.dma_start(x_in[:], rows(x_v, k)).then_inc(x_loaded, 16)

            def store(k):
                sp.wait_ge(g_done, BASE + k * 2 + 2)
                sp.dma_start(rows(g_v, k), g_out[:]).then_inc(g_stored, 16)

            body(0)
            body(1)
            with sp.Fori(2, BLOCKS) as k:
                body(k)
                store(k - 2)
            store(BLOCKS - 2)
            store(BLOCKS - 1)
            sp.wait_ge(g_stored, BASE + 16 * BLOCKS)

        @block.gpsimd
        def _(pool):
            nc.gpsimd.memset(minus_half[:], -0.5).then_inc(half_set, 1)
            pool.wait_ge(half_set, BASE + 1)

            def inverse_deviation(k):
                pool.wait_ge(stats_done, BASE + k * 5 + 5)
                nc.gpsimd.tensor_tensor(rstd[:], var_eps[:], minus_half[:], ALU.pow).then_inc(rstd_done, 1)

            def low_parts(k, half):
                for m in range(NCH):
                    n = k * 2 * NCH + half * NCH + m
                    w = MEMB[half * NCH + m]
                    pool.wait_ge(high_done, BASE + n + 1)
                    nc.gpsimd.tensor_tensor(hT[1][0:w, half, m], hid[0:w, half, m], hT[0][0:w, half, m].bitcast(F32),
                                            ALU.subtract).then_inc(low_done, 1)

            inverse_deviation(0)
            low_parts(0, 0)
            inverse_deviation(1)
            low_parts(0, 1)

            def body(k, more):
                low_parts(k, 0)
                if more:
                    inverse_deviation(k + 1)
                low_parts(k, 1)

            with pool.Fori(1, BLOCKS - 1) as k:
                body(k, True)
            body(BLOCKS - 1, False)

        @block.scalar
        def _(act):
            def take_xT(k):
                for ki in range(KI):
                    act.wait_ge(turned, BASE + k * KI + ki + 1)
                    if ki == 0:
                        act.wait_ge(up_full, BASE + k * 2 * NCH)
                    nc.scalar.activation(xT[0][:, ki], ps_xT[:, ki], ACT.Copy).then_inc(xT_high, 1)

            def chunk_gate(k, half, m):
                n = k * 2 * NCH + half * NCH + m
                w = MEMB[half * NCH + m]
                act.wait_ge(gate_full, BASE + n + 1)
                act.wait_ge(hid_done, BASE + n - 1)
                func = ACT.Silu if sparse else ACT.Sigmoid
                nc.scalar.activation(act_gate[0:w, n_par(half, m)], ps_up[0:w, 2 * n_par(half, m)],
                                     func).then_inc(gate_taken, 1)

            def magnitude(k, half, m):
                n = k * 2 * NCH + half * NCH + m
                act.wait_ge(hid_done, BASE + n + 1)
                if m == 0:
                    act.wait_ge(beats_done, BASE + (k * 2 + half) * 6)
                nc.scalar.activation(mag[:, m], hid[:, half, m], ACT.Abs).then_inc(mag_done, 1)

            def high_part(k, half, m):
                n = k * 2 * NCH + half * NCH + m
                w = MEMB[half * NCH + m]
                act.wait_ge(kept if sparse else hid_done, BASE + n + 1)
                if m == 0:
                    act.wait_ge(down_done, BASE + k * 2 + half - 1)
                nc.scalar.activation(hT[0][0:w, half, m], hid[0:w, half, m], ACT.Copy).then_inc(high_done, 1)

            def out_sigmoid(k):
                act.wait_ge(down_done, BASE + k * 2 + 2)
                act.wait_ge(g_done, BASE + k * 2)
                for t in range(2):
                    func = ACT.Silu if sparse else ACT.Sigmoid
                    if sparse and t == 0:
                        act.wait_ge(g_stored, BASE + k * 16)
                    out = g_out[:, 2 * t:2 * t + 2].rearrange("p i d -> p (i d)") if sparse else sig[:, t]
                    ins = nc.scalar.activation(out, ps_down[:, t], func)
                    ins.then_inc(g_done if sparse else sig_done, 1)

            def half_block(k, half):
                for m in range(NCH):
                    chunk_gate(k, half, m)
                    if not sparse and m:
                        high_part(k, half, m - 1)
                if sparse:
                    for m in range(NCH):
                        magnitude(k, half, m)
                    for m in range(NCH):
                        high_part(k, half, m)
                else:
                    high_part(k, half, NCH - 1)

            take_xT(0)
            half_block(0, 0)
            half_block(0, 1)
            with act.Fori(1, BLOCKS) as k:
                take_xT(k)
                half_block(k, 0)
                out_sigmoid(k - 1)
                half_block(k, 1)
            out_sigmoid(BLOCKS - 1)

        ln_sems = (x_loaded, bn_done, stats_done, rstd_done, xn_done, stood_alone)
        ln_bufs = (x_in, xn, bn, mv, var_eps, rstd)

        @block.vector
        def _(dve):
            def norm(k):
                layer_norm_dve(nc, dve, k, ln_sems + ((xT_ready, k * KI),), ln_bufs)

            def low_xT(k):
                for ki in range(KI):
                    dve.wait_ge(xT_high, BASE + k * KI + ki + 1)
                    nc.vector.tensor_tensor(xT[1][:, ki], ps_xT[:, ki], xT[0][:, ki].bitcast(F32),
                                            ALU.subtract).then_inc(xT_ready, 1)

            def hidden(k, half, m):
                n = k * 2 * NCH + half * NCH + m
                w = MEMB[half * NCH + m]
                dve.wait_ge(gate_taken, BASE + n + 1)
                dve.wait_ge(up_full, BASE + n + 1)
                if m == 0:
                    dve.wait_ge(low_done, BASE + (k * 2 + half - 1) * NCH)
                nc.vector.tensor_tensor(hid[0:w, half, m], ps_up[0:w, 2 * n_par(half, m) + 1],
                                        act_gate[0:w, n_par(half, m)], ALU.mult).then_inc(hid_done, 1)

            def two_of_four(k, half):
                q = k * 2 + half
                dve.wait_ge(mag_done, BASE + (q + 1) * NCH)
                dve.wait_ge(kept, BASE + q * NCH)
                pairs = [(0, 1), (0, 2), (0, 3), (1, 2), (1, 3), (2, 3)]
                for c, (i, j) in enumerate(pairs):
                    nc.vector.tensor_tensor(beats[:, c], mag[:, i], mag[:, j], ALU.is_ge).then_inc(beats_done, 1)
                dve.wait_ge(beats_done, BASE + q * 6 + 6)
                first = [(0, 1, ALU.add), (3, 0, ALU.subtract), (5, 1, ALU.subtract), (2, 4, ALU.add)]
                for c, (i, j, op) in enumerate(first):
                    nc.vector.tensor_tensor(half_votes[:, c], beats[:, i], beats[:, j], op).then_inc(votes_done, 1)
                second = [(2, ALU.add), (4, ALU.add), (3, ALU.subtract), (5, ALU.add)]
                dve.wait_ge(votes_done, BASE + q * 8 + 4)
                for c, (j, op) in enumerate(second):
                    nc.vector.tensor_tensor(votes[:, c], half_votes[:, c], beats[:, j], op).then_inc(votes_done, 1)
                keep = [(2.0, ALU.is_ge), (1.0, ALU.is_ge), (0.0, ALU.is_ge), (1.0, ALU.is_le)]
                dve.wait_ge(votes_done, BASE + q * 8 + 8)
                for m, (bound, op) in enumerate(keep):
                    nc.vector.scalar_tensor_tensor(hid[:, half, m], votes[:, m], bound, hid[:, half, m],
                                                   op, ALU.mult).then_inc(kept, 1)

            def half_block(k, half):
                for m in range(NCH):
                    hidden(k, half, m)
                if sparse:
                    two_of_four(k, half)

            def out_gate(k):
                for t in range(2):
                    dve.wait_ge(sig_done, BASE + k * 2 + t + 1)
                    if t == 0:
                        dve.wait_ge(g_stored, BASE + k * 16)
                    nc.vector.tensor_tensor(g_out[:, 2 * t:2 * t + 2].rearrange("p i d -> p (i d)"), ps_down[:, t],
                                            sig[:, t], ALU.mult).then_inc(g_done, 1)

            norm(0)
            low_xT(0)
            half_block(0, 0)
            norm(1)
            half_block(0, 1)

            def body(k, more):
                low_xT(k)
                half_block(k, 0)
                if not sparse:
                    out_gate(k - 1)
                if more:
                    norm(k + 1)
                half_block(k, 1)

            with dve.Fori(1, BLOCKS - 1) as k:
                body(k, True)
            body(BLOCKS - 1, False)
            if not sparse:
                out_gate(BLOCKS - 1)

        @block.tensor
        def _(pe):
            def turn(k):
                for ki in range(KI):
                    if ki == 0:
                        pe.wait_ge(xn_done, BASE + k + 1)
                    pe.wait_ge(xT_ready, BASE + (k - 1) * KI + ki + 1)
                    for i in range(BT):
                        ins = nc.tensor.transpose(ps_xT[:, ki, i * P:(i + 1) * P], xn[:, i, ki * P:(ki + 1) * P], ident)
                    ins.then_inc(turned, 1)

            def up(k, half):
                for m in range(NCH):
                    n = k * 2 * NCH + half * NCH + m
                    w = MEMB[half * NCH + m]
                    if half == 0 and m == 0:
                        pe.wait_ge(xT_ready, BASE + k * KI + KI)
                    for which, taken, full in ((0, gate_taken, gate_full), (1, hid_done, up_full)):
                        pe.wait_ge(taken, BASE + n - 1)
                        out = ps_up[0:w, 2 * n_par(half, m) + which]
                        for ki in range(KI):
                            for c, (wp, xp) in enumerate(passes):
                                ins = nc.tensor.matmul(out, w_up_parts[wp][:, which, ki, half * NCH + m, 0:w],
                                                       xT[xp][:, ki], start=(ki == 0 and c == 0),
                                                       stop=(ki == KI - 1 and c == len(passes) - 1))
                        ins.then_inc(full, 1)

            def down(k, half):
                q = k * 2 + half
                pe.wait_ge(low_done, BASE + (q + 1) * NCH)
                if half == 0:
                    pe.wait_ge(g_done, BASE + k * 2)
                for i in range(BT):
                    for m in range(NCH):
                        w = MEMB[half * NCH + m]
                        for c, (wp, hp) in enumerate(passes):
                            ins = nc.tensor.matmul(
                                ps_down[:, i // 2, (i % 2) * D:(i % 2 + 1) * D], hT[hp][0:w, half, m, i * P:(i + 1) * P],
                                w_down_parts[wp][0:w, half * NCH + m],
                                start=(half == 0 and m == 0 and c == 0 and i % 2 == 0),
                                stop=(half == 1 and m == NCH - 1 and c == len(passes) - 1),
                                skip_group_check=True)
                ins.then_inc(down_done, 1)

            turn(0)
            up(0, 0)
            up(0, 1)
            with pe.Fori(1, BLOCKS) as k:
                turn(k)
                down(k - 1, 0)
                up(k, 0)
                down(k - 1, 1)
                up(k, 1)
            down(BLOCKS - 1, 0)
            down(BLOCKS - 1, 1)



SLOTS = 48
LEAD = 12
NORM_SLOTS = (1, 13)
CONSTS_SET = 4
STEPS = [(0, j) for j in range(4)] + [(1, j) for j in range(8)]
PIECES = [(i, 0) for i in range(4)] + [(i, c) for i in range(4, 8) for c in range(2)]

PROJECT = [[("q", c, 0), ("q", c, 1), ("k", c, 0), ("k", c, 1), ("v", c, 0), ("v", c, 1)] for c in range(KI)]
NORM = [("x", u, ki) for u in range(2) for ki in range(KI)]
OUTS = [("o", 2), ("o", 3)]
TURN_SLOT, BACK_SLOT, HIGH_SLOT = 21, 25, 28
BEHIND = 16


def small_work(last):
    at = [dict() for _ in range(GROUPS)]
    for g in range(GROUPS):
        if g < GROUPS - 1 or not last:
            at[g][40] = ("m", (g + 1) % GROUPS)
    for n, item in enumerate(PROJECT[1]):
        at[0][1 + 3 * n] = item
    at[GROUPS - 1].update({36: ("o", 0), 45: ("o", 1)})
    if not last:
        for n, item in enumerate(NORM):
            at[1][(8, 11, 30, 34)[n]] = item
        for n, item in enumerate(PROJECT[0]):
            at[2][(1, 4, 9, 11, 14, 17)[n]] = item
    return at


def is_ahead(item):
    return item[0] == "x" or (item[0] in "qkv" and item[1] == 0) or item == ("m", 0)


def order_of(last):
    at = small_work(last)
    seq = [at[g][n] for g in range(GROUPS) for n in sorted(at[g])]
    return seq + OUTS


FIRST = NORM + PROJECT[0] + [("m", 0)]
PER = len(order_of(False))


def attention_pass(nc, known, layer, x_dram, g_dram, out_dram, stack_dram, w_parts, w_out_parts, gammas, consts, small, s_qscale):
    biased = layer == 1
    passes = [(0, 0), (0, 1)] + ([(1, 0)] if len(w_parts) == 2 else [])
    HT = TILES // 2
    RP = 8
    BLKS = BANK // VW
    NE, NM = 3, 2

    with ExitStack() as ctx:
        def sb(nm, shape, dt):
            return ctx.enter_context(nc.sbuf_tensor(f"a{layer}_{nm}", shape, dt))

        def ps(nm, n):
            return ctx.enter_context(nc.psum_tensor(f"a{layer}_{nm}", [P, n, BANK], F32))

        counts = []

        def sem(nm):
            counts.append(semaphore(nc, known, f"att_{nm}"))
            return counts[-1]

        x_in = sb("x_in", [P, HT, D], F32)
        bn = sb("bn", [P, HT, 6], F32)
        mv = sb("mv", [P, HT, 2], F32)
        var_eps = sb("var_eps", [P, HT], F32)
        rstd = sb("rstd", [P, HT], F32)
        minus_half = sb("minus_half", [P, HT], F32)
        xT = [sb(f"xT{i}", [P, KI, T], F32R) for i in range(2)]
        qk = sb("qk", [P, 2, BANK], F32)
        rest = sb("rest", [P, 2, BANK], F32)
        parts = sb("parts", [P, 2, 3, T], BF16)
        q_stack = sb("q_stack", [P, HEADS, T], BF16)
        k_stack = sb("k_stack", [P, HEADS, T], BF16)
        v = sb("v", [P, TILES, HEADS, VW], F32)
        max_in = sb("max_in", [P, 2, 2, HG, TILES], F32)
        max_tmp = sb("max_tmp", [P, 2, HG, TILES], F32)
        max_parts = sb("max_parts", [P, TILES, HG, MAXROWS], BF16)
        maxT = sb("maxT", [HG * MAXROWS, T], BF16)
        junk = sb("junk", [P, NM, BANK], BF16)
        mask_add = sb("mask_add", [P, BANK], BF16)
        tri = sb("tri", [P, P], BF16)
        ident_b = sb("ident_b", [P, P], BF16)
        probs = sb("probs", [P, RP, BANK], F32)
        turned = sb("turned", [P, BLKS, VW], F32)
        inverse = sb("inverse", [P, BLKS], F32)
        pair = sb("pair", [P, 2, BLKS, 2, DH], F32)
        attn_raw = sb("attn_raw", [P, BANK], F32)
        attn = [sb(f"attn{i}", [P, KI, T], F32R) for i in range(2)]
        x_old = sb("x_old", [P, TILES, D], F32)
        g_in = sb("g_in", [P, TILES, D], F32)
        s_scaled = sb("s_scaled", [P, 2, 2 * D], F32)

        ps_exp = ps("ps_exp", NE)
        ps_max = ps("ps_max", NM)
        ps_small = ps("ps_small", 1)
        ps_pv = ps("ps_pv", 2)

        x_loaded, bn_done, stats_done, rstd_done, xn_done = (
            sem("x_loaded"), sem("bn_done"), sem("stats_done"), sem("rstd_done"), sem("xn_done"))
        const_set, dve_set, stood_alone = sem("const_set"), sem("dve_set"), sem("stood_alone")
        small_full = sem("small_full")
        xT_high, xT_ready = sem("xT_high"), sem("xT_ready")
        qk_ready, high_done, rest_done, mid_done, low_done = (
            sem("qk_ready"), sem("high_done"), sem("rest_done"), sem("mid_done"), sem("low_done"))
        parts_stored, stack_loaded, v_ready = sem("parts_stored"), sem("stack_loaded"), sem("v_ready")
        max_full, max_taken = sem("max_full"), sem("max_taken")
        neg_step = sem("neg_step")
        max_step, max_split, maxT_ready, maxT_loaded = sem("max_step"), sem("max_split"), sem("maxT_ready"), sem("maxT_loaded")
        exp_full, exp_done, pv_done = sem("exp_full"), sem("exp_done"), sem("pv_done")
        pv_turned, inverted, pair_done, turned_back = sem("pv_turned"), sem("inverted"), sem("pair_done"), sem("turned_back")
        attn_high, attn_ready = sem("attn_high"), sem("attn_ready")
        ends_loaded, s_done, gated, x_added, out_stored = (
            sem("ends_loaded"), sem("s_done"), sem("gated"), sem("x_added"), sem("out_stored"))
        block = ctx.enter_context(nc.Block())

        ident = consts[:, C_IDENT:C_IDENT + P]
        x_half = x_dram.rearrange("(k i p) d -> k p i d", i=HT, p=P)
        x_all = x_dram.rearrange("(k i p) d -> k p i d", i=TILES, p=P)
        g_all = g_dram.rearrange("(k i p) d -> k p i d", i=TILES, p=P)
        out_pair = out_dram.rearrange("(k i p) d -> k p i d", i=2, p=P)

        def rows(view, k):
            return view[bass.ds(k, 1)].rearrange("o p i d -> p (o i) d")

        def flat(ap):
            return ap.rearrange("p i d -> p (i d)")

        first_at = {key: n for n, key in enumerate(FIRST)}
        body_at = {key: n for n, key in enumerate(order_of(False))}
        last_at = {key: n for n, key in enumerate(order_of(True))}

        def small_count(section, it, key):
            if section == "first":
                return first_at[key] + 1
            return len(FIRST) + it * PER + (last_at if section == "last" else body_at)[key] + 1

        def group_no(b, g):
            return b * GROUPS + g

        def step_no(b, g, s):
            return group_no(b, g) * len(STEPS) + s

        def lead_tile(g, n):
            groups, tile = (1, n + LEAD) if n + LEAD < SLOTS else (2, n + LEAD - SLOTS)
            return (g + groups) // GROUPS, (g + groups) % GROUPS, tile

        def width(t, j):
            start = max(j * P, t * BANK)
            return start, (t + 1) * BANK - start

        @block.sync
        def _(sp):
            for s in counts:
                sp.sem_inc(s, BASE)

            def load_x(b, u):
                sp.wait_ge(xT_ready, BASE + (b * 2 + u) * KI)
                sp.dma_start(x_in[:], rows(x_half, b * 2 + u)).then_inc(x_loaded, 16)

            def stack(b, c):
                sp.wait_ge(low_done, BASE + (b * KI + c) * 4 + 4)
                sp.wait_ge(stack_loaded, BASE + (b * KI + c - 1) * 192)
                sp.dma_start(stack_dram[c].rearrange("q w p t -> p q w t"), parts[:]).then_inc(parts_stored, 16)
                sp.wait_ge(parts_stored, BASE + (b * KI + c + 1) * 16)
                sp.wait_ge(pv_done, BASE + step_no(b - 1, 2 * c + 1, len(STEPS) - 1) + 1)
                for s in range(SPLITS // DH):
                    for dst, w, which in ((q_stack, 0, Q_PARTS[s]), (k_stack, 1, K_PARTS[s])):
                        sp.dma_start(dst[s * DH:(s + 1) * DH, c * HC:(c + 1) * HC, :],
                                     stack_dram[c, w, which].rearrange("(h d) t -> d h t", d=DH)).then_inc(stack_loaded, 16)

            def load_max(b, g):
                sp.wait_ge(maxT_ready, BASE + group_no(b, g) + 1)
                for h in range(HG):
                    sp.dma_start(q_stack[SPLITS:SPLITS + MAXROWS, g * HG + h, :],
                                 maxT[h * MAXROWS:(h + 1) * MAXROWS, :]).then_inc(maxT_loaded, 16)

            def load_ends(b):
                sp.wait_ge(out_stored, BASE + b * 64)
                sp.dma_start(x_old[:], rows(x_all, b)).then_inc(ends_loaded, 16)
                sp.dma_start(g_in[:], rows(g_all, b)).then_inc(ends_loaded, 16)

            def store_ends(b):
                for i in range(4):
                    sp.wait_ge(x_added, BASE + b * 4 + i + 1)
                    sp.dma_start(rows(out_pair, b * 4 + i), x_old[:, 2 * i:2 * i + 2]).then_inc(out_stored, 16)

            def sequence(b, more):
                stack(b, 1)
                load_ends(b)
                load_max(b, 1)
                if more:
                    load_x(b + 1, 0)
                    load_x(b + 1, 1)
                load_max(b, 2)
                if more:
                    stack(b + 1, 0)
                load_max(b, 3)
                if more:
                    load_max(b + 1, 0)
                store_ends(b)

            load_x(0, 0)
            load_x(0, 1)
            stack(0, 0)
            load_max(0, 0)
            with sp.Fori(0, B - 1) as b:
                sequence(b, True)
            sequence(B - 1, False)
            sp.wait_ge(out_stored, BASE + B * 64)

        @block.gpsimd
        def _(pool):
            nc.gpsimd.memset(minus_half[:], -0.5).then_inc(const_set, 1)
            nc.gpsimd.memset(max_in[:], LOWEST).then_inc(const_set, 1)
            nc.gpsimd.memset(v[:], 1.0).then_inc(const_set, 1)
            pool.wait_ge(const_set, BASE + CONSTS_SET - 1)
            nc.gpsimd.memset(k_stack[SPLITS:SPLITS + MAXROWS], 1.0).then_inc(const_set, 1)
            pool.wait_ge(const_set, BASE + CONSTS_SET)

            def inverse_deviation(b, u):
                pool.wait_ge(stats_done, BASE + (b * 2 + u) * 5 + 5)
                nc.gpsimd.tensor_tensor(rstd[:], var_eps[:], minus_half[:], ALU.pow).then_inc(rstd_done, 1)

            def split(b, c, pieces=range(4)):
                for n in pieces:
                    no = (b * KI + c) * 4 + n
                    pool.wait_ge(high_done, BASE + no + 1)
                    pool.wait_ge(low_done, BASE + no - 1)
                    w, cols = n // 2, slice((n % 2) * BANK, (n % 2 + 1) * BANK)
                    nc.gpsimd.tensor_tensor(rest[:, n % 2], qk[:, n % 2], parts[:, w, 0, cols],
                                            ALU.subtract).then_inc(rest_done, 1)
                    pool.wait_ge(mid_done, BASE + no + 1)
                    nc.gpsimd.tensor_tensor(parts[:, w, 2, cols], rest[:, n % 2], parts[:, w, 1, cols],
                                            ALU.subtract).then_inc(low_done, 1)

            def split_max(b, g):
                gn = group_no(b, g)
                pool.wait_ge(max_step, BASE + gn * 4 + 1)
                pool.wait_ge(maxT_ready, BASE + gn)
                pool.sem_inc(stood_alone, 1)
                top = max_parts[:].rearrange("p i h w -> p h i w")
                nc.gpsimd.tensor_copy(top[:, :, :, 0], max_tmp[:, 0]).then_inc(max_step, 1)
                pool.wait_ge(max_step, BASE + gn * 4 + 2)
                nc.gpsimd.tensor_tensor(max_tmp[:, 1], max_tmp[:, 0], top[:, :, :, 0], ALU.subtract).then_inc(max_step, 1)
                pool.wait_ge(max_step, BASE + gn * 4 + 3)
                pool.sem_inc(stood_alone, 1)
                nc.gpsimd.tensor_copy(top[:, :, :, 1], max_tmp[:, 1]).then_inc(max_step, 1)
                pool.wait_ge(max_step, BASE + gn * 4 + 4)
                nc.gpsimd.tensor_tensor(top[:, :, :, 2], max_tmp[:, 1], top[:, :, :, 1], ALU.subtract).then_inc(max_split, 1)

            def normalise(b, g, t):
                no = group_no(b, g) * 2 + t
                pool.wait_ge(inverted, BASE + no + 1)
                pool.wait_ge(turned_back, BASE + (b * KI + g // 2) * 2 + t - 1)
                nc.gpsimd.tensor_tensor(pair[:, t, :, g % 2], turned[:, :, 0:DH],
                                        inverse[:].unsqueeze(2).broadcast_to([P, BLKS, DH]),
                                        ALU.mult).then_inc(pair_done, 1)

            def low_attention(b, c, t):
                no = (b * KI + c) * 2 + t
                pool.wait_ge(attn_high, BASE + no + 1)
                cols = slice(t * BANK, (t + 1) * BANK)
                nc.gpsimd.tensor_tensor(attn[1][:, c, cols], attn_raw[:], attn[0][:, c, cols].bitcast(F32),
                                        ALU.subtract).then_inc(attn_ready, 1)

            def add(b, i):
                no = b * 4 + i
                pool.wait_ge(ends_loaded, BASE + (b + 1) * 32)
                pool.wait_ge(s_done, BASE + no + 1)
                pair = slice(2 * i, 2 * i + 2)
                nc.gpsimd.tensor_tensor(flat(g_in[:, pair]), s_scaled[:, i % 2], flat(g_in[:, pair]),
                                        ALU.mult).then_inc(gated, 1)
                pool.wait_ge(gated, BASE + no + 1)
                nc.gpsimd.tensor_tensor(flat(x_old[:, pair]), flat(g_in[:, pair]), flat(x_old[:, pair]),
                                        ALU.add).then_inc(x_added, 1)

            def sequence(b, more):
                split(b, 1)
                normalise(b, 0, 0)
                split_max(b, 1)
                if more:
                    inverse_deviation(b + 1, 0)
                normalise(b, 0, 1)
                if more:
                    inverse_deviation(b + 1, 1)
                normalise(b, 1, 0)
                low_attention(b, 0, 0)
                split_max(b, 2)
                if more:
                    split(b + 1, 0, (0, 1))
                normalise(b, 1, 1)
                if more:
                    split(b + 1, 0, (2, 3))
                low_attention(b, 0, 1)
                normalise(b, 2, 0)
                split_max(b, 3)
                normalise(b, 2, 1)
                normalise(b, 3, 0)
                low_attention(b, 1, 0)
                if more:
                    split_max(b + 1, 0)
                add(b, 0)
                add(b, 1)
                normalise(b, 3, 1)
                low_attention(b, 1, 1)
                add(b, 2)
                add(b, 3)

            inverse_deviation(0, 0)
            inverse_deviation(0, 1)
            split(0, 0)
            split_max(0, 0)
            with pool.Fori(0, B - 1) as b:
                sequence(b, True)
            sequence(B - 1, False)

        @block.scalar
        def _(act):
            def take_xT(sec, it, b, u, ki):
                act.wait_ge(small_full, BASE + small_count(sec, it, ("x", u, ki)))
                nc.scalar.activation(xT[0][:, ki, u * BANK:(u + 1) * BANK], ps_small[:, 0],
                                     ACT.Copy).then_inc(xT_high, 1)

            def take_qk(sec, it, b, what, c, u):
                n = (2 if what == "k" else 0) + u
                no = (b * KI + c) * 4 + n
                act.wait_ge(small_full, BASE + small_count(sec, it, (what, c, u)))
                act.wait_ge(rest_done, BASE + no - 1)
                scale, bias = 1.0, 0.0
                if what == "q":
                    scale = s_qscale if layer == 0 else DH ** -0.5
                if biased:
                    at = (S_QB if what == "q" else S_KB) + c
                    bias = small[:, at:at + 1]
                func = ACT.Identity
                nc.scalar.activation(qk[:, n % 2], ps_small[:, 0], func, scale=scale, bias=bias).then_inc(qk_ready, 1)

            def take_v(sec, it, b, c, u):
                act.wait_ge(small_full, BASE + small_count(sec, it, ("v", c, u)))
                act.wait_ge(pv_done, BASE + step_no(b - 1, 2 * c + 1, len(STEPS) - 1) + 1)
                act.wait_ge(const_set, BASE + CONSTS_SET)
                dst = v[:, u * HT:(u + 1) * HT, c * HC:(c + 1) * HC, 0:DH]
                src = ps_small[:, 0].rearrange("p (i h d) -> p i h d", i=HT, d=DH)
                nc.scalar.activation(dst, src, ACT.Copy).then_inc(v_ready, 1)

            def take_max(sec, it, b, g):
                act.wait_ge(small_full, BASE + small_count(sec, it, ("m", g)))
                act.wait_ge(maxT_loaded, BASE + group_no(b, g) * 64)
                src = ps_small[0:HG * MAXROWS, 0].bitcast(BF16)
                nc.scalar.activation(maxT[:], src, ACT.Copy).then_inc(maxT_ready, 1)

            def high_attention(b, c, t):
                act.wait_ge(turned_back, BASE + (b * KI + c) * 2 + t + 1)
                act.wait_ge(s_done, BASE + b * 4)
                nc.scalar.activation(attn[0][:, c, t * BANK:(t + 1) * BANK], attn_raw[:], ACT.Copy).then_inc(attn_high, 1)

            def exponential(b, g, n):
                s, h = n // HG, n % HG
                no = step_no(b, g, s) * HG + h
                _, w = width(*STEPS[s])
                act.wait_ge(exp_full, BASE + no + 1)
                act.wait_ge(pv_done, BASE + step_no(b, g, s) - 1)
                nc.scalar.activation(probs[:, n % RP, 0:w], ps_exp[:, n % NE, 0:w], ACT.Exp).then_inc(exp_done, 1)

            def sequence(sec, b, last):
                more = not last
                at = small_work(last)
                for g in range(GROUPS):
                    for n in range(SLOTS):
                        if n in at[g]:
                            small_item(sec, b, at[g][n], b + 1 if is_ahead(at[g][n]) else b)
                        exponential(b, g, n)
                        if n == HIGH_SLOT and g % 2:
                            high_attention(b, g // 2, 0)
                        if n == HIGH_SLOT - BEHIND and g == 2:
                            high_attention(b, 0, 1)
                high_attention(b, 1, 1)

            def small_item(sec, it, key, b):
                kind = key[0]
                if kind == "x":
                    take_xT(sec, it, b, key[1], key[2])
                elif kind in "qk":
                    take_qk(sec, it, b, kind, key[1], key[2])
                elif kind == "v" and not biased:
                    take_v(sec, it, b, key[1], key[2])
                elif kind == "m":
                    take_max(sec, it, b, key[1])

            for key in FIRST:
                small_item("first", 0, key, 0)
            with act.Fori(0, B - 1) as b:
                sequence("body", b, False)
            sequence("last", B - 1, True)

        @block.vector
        def _(dve):
            nc.vector.tensor_copy(mask_add[:], consts[:, C_MAXMASK:C_MAXMASK + BANK]).then_inc(dve_set, 1)
            nc.vector.tensor_copy(tri[:], consts[:, C_TRI:C_TRI + P]).then_inc(dve_set, 1)
            nc.vector.tensor_copy(ident_b[:], ident).then_inc(dve_set, 1)
            dve.wait_ge(const_set, BASE + CONSTS_SET)

            ln_sems = (x_loaded, bn_done, stats_done, rstd_done, xn_done, stood_alone)
            ln_bufs = (x_in, x_in, bn, mv, var_eps, rstd)

            def norm(b, u):
                free = (xT_ready, (b * 2 + u) * KI)
                layer_norm_dve(nc, dve, b * 2 + u, ln_sems + (free,), ln_bufs)

            def low_xT(sec, it, b, u, ki):
                no = (b * 2 + u) * KI + ki
                dve.wait_ge(xT_high, BASE + no + 1)
                cols = slice(u * BANK, (u + 1) * BANK)
                nc.vector.tensor_tensor(xT[1][:, ki, cols], ps_small[:, 0], xT[0][:, ki, cols].bitcast(F32),
                                        ALU.subtract).then_inc(xT_ready, 1)

            def split(b, what, c, u):
                n = (2 if what == "k" else 0) + u
                no = (b * KI + c) * 4 + n
                w, cols = n // 2, slice((n % 2) * BANK, (n % 2 + 1) * BANK)
                dve.wait_ge(qk_ready, BASE + no + 1)
                dve.wait_ge(parts_stored, BASE + (b * KI + c) * 16)
                nc.vector.tensor_copy(parts[:, w, 0, cols], qk[:, n % 2]).then_inc(high_done, 1)
                dve.wait_ge(rest_done, BASE + no + 1)
                nc.vector.tensor_copy(parts[:, w, 1, cols], rest[:, n % 2]).then_inc(mid_done, 1)

            def take_v(sec, it, b, c, u):
                dve.wait_ge(small_full, BASE + small_count(sec, it, ("v", c, u)))
                dve.wait_ge(pv_done, BASE + step_no(b - 1, 2 * c + 1, len(STEPS) - 1) + 1)
                dst = v[:, u * HT:(u + 1) * HT, c * HC:(c + 1) * HC, 0:DH]
                src = ps_small[:, 0].rearrange("p (i h d) -> p i h d", i=HT, d=DH)
                for i in range(HT):
                    bias = small[:, S_VB + c * P:S_VB + (c + 1) * P].rearrange("p (h d) -> p h d", d=DH)
                    ins = nc.vector.tensor_tensor(dst[:, i], src[:, i], bias, ALU.add)
                ins.then_inc(v_ready, 1)

            def maximum(b, g, tile):
                no = group_no(b, g) * SLOTS + tile
                h, (i, piece) = tile // 12, PIECES[tile % 12]
                w = min((i + 1) * P - piece * BANK, BANK)
                if tile == 0:
                    dve.wait_ge(neg_step, BASE + group_no(b, g) - 1)
                dve.wait_ge(max_full, BASE + no + 1)
                out = max_in[:, g % 2, piece, h, i:i + 1]
                src = ps_max[:, tile % NM, 0:w]
                if i * P < (piece + 1) * BANK:
                    dve.sem_inc(stood_alone, 1)
                    nc.vector.tensor_tensor_reduce(junk[:, tile % NM, 0:w], src, mask_add[:, BANK - w:BANK], 1.0, LOWEST,
                                                   ALU.add, ALU.max, out).then_inc(max_taken, 1)
                else:
                    nc.vector.tensor_reduce(out, src, AX.X, ALU.max).then_inc(max_taken, 1)

            def negate_max(b, g):
                gn = group_no(b, g)
                dve.wait_ge(max_taken, BASE + (gn + 1) * SLOTS)
                dve.wait_ge(max_split, BASE + gn)
                nc.vector.scalar_tensor_tensor(max_tmp[:, 1], max_in[:, g % 2, 0], 1.0, max_in[:, g % 2, 1],
                                               ALU.mult, ALU.max).then_inc(neg_step, 1)
                dve.wait_ge(neg_step, BASE + gn + 1)
                nc.vector.tensor_scalar(max_tmp[:, 0], max_tmp[:, 1], -1.0, None, ALU.mult).then_inc(max_step, 1)

            def turn(b, g, t):
                no = group_no(b, g) * 2 + t
                dve.wait_ge(pv_done, BASE + step_no(b, g, 3 if t == 0 else 11) + 1)
                dve.wait_ge(pair_done, BASE + no)
                nc.vector.transpose(turned[:].rearrange("p k c -> p (k c)"), ps_pv[:, t]).then_inc(pv_turned, 1)
                dve.wait_ge(pv_turned, BASE + no + 1)
                nc.vector.reciprocal(inverse[:], turned[:, :, DH]).then_inc(inverted, 1)

            def turn_back(b, c, t):
                dve.wait_ge(pair_done, BASE + group_no(b, 2 * c + 1) * 2 + t + 1)
                dve.wait_ge(attn_ready, BASE + (b * KI + c) * 2 + t)
                nc.vector.transpose(attn_raw[:], pair[:, t].rearrange("p k e d -> p (k e d)")).then_inc(turned_back, 1)

            def scale_out(sec, it, b, i):
                no = b * 4 + i
                dve.wait_ge(small_full, BASE + small_count(sec, it, ("o", i)))
                dve.wait_ge(gated, BASE + no - 1)
                out = s_scaled[:, i % 2]
                if biased:
                    bias = small[:, S_PB:S_PB + D]
                    for j in range(2):
                        ins = nc.vector.tensor_tensor(out[:, j * D:(j + 1) * D], ps_small[:, 0, j * D:(j + 1) * D],
                                                      bias, ALU.add)
                    ins.then_inc(s_done, 1)
                else:
                    nc.vector.tensor_scalar(out, ps_small[:, 0], gammas[:, 5:6], None, ALU.mult).then_inc(s_done, 1)

            def small_item(sec, it, key, b):
                kind = key[0]
                if kind == "x":
                    low_xT(sec, it, b, key[1], key[2])
                elif kind in "qk":
                    split(b, kind, key[1], key[2])
                elif kind == "v" and biased:
                    take_v(sec, it, b, key[1], key[2])
                elif kind == "o":
                    scale_out(sec, it, b, key[1])

            def sequence(sec, b, last):
                at = small_work(last)
                for g in range(GROUPS):
                    for n in range(SLOTS):
                        if not last and g == 1 and n in NORM_SLOTS:
                            norm(b + 1, NORM_SLOTS.index(n))
                        if n in at[g]:
                            small_item(sec, b, at[g][n], b + 1 if is_ahead(at[g][n]) else b)
                        if n == TURN_SLOT:
                            turn(b, g, 0)
                        if n == BACK_SLOT and g % 2:
                            turn_back(b, g // 2, 0)
                        if n == TURN_SLOT - BEHIND and g:
                            turn(b, g - 1, 1)
                        if n == BACK_SLOT - BEHIND and g == 2:
                            turn_back(b, 0, 1)
                        ahead, mg, tile = lead_tile(g, n)
                        if last and ahead:
                            continue
                        maximum(b + ahead, mg, tile)
                        if tile == SLOTS - 1:
                            negate_max(b + ahead, mg)
                turn(b, GROUPS - 1, 1)
                turn_back(b, 1, 1)
                for _, i in OUTS:
                    scale_out(sec, b, b, i)

            for u in range(2):
                norm(0, u)
                for ki in range(KI):
                    low_xT("first", 0, 0, u, ki)
            for key in PROJECT[0]:
                small_item("first", 0, key, 0)
            for tile in range(SLOTS):
                maximum(0, 0, tile)
            negate_max(0, 0)
            for tile in range(LEAD):
                maximum(0, 1, tile)
            with dve.Fori(0, B - 1) as b:
                sequence("body", b, False)
            sequence("last", B - 1, True)

        @block.tensor
        def _(pe):
            out = ps_small[:, 0]

            def taken(item, b):
                kind = item[0]
                if kind == "x":
                    return xT_ready, (b * 2 + item[1]) * KI + item[2] + 1
                if kind in "qk":
                    return qk_ready, (b * KI + item[1]) * 4 + (2 if kind == "k" else 0) + item[2] + 1
                if kind == "v":
                    return v_ready, (b * KI + item[1]) * 2 + item[2] + 1
                if kind == "m":
                    return maxT_ready, group_no(b, item[1]) + 1
                return s_done, b * 4 + item[1] + 1

            def project(b, what, c, u):
                pe.wait_ge(xT_ready, BASE + (b + 1) * 2 * KI)
                for ki in range(KI):
                    for n, (wp, xp) in enumerate(passes):
                        ins = nc.tensor.matmul(out, w_parts[wp][:, "qk".index(what), ki, c * P:(c + 1) * P],
                                               xT[xp][:, ki, u * BANK:(u + 1) * BANK],
                                               start=(ki == 0 and n == 0), stop=(ki == KI - 1 and n == len(passes) - 1))
                ins.then_inc(small_full, 1)

            def values(c, u):
                for i in range(HT):
                    tile = slice((u * HT + i) * P, (u * HT + i + 1) * P)
                    for ki in range(KI):
                        for n, (wp, xp) in enumerate(passes):
                            ins = nc.tensor.matmul(out[:, i * P:(i + 1) * P], xT[xp][:, ki, tile],
                                                   w_parts[wp][:, 2, ki, c * P:(c + 1) * P],
                                                   start=(ki == 0 and n == 0),
                                                   stop=(ki == KI - 1 and n == len(passes) - 1))
                ins.then_inc(small_full, 1)

            def turn_x(b, u, ki):
                pe.wait_ge(xn_done, BASE + b * 2 + u + 1)
                for i in range(HT):
                    ins = nc.tensor.transpose(out[:, i * P:(i + 1) * P], x_in[:, i, ki * P:(ki + 1) * P], ident)
                ins.then_inc(small_full, 1)

            def turn_max(b, g):
                pe.wait_ge(max_split, BASE + group_no(b, g) + 1)
                to = out[0:HG * MAXROWS].bitcast(BF16)
                for i in range(TILES):
                    ins = nc.tensor.transpose(to[:, i * P:(i + 1) * P],
                                              max_parts[:, i].rearrange("p h w -> p (h w)"), ident_b[:])
                ins.then_inc(small_full, 1)

            def project_out(b, i):
                pe.wait_ge(attn_ready, BASE + (b * KI + KI - 1) * 2 + i // 2 + 1)
                for j in range(2):
                    tile = slice((2 * i + j) * P, (2 * i + j + 1) * P)
                    for c in range(KI):
                        for n, (wp, ap) in enumerate(passes):
                            ins = nc.tensor.matmul(out[:, j * D:(j + 1) * D], attn[ap][:, c, tile], w_out_parts[wp][:, c],
                                                   start=(c == 0 and n == 0),
                                                   stop=(c == KI - 1 and n == len(passes) - 1))
                ins.then_inc(small_full, 1)

            def small_item(item, b, before):
                for it, bb in before:
                    s, count = taken(it, bb)
                    pe.wait_ge(s, BASE + count)
                kind = item[0]
                if kind == "x":
                    turn_x(b, item[1], item[2])
                elif kind in "qk":
                    project(b, kind, item[1], item[2])
                elif kind == "v":
                    values(item[1], item[2])
                elif kind == "m":
                    turn_max(b, item[1])
                else:
                    project_out(b, item[1])

            def max_tile(b, g, tile):
                no = group_no(b, g) * SLOTS + tile
                head, (i, piece) = g * HG + tile // 12, PIECES[tile % 12]
                w = min((i + 1) * P - piece * BANK, BANK)
                if tile == 0:
                    c = g // 2
                    pe.wait_ge(stack_loaded, BASE + (b * KI + c + 1) * 192)
                pe.wait_ge(max_taken, BASE + no - NM + 1)
                nc.tensor.matmul(ps_max[:, tile % NM, 0:w], q_stack[0:SPLITS, head, i * P:(i + 1) * P],
                                 k_stack[0:SPLITS, head, piece * BANK:piece * BANK + w],
                                 start=True, stop=True).then_inc(max_full, 1)

            def scores(b, g, n):
                s, h = n // HG, n % HG
                t, j = STEPS[s]
                head = g * HG + h
                q0, w = width(t, j)
                diagonal = q0 == j * P
                no = step_no(b, g, s) * HG + h
                if n == 0:
                    pe.wait_ge(maxT_loaded, BASE + (group_no(b, g) + 1) * 64)
                pe.wait_ge(exp_done, BASE + no - NE + 1)
                rows_ = SPLITS + MAXROWS
                ins = nc.tensor.matmul(ps_exp[:, n % NE, 0:w], k_stack[0:rows_, head, j * P:(j + 1) * P],
                                       q_stack[0:rows_, head, q0:q0 + w], start=True, stop=not diagonal)
                if diagonal:
                    ins = nc.tensor.matmul(ps_exp[:, n % NE, 0:P], ident_b[:], tri[:], start=False, stop=True)
                ins.then_inc(exp_full, 1)

            def weigh(b, g, s):
                t, j = STEPS[s]
                q0, w = width(t, j)
                last_j = 3 if t == 0 else 7
                pe.wait_ge(exp_done, BASE + step_no(b, g, s) * HG + HG)
                if j == 0:
                    pe.wait_ge(pv_turned, BASE + group_no(b, g) * 2 + t - 1)
                    if t == 0:
                        pe.wait_ge(v_ready, BASE + (b * KI + g // 2 + 1) * 2)
                for h in range(HG):
                    ins = nc.tensor.matmul(ps_pv[h * VW:(h + 1) * VW, t, q0 - t * BANK:q0 - t * BANK + w],
                                           v[:, j, g * HG + h], probs[:, (s * HG + h) % RP, 0:w],
                                           start=(j == 0), stop=(j == last_j))
                ins.then_inc(pv_done, 1)

            def sequence(b, last):
                at = small_work(last)
                before = [(("o", 3), b - 1), (("m", 0), b)]
                for g in range(GROUPS):
                    for n in range(SLOTS):
                        if n in at[g]:
                            item = at[g][n]
                            bb = b + 1 if is_ahead(item) else b
                            small_item(item, bb, before)
                            before = [(item, bb)]
                        scores(b, g, n)
                        if n % HG == HG - 1:
                            if n >= HG:
                                weigh(b, g, n // HG - 1)
                            elif g:
                                weigh(b, g - 1, len(STEPS) - 1)
                        ahead, mg, tile = lead_tile(g, n)
                        if not (last and ahead):
                            max_tile(b + ahead, mg, tile)
                weigh(b, GROUPS - 1, len(STEPS) - 1)
                for item in OUTS:
                    small_item(item, b, before)
                    before = [(item, b)]

            pe.wait_ge(dve_set, BASE + 3)
            pe.wait_ge(const_set, BASE + CONSTS_SET)
            before = []
            for item in FIRST[:-1]:
                small_item(item, 0, before)
                before = [(item, 0)]
            for tile in range(SLOTS):
                max_tile(0, 0, tile)
            small_item(FIRST[-1], 0, before)
            for tile in range(LEAD):
                max_tile(0, 1, tile)
            with pe.Fori(0, B - 1) as b:
                sequence(b, False)
            sequence(B - 1, True)


def build(nc, x, consts_dram, small_dram, a0_w, a0_wo, f0_up, f0_down, a1_w, a1_wo, f1_up, f1_down, out):
    known = {}
    g_dram = nc.dram_tensor("gate", [B * T, D], F32).ap()
    x1_dram = nc.dram_tensor("x_after_layer_0", [B * T, D], F32).ap()
    stack_dram = nc.dram_tensor("qk_parts", [KI, 2, 3, P, T], BF16).ap()
    with ExitStack() as ctx:
        consts = ctx.enter_context(nc.sbuf_tensor("consts", [P, C_END], F32))
        small = ctx.enter_context(nc.sbuf_tensor("small", [P, S_END], F32))
        gammas = ctx.enter_context(nc.sbuf_tensor("gammas", [P, 8], F32))
        with ExitStack() as c0:
            loaded = nc.alloc_semaphore("consts_loaded")
            bias_scaled = nc.alloc_semaphore("bias_scaled")
            block = c0.enter_context(nc.Block())

            @block.sync
            def _(sp):
                sp.dma_start(consts[:], consts_dram).then_inc(loaded, 16)
                sp.dma_start(small[:], small_dram).then_inc(loaded, 16)

            @block.vector
            def _(dve):
                dve.wait_ge(loaded, 32)
                q_bias = small[:, S_QB:S_QB + KI]
                nc.vector.tensor_scalar(q_bias, q_bias, DH ** -0.5, None, ALU.mult).then_inc(bias_scaled, 1)
                dve.wait_ge(bias_scaled, 1)

        with ExitStack() as c0:
            up = c0.enter_context(nc.sbuf_tensor("f0_up", [P, 2, KI, 6, P], F32R))
            down = c0.enter_context(nc.sbuf_tensor("f0_down", [P, 6, D], F32R))
            wide = KI * 6 * P
            count = HID[0] * D
            ternary_weights(nc, "f0u", f0_up, 2 * wide, up[:].rearrange("p w k c m -> p (w k c m)"),
                         [(0, wide, 6), (wide, wide, 7)], 0.0, 1e-8, count, gammas)
            ternary_weights(nc, "f0d", f0_down, 6 * D, down[:].rearrange("p c d -> p (c d)"),
                         [(0, 6 * D, 6)], 0.0, 1e-8, count, gammas)
            ffn_pass(nc, known, 0, x, g_dram, [up], [down], gammas, consts)
        with ExitStack() as c0:
            w = c0.enter_context(nc.sbuf_tensor("a0_w", [P, 3, KI, D], F32R))
            wo = c0.enter_context(nc.sbuf_tensor("a0_wo", [P, KI, D], F32R))
            wide = KI * D
            ternary_weights(nc, "a0w", a0_w, 3 * wide, w[:].rearrange("p w k m -> p (w k m)"),
                         [(i * wide, wide, i) for i in range(3)], 1e-5, 0.0, D * D, gammas)
            ternary_weights(nc, "a0o", a0_wo, wide, wo[:].rearrange("p c d -> p (c d)"),
                         [(0, wide, 3)], 1e-5, 0.0, D * D, gammas)
            scales(nc, gammas)
            attention_pass(nc, known, 0, x, g_dram, x1_dram, stack_dram, [w], [wo], gammas, consts, small, gammas[:, 4:5])
        with nc.Block() as block:
            @block.sync
            def _(sp):
                for s in known.values():
                    sp.sem_clear(s)

        with ExitStack() as c0:
            up = [c0.enter_context(nc.sbuf_tensor(f"f1_up{i}", [P, 2, KI, 8, P], F32R)) for i in range(2)]
            down = [c0.enter_context(nc.sbuf_tensor(f"f1_down{i}", [P, 8, D], F32R)) for i in range(2)]
            flat_up = [u[:].rearrange("p w k c m -> p (w k c m)") for u in up]
            flat_down = [d[:].rearrange("p c d -> p (c d)") for d in down]
            split_weights(nc, "f1u", f1_up, 2 * KI * 8 * P, *flat_up)
            split_weights(nc, "f1d", f1_down, 8 * D, *flat_down)
            ffn_pass(nc, known, 1, x1_dram, g_dram, up, down, gammas, consts)
        with ExitStack() as c0:
            w = [c0.enter_context(nc.sbuf_tensor(f"a1_w{i}", [P, 3, KI, D], F32R)) for i in range(2)]
            wo = [c0.enter_context(nc.sbuf_tensor(f"a1_wo{i}", [P, KI, D], F32R)) for i in range(2)]
            flat_w = [u[:].rearrange("p w k m -> p (w k m)") for u in w]
            split_weights(nc, "a1w", a1_w, 3 * KI * D, *flat_w)
            split_weights(nc, "a1o", a1_wo, KI * D, *[u[:].rearrange("p c d -> p (c d)") for u in wo])
            attention_pass(nc, known, 1, x1_dram, g_dram, out, stack_dram, w, wo, gammas, consts, small, None)


def scales(nc, gammas):
    with ExitStack() as ctx:
        made = nc.alloc_semaphore("scales_made")
        block = ctx.enter_context(nc.Block())

        @block.vector
        def _(dve):
            nc.vector.tensor_scalar(gammas[:, 4:5], gammas[:, 0:1], gammas[:, 1:2], DH ** -0.5,
                                    ALU.mult, ALU.mult).then_inc(made, 1)
            nc.vector.tensor_scalar(gammas[:, 5:6], gammas[:, 2:3], gammas[:, 3:4], None,
                                    ALU.mult).then_inc(made, 1)
            dve.wait_ge(made, 2)


def laid_out(inputs):
    import numpy as np

    f = {k: np.asarray(v) for k, v in inputs.items()}

    def by_row(w):
        return w.reshape(-1, P, w.shape[1]).transpose(1, 0, 2)

    def out_rows(w):
        return w.reshape(KI, 2, HG, DH, D).transpose(2, 1, 3, 0, 4)

    def thirds(ws):
        return np.stack([by_row(w) for w in ws], 1)

    pad = 6 * P - HID[0]
    f0 = np.stack([by_row(np.pad(f[n].T, ((0, 0), (0, pad)))) for n in ("L0_ffn_w1", "L0_ffn_w2")], 1)
    f0d = by_row(np.pad(f["L0_ffn_w3"].T, ((0, pad), (0, 0))))

    def fours(w):
        k = by_row(w)
        return k.reshape(P, KI, 2, P, 4).transpose(0, 1, 2, 4, 3).reshape(P, KI, 8 * P)

    f1 = np.stack([fours(f[n]) for n in ("L1_ffn_w_gate", "L1_ffn_w_up")], 1)
    f1d = f["L1_ffn_w_down"].reshape(2, P, 4, D).transpose(1, 0, 2, 3)
    wa, ba = f["L1_attn_W_attn"], f["L1_attn_b_attn"]

    consts = np.zeros((P, C_END), np.float32)
    p, c = np.arange(P)[:, None], np.arange(P)[None, :]
    consts[:, C_IDENT:C_IDENT + P] = p == c
    consts[:, C_TRI:C_TRI + P] = np.where(p > c, NEG, 0.0)
    consts[:, C_MAXMASK + BANK - P:C_END] = np.where(c > p, NEG, 0.0)
    small = np.zeros((P, S_END), ba.dtype)
    small[:, S_QB:S_QB + KI] = ba[0:D].reshape(KI, P).T
    small[:, S_KB:S_KB + KI] = ba[D:2 * D].reshape(KI, P).T
    small[:, S_VB:S_VB + D] = ba[None, 2 * D:]
    small[:, S_PB:S_PB + D] = f["L1_attn_b_proj"][None]

    def rows(a):
        return np.ascontiguousarray(a.reshape(P, -1))

    return {
        "x": f["L0_attn_x"].reshape(B * T, D), "consts": consts, "small": small,
        "a0_w": rows(thirds([f[f"L0_attn_w{n}"].T for n in "qkv"])), "a0_wo": rows(out_rows(f["L0_attn_wo"].T)),
        "f0_up": rows(f0), "f0_down": rows(f0d),
        "a1_w": rows(thirds([wa[:, i * D:(i + 1) * D] for i in range(3)])), "a1_wo": rows(out_rows(f["L1_attn_W_proj"])),
        "f1_up": rows(f1), "f1_down": rows(f1d),
    }


def kernel(**inputs):
    import numpy as _np
    import concourse.bacc as _bacc
    from concourse import mybir as _mybir
    from concourse.bass_utils import run_bass_kernel_spmd as _run

    nc = _bacc.Bacc("TRN2", target_bir_lowering=False, num_devices=1)
    arrays, args = {}, []
    for name, a in laid_out(inputs).items():
        a = _np.ascontiguousarray(a)
        arrays[f"in_{name}"] = a
        args.append(nc.dram_tensor(f"in_{name}", a.shape, _mybir.dt.from_np(a.dtype), kind="ExternalInput").ap())
    out = nc.dram_tensor("out_x", (B * T, D), F32, kind="ExternalOutput").ap()
    build(nc, *args, out)
    r = _run(nc, [arrays], core_ids=[0])
    return r.results[0]["out_x"].reshape(B, T, D)
```

```python
from contextlib import ExitStack

import concourse.bass as bass
from concourse import mybir

F32 = mybir.dt.float32
F32R = mybir.dt.float32r
BF16 = mybir.dt.bfloat16
ALU = mybir.AluOpType
ACT = mybir.ActivationFunctionType
AX = mybir.AxisListType

P = 128
BANK = 512
B, T, D = 4, 1024, 256
HEADS, DH = 16, 16
KI = D // P
TILES = T // P
HG = 4
GROUPS = HEADS // HG
HC = P // DH
VW = 32
HID = (704, 1024)
EPS_LN = 1e-5
NEG = -1e30
LOWEST = -3e38
SPLITS = 96
MAXROWS = 3
MAX_AT = P - MAXROWS
Q_PARTS = (0, 0, 0, 1, 1, 2)
K_PARTS = (0, 1, 2, 0, 1, 0)
C_IDENT, C_MAXMASK = 0, 128
C_END = C_MAXMASK + P
S_QB, S_KB, S_VB, S_PB = 0, KI, 2 * KI, 2 * KI + D
S_END = 2 * KI + 2 * D


BASE = 512


def semaphore(nc, known, name):
    if name not in known:
        known[name] = nc.alloc_semaphore(name)
    return known[name]


def split_weights(nc, name, raw_dram, width, high, low):
    with ExitStack() as ctx:
        raw = ctx.enter_context(nc.sbuf_tensor(f"{name}_raw", [P, width], F32))
        loaded = nc.alloc_semaphore(f"{name}_loaded")
        high_done = nc.alloc_semaphore(f"{name}_high_done")
        low_done = nc.alloc_semaphore(f"{name}_low_done")
        block = ctx.enter_context(nc.Block())

        @block.sync
        def _(sp):
            sp.dma_start(raw[:], raw_dram).then_inc(loaded, 16)

        @block.scalar
        def _(act):
            act.wait_ge(loaded, 16)
            nc.scalar.activation(high, raw[:], ACT.Copy).then_inc(high_done, 1)

        @block.vector
        def _(dve):
            dve.wait_ge(high_done, 1)
            nc.vector.tensor_tensor(low, raw[:], high.bitcast(F32), ALU.subtract).then_inc(low_done, 1)
            dve.wait_ge(low_done, 1)


def ternary_weights(nc, name, raw_dram, width, out, pieces, floor, eps, count, gammas):
    with ExitStack() as ctx:
        raw = ctx.enter_context(nc.sbuf_tensor(f"{name}_raw", [P, width], F32))
        loaded = nc.alloc_semaphore(f"{name}_loaded")
        summed = nc.alloc_semaphore(f"{name}_summed")
        totalled = nc.alloc_semaphore(f"{name}_totalled")
        gamma_step = nc.alloc_semaphore(f"{name}_gamma_step")
        above_done = nc.alloc_semaphore(f"{name}_above_done")
        parts_done = nc.alloc_semaphore(f"{name}_parts_done")
        n = len(pieces)
        junk = ctx.enter_context(nc.sbuf_tensor(f"{name}_junk", [P, width], F32))
        sums = ctx.enter_context(nc.sbuf_tensor(f"{name}_sums", [P, n], F32))
        ones = ctx.enter_context(nc.sbuf_tensor(f"{name}_ones", [P, P], F32))
        half = ctx.enter_context(nc.sbuf_tensor(f"{name}_half", [P, 2, n], F32))
        total = ctx.enter_context(nc.psum_tensor(f"{name}_total", [P, BANK], F32))
        block = ctx.enter_context(nc.Block())

        @block.sync
        def _(sp):
            sp.dma_start(raw[:], raw_dram).then_inc(loaded, 16)

        @block.scalar
        def _(act):
            act.wait_ge(loaded, 16)
            for i, (c0, w, _) in enumerate(pieces):
                nc.scalar.activation(junk[:, c0:c0 + w], raw[:, c0:c0 + w], ACT.Abs,
                                     accum_out=sums[:, i:i + 1]).then_inc(summed, 1)

        @block.tensor
        def _(pe):
            pe.wait_ge(summed, n + 1)
            nc.tensor.matmul(total[:, 0:n], ones[:], sums[:], start=True, stop=True).then_inc(totalled, 1)

        @block.vector
        def _(dve):
            nc.vector.memset(ones[:], 1.0).then_inc(summed, 1)
            dve.wait_ge(totalled, 1)
            g0 = pieces[0][2]
            nc.vector.tensor_scalar(gammas[:, g0:g0 + n], total[:, 0:n], 1.0 / count, floor,
                                    ALU.mult, ALU.max).then_inc(gamma_step, 1)
            dve.wait_ge(gamma_step, 1)
            nc.vector.tensor_scalar(half[:, 0], gammas[:, g0:g0 + n], eps, 0.5,
                                    ALU.add, ALU.mult).then_inc(gamma_step, 1)
            nc.vector.tensor_scalar(half[:, 1], gammas[:, g0:g0 + n], eps, -0.5,
                                    ALU.add, ALU.mult).then_inc(gamma_step, 1)
            dve.wait_ge(gamma_step, 3)
            for i, (c0, w, _) in enumerate(pieces):
                nc.vector.tensor_scalar(junk[:, c0:c0 + w], raw[:, c0:c0 + w], half[:, 0, i:i + 1], None,
                                        ALU.is_gt).then_inc(above_done, 1)
            for i, (c0, w, _) in enumerate(pieces):
                dve.wait_ge(above_done, i + 1)
                nc.vector.scalar_tensor_tensor(junk[:, c0:c0 + w], raw[:, c0:c0 + w], half[:, 1, i:i + 1],
                                               junk[:, c0:c0 + w], ALU.is_lt, ALU.subtract).then_inc(above_done, 1)
            dve.wait_ge(above_done, 2 * n)
            nc.vector.tensor_scalar(out, junk[:], -1.0, None, ALU.mult).then_inc(parts_done, 1)


def layer_norm_dve(nc, dve, k, sems, bufs):
    x_loaded, bn_done, stats_done, rstd_done, xn_done, stood_alone, xn_free = sems
    x_in, xn, bn, mv, var_eps, rstd = bufs
    dve.wait_ge(x_loaded, BASE + (k + 1) * 16)
    for i in range(4):
        nc.vector.bn_stats(bn[:, i], x_in[:, i]).then_inc(bn_done, 1)
    for i in range(4):
        if i == 0:
            dve.wait_ge(bn_done, BASE + k * 4 + 4)
            dve.sem_inc(stood_alone, 1)
        nc.vector.bn_aggr(mv[:, i], bn[:, i]).then_inc(stats_done, 1)
    dve.wait_ge(stats_done, BASE + k * 5 + 4)
    nc.vector.tensor_scalar(var_eps[:], mv[:, :, 1], EPS_LN, None, ALU.add).then_inc(stats_done, 1)
    dve.wait_ge(rstd_done, BASE + k + 1)
    dve.wait_ge(xn_free[0], BASE + xn_free[1])
    for i in range(4):
        ins = nc.vector.tensor_scalar(xn[:, i], x_in[:, i], mv[:, i, 0:1], rstd[:, i:i + 1],
                                      ALU.subtract, ALU.mult)
    ins.then_inc(xn_done, 1)


def ffn_pass(nc, known, layer, x_dram, g_dram, w_up_parts, w_down_parts, gammas, consts):
    sparse = layer == 1
    NCH = 4 if sparse else 3
    BLOCKS = B * T // BANK
    BT = BANK // P
    MEMB = [P] * 8 if sparse else [P] * 5 + [HID[0] - 5 * P]
    NW = len(w_up_parts)
    passes = [(0, 0), (0, 1)] + ([(1, 0)] if NW == 2 else [])

    with ExitStack() as ctx:
        def sb(nm, shape, dt):
            return ctx.enter_context(nc.sbuf_tensor(f"f{layer}_{nm}", shape, dt))

        counts = []

        def sem(nm):
            counts.append(semaphore(nc, known, f"ffn_{nm}"))
            return counts[-1]

        x_in = sb("x_in", [P, BT, D], F32)
        xn = sb("xn", [P, BT, D], F32)
        bn = sb("bn", [P, BT, 6], F32)
        mv = sb("mv", [P, BT, 2], F32)
        var_eps = sb("var_eps", [P, BT], F32)
        rstd = sb("rstd", [P, BT], F32)
        minus_half = sb("minus_half", [P, BT], F32)
        xT = [sb(f"xT{i}", [P, KI, BANK], F32R) for i in range(2)]
        act_gate = sb("act_gate", [P, 2, BANK], F32)
        hid = sb("hid", [P, 2, NCH, BANK], F32)
        hT = [sb(f"hT{i}", [P, 2, NCH, BANK], F32R) for i in range(2)]
        sig = sb("sig", [P, 2, BANK], F32)
        g_out = sb("g_out", [P, BT, D], F32)
        if sparse:
            mag = sb("mag", [P, NCH, BANK], F32)
            beats = sb("beats", [P, 6, BANK], BF16)
            votes = sb("votes", [P, 4, BANK], BF16)
            half_votes = sb("half_votes", [P, 4, BANK], BF16)
        ps_up = ctx.enter_context(nc.psum_tensor(f"f{layer}_ps_up", [P, 4, BANK], F32))
        ps_xT = ctx.enter_context(nc.psum_tensor(f"f{layer}_ps_xT", [P, KI, BANK], F32))
        ps_down = ctx.enter_context(nc.psum_tensor(f"f{layer}_ps_down", [P, 2, BANK], F32))

        x_loaded, bn_done, stats_done, rstd_done, xn_done = (
            sem("x_loaded"), sem("bn_done"), sem("stats_done"), sem("rstd_done"), sem("xn_done"))
        half_set, stood_alone = sem("half_set"), sem("stood_alone")
        turned, xT_high, xT_ready = sem("turned"), sem("xT_high"), sem("xT_ready")
        gate_full, up_full, gate_taken, hid_done = sem("gate_full"), sem("up_full"), sem("gate_taken"), sem("hid_done")
        mag_done, beats_done, votes_done, kept = sem("mag_done"), sem("beats_done"), sem("votes_done"), sem("kept")
        high_done, low_done = sem("high_done"), sem("low_done")
        down_done, sig_done, g_done, g_stored = sem("down_done"), sem("sig_done"), sem("g_done"), sem("g_stored")
        block = ctx.enter_context(nc.Block())
        ident = consts[:, C_IDENT:C_IDENT + P]

        def n_par(half, m):
            return (half * NCH + m) % 2

        x_v = x_dram.rearrange("(k i p) d -> k p i d", i=BT, p=P)
        g_v = g_dram.rearrange("(k i p) d -> k p i d", i=BT, p=P)

        def rows(v, k):
            return v[bass.ds(k, 1)].rearrange("o p i d -> p (o i) d")

        @block.sync
        def _(sp):
            for s in counts:
                sp.sem_inc(s, BASE)

            def body(k):
                sp.wait_ge(xn_done, BASE + k)
                sp.dma_start(x_in[:], rows(x_v, k)).then_inc(x_loaded, 16)

            def store(k):
                sp.wait_ge(g_done, BASE + k * 2 + 2)
                sp.dma_start(rows(g_v, k), g_out[:]).then_inc(g_stored, 16)

            body(0)
            body(1)
            with sp.Fori(2, BLOCKS) as k:
                body(k)
                store(k - 2)
            store(BLOCKS - 2)
            store(BLOCKS - 1)
            sp.wait_ge(g_stored, BASE + 16 * BLOCKS)

        @block.gpsimd
        def _(pool):
            nc.gpsimd.memset(minus_half[:], -0.5).then_inc(half_set, 1)
            pool.wait_ge(half_set, BASE + 1)

            def inverse_deviation(k):
                pool.wait_ge(stats_done, BASE + k * 5 + 5)
                nc.gpsimd.tensor_tensor(rstd[:], var_eps[:], minus_half[:], ALU.pow).then_inc(rstd_done, 1)

            def low_parts(k, half):
                for m in range(NCH):
                    n = k * 2 * NCH + half * NCH + m
                    w = MEMB[half * NCH + m]
                    pool.wait_ge(high_done, BASE + n + 1)
                    nc.gpsimd.tensor_tensor(hT[1][0:w, half, m], hid[0:w, half, m], hT[0][0:w, half, m].bitcast(F32),
                                            ALU.subtract).then_inc(low_done, 1)

            inverse_deviation(0)
            low_parts(0, 0)
            inverse_deviation(1)
            low_parts(0, 1)

            def body(k, more):
                low_parts(k, 0)
                if more:
                    inverse_deviation(k + 1)
                low_parts(k, 1)

            with pool.Fori(1, BLOCKS - 1) as k:
                body(k, True)
            body(BLOCKS - 1, False)

        @block.scalar
        def _(act):
            def take_xT(k):
                for ki in range(KI):
                    act.wait_ge(turned, BASE + k * KI + ki + 1)
                    if ki == 0:
                        act.wait_ge(up_full, BASE + k * 2 * NCH)
                    nc.scalar.activation(xT[0][:, ki], ps_xT[:, ki], ACT.Copy).then_inc(xT_high, 1)

            def chunk_gate(k, half, m):
                n = k * 2 * NCH + half * NCH + m
                w = MEMB[half * NCH + m]
                act.wait_ge(gate_full, BASE + n + 1)
                act.wait_ge(hid_done, BASE + n - 1)
                func = ACT.Silu if sparse else ACT.Sigmoid
                nc.scalar.activation(act_gate[0:w, n_par(half, m)], ps_up[0:w, 2 * n_par(half, m)],
                                     func).then_inc(gate_taken, 1)

            def magnitude(k, half, m):
                n = k * 2 * NCH + half * NCH + m
                act.wait_ge(hid_done, BASE + n + 1)
                if m == 0:
                    act.wait_ge(beats_done, BASE + (k * 2 + half) * 6)
                nc.scalar.activation(mag[:, m], hid[:, half, m], ACT.Abs).then_inc(mag_done, 1)

            def high_part(k, half, m):
                n = k * 2 * NCH + half * NCH + m
                w = MEMB[half * NCH + m]
                act.wait_ge(kept if sparse else hid_done, BASE + n + 1)
                if m == 0:
                    act.wait_ge(down_done, BASE + k * 2 + half - 1)
                nc.scalar.activation(hT[0][0:w, half, m], hid[0:w, half, m], ACT.Copy).then_inc(high_done, 1)

            def out_sigmoid(k):
                act.wait_ge(down_done, BASE + k * 2 + 2)
                act.wait_ge(g_done, BASE + k * 2)
                for t in range(2):
                    func = ACT.Silu if sparse else ACT.Sigmoid
                    if sparse and t == 0:
                        act.wait_ge(g_stored, BASE + k * 16)
                    out = g_out[:, 2 * t:2 * t + 2].rearrange("p i d -> p (i d)") if sparse else sig[:, t]
                    ins = nc.scalar.activation(out, ps_down[:, t], func)
                    ins.then_inc(g_done if sparse else sig_done, 1)

            def half_block(k, half):
                for m in range(NCH):
                    chunk_gate(k, half, m)
                    if not sparse and m:
                        high_part(k, half, m - 1)
                if sparse:
                    for m in range(NCH):
                        magnitude(k, half, m)
                    for m in range(NCH):
                        high_part(k, half, m)
                else:
                    high_part(k, half, NCH - 1)

            take_xT(0)
            half_block(0, 0)
            half_block(0, 1)
            with act.Fori(1, BLOCKS) as k:
                take_xT(k)
                half_block(k, 0)
                out_sigmoid(k - 1)
                half_block(k, 1)
            out_sigmoid(BLOCKS - 1)

        ln_sems = (x_loaded, bn_done, stats_done, rstd_done, xn_done, stood_alone)
        ln_bufs = (x_in, xn, bn, mv, var_eps, rstd)

        @block.vector
        def _(dve):
            def norm(k):
                layer_norm_dve(nc, dve, k, ln_sems + ((xT_ready, k * KI),), ln_bufs)

            def low_xT(k):
                for ki in range(KI):
                    dve.wait_ge(xT_high, BASE + k * KI + ki + 1)
                    nc.vector.tensor_tensor(xT[1][:, ki], ps_xT[:, ki], xT[0][:, ki].bitcast(F32),
                                            ALU.subtract).then_inc(xT_ready, 1)

            def hidden(k, half, m):
                n = k * 2 * NCH + half * NCH + m
                w = MEMB[half * NCH + m]
                dve.wait_ge(gate_taken, BASE + n + 1)
                dve.wait_ge(up_full, BASE + n + 1)
                if m == 0:
                    dve.wait_ge(low_done, BASE + (k * 2 + half - 1) * NCH)
                nc.vector.tensor_tensor(hid[0:w, half, m], ps_up[0:w, 2 * n_par(half, m) + 1],
                                        act_gate[0:w, n_par(half, m)], ALU.mult).then_inc(hid_done, 1)

            def two_of_four(k, half):
                q = k * 2 + half
                dve.wait_ge(mag_done, BASE + (q + 1) * NCH)
                dve.wait_ge(kept, BASE + q * NCH)
                pairs = [(0, 1), (0, 2), (0, 3), (1, 2), (1, 3), (2, 3)]
                for c, (i, j) in enumerate(pairs):
                    nc.vector.tensor_tensor(beats[:, c], mag[:, i], mag[:, j], ALU.is_ge).then_inc(beats_done, 1)
                dve.wait_ge(beats_done, BASE + q * 6 + 6)
                first = [(0, 1, ALU.add), (3, 0, ALU.subtract), (5, 1, ALU.subtract), (2, 4, ALU.add)]
                for c, (i, j, op) in enumerate(first):
                    nc.vector.tensor_tensor(half_votes[:, c], beats[:, i], beats[:, j], op).then_inc(votes_done, 1)
                second = [(2, ALU.add), (4, ALU.add), (3, ALU.subtract), (5, ALU.add)]
                dve.wait_ge(votes_done, BASE + q * 8 + 4)
                for c, (j, op) in enumerate(second):
                    nc.vector.tensor_tensor(votes[:, c], half_votes[:, c], beats[:, j], op).then_inc(votes_done, 1)
                keep = [(2.0, ALU.is_ge), (1.0, ALU.is_ge), (0.0, ALU.is_ge), (1.0, ALU.is_le)]
                dve.wait_ge(votes_done, BASE + q * 8 + 8)
                for m, (bound, op) in enumerate(keep):
                    nc.vector.scalar_tensor_tensor(hid[:, half, m], votes[:, m], bound, hid[:, half, m],
                                                   op, ALU.mult).then_inc(kept, 1)

            def half_block(k, half):
                for m in range(NCH):
                    hidden(k, half, m)
                if sparse:
                    two_of_four(k, half)

            def out_gate(k):
                for t in range(2):
                    dve.wait_ge(sig_done, BASE + k * 2 + t + 1)
                    if t == 0:
                        dve.wait_ge(g_stored, BASE + k * 16)
                    nc.vector.tensor_tensor(g_out[:, 2 * t:2 * t + 2].rearrange("p i d -> p (i d)"), ps_down[:, t],
                                            sig[:, t], ALU.mult).then_inc(g_done, 1)

            norm(0)
            low_xT(0)
            half_block(0, 0)
            norm(1)
            half_block(0, 1)

            def body(k, more):
                low_xT(k)
                half_block(k, 0)
                if not sparse:
                    out_gate(k - 1)
                if more:
                    norm(k + 1)
                half_block(k, 1)

            with dve.Fori(1, BLOCKS - 1) as k:
                body(k, True)
            body(BLOCKS - 1, False)
            if not sparse:
                out_gate(BLOCKS - 1)

        @block.tensor
        def _(pe):
            def turn(k):
                for ki in range(KI):
                    if ki == 0:
                        pe.wait_ge(xn_done, BASE + k + 1)
                    pe.wait_ge(xT_ready, BASE + (k - 1) * KI + ki + 1)
                    for i in range(BT):
                        ins = nc.tensor.transpose(ps_xT[:, ki, i * P:(i + 1) * P], xn[:, i, ki * P:(ki + 1) * P], ident)
                    ins.then_inc(turned, 1)

            def up(k, half):
                for m in range(NCH):
                    n = k * 2 * NCH + half * NCH + m
                    w = MEMB[half * NCH + m]
                    if half == 0 and m == 0:
                        pe.wait_ge(xT_ready, BASE + k * KI + KI)
                    for which, taken, full in ((0, gate_taken, gate_full), (1, hid_done, up_full)):
                        pe.wait_ge(taken, BASE + n - 1)
                        out = ps_up[0:w, 2 * n_par(half, m) + which]
                        for ki in range(KI):
                            for c, (wp, xp) in enumerate(passes):
                                ins = nc.tensor.matmul(out, w_up_parts[wp][:, which, ki, half * NCH + m, 0:w],
                                                       xT[xp][:, ki], start=(ki == 0 and c == 0),
                                                       stop=(ki == KI - 1 and c == len(passes) - 1))
                        ins.then_inc(full, 1)

            def down(k, half):
                q = k * 2 + half
                pe.wait_ge(low_done, BASE + (q + 1) * NCH)
                if half == 0:
                    pe.wait_ge(g_done, BASE + k * 2)
                for i in range(BT):
                    for m in range(NCH):
                        w = MEMB[half * NCH + m]
                        for c, (wp, hp) in enumerate(passes):
                            ins = nc.tensor.matmul(
                                ps_down[:, i // 2, (i % 2) * D:(i % 2 + 1) * D], hT[hp][0:w, half, m, i * P:(i + 1) * P],
                                w_down_parts[wp][0:w, half * NCH + m],
                                start=(half == 0 and m == 0 and c == 0 and i % 2 == 0),
                                stop=(half == 1 and m == NCH - 1 and c == len(passes) - 1),
                                skip_group_check=True)
                ins.then_inc(down_done, 1)

            turn(0)
            up(0, 0)
            up(0, 1)
            with pe.Fori(1, BLOCKS) as k:
                turn(k)
                down(k - 1, 0)
                up(k, 0)
                down(k - 1, 1)
                up(k, 1)
            down(BLOCKS - 1, 0)
            down(BLOCKS - 1, 1)



SLOTS = 48
LEAD = 12
LN_WORK = {(0, 33): ("aggregate", 0, 0), (1, 24): ("aggregate", 1, 0)}
for _i in range(4):
    LN_WORK[0, 20 + 3 * _i] = ("statistics", 0, _i)
    LN_WORK[0, 38 + 2 * _i] = ("norm", 0, _i)
    LN_WORK[1, 12 + 3 * _i] = ("statistics", 1, _i)
    LN_WORK[1, 28 + 2 * _i] = ("norm", 1, _i)
CONSTS_SET = 4
STEPS = [(0, j) for j in (0, 3, 1, 2)] + [(1, j) for j in (0, 7, 1, 6, 2, 5, 3, 4)]
DIAGONAL = [s for s, (t, j) in enumerate(STEPS) if j * P >= t * BANK]
PIECES = [(0, 0), (4, 0), (1, 0), (5, 0), (2, 0), (6, 0), (4, 1), (7, 0), (5, 1), (3, 0), (6, 1), (7, 1)]

PROJECT = [[("q", c, 0), ("q", c, 1), ("k", c, 0), ("k", c, 1), ("v", c, 0), ("v", c, 1)] for c in range(KI)]
NORM = [("x", u, ki) for u in range(2) for ki in range(KI)]
OUTS = [("o", 2), ("o", 3)]
TURN_SLOT, BACK_SLOT, HIGH_SLOT = 22, 26, 29
BEHIND = 16
WEIGH_LAG = 6
SPLIT_MAX_SLOT = 36
PART_SLOTS = ((4, 7, 10, 13), (5, 8, 13, 15))


def small_work(kind):
    last = kind == "last"
    at = [dict() for _ in range(GROUPS)]
    for g in range(GROUPS):
        if g < GROUPS - 1 or not last:
            at[g][40] = ("m", (g + 1) % GROUPS)
    for n, item in enumerate(PROJECT[1]):
        at[0][1 + 3 * n] = item
    at[GROUPS - 1].update({36: ("o", 0), 45: ("o", 1)})
    if kind != "first":
        at[0].update({20: ("o", 2), 26: ("o", 3)})
    if not last:
        for n, item in enumerate(NORM):
            at[1][(2, 5, 37, 43)[n]] = item
        for n, item in enumerate(PROJECT[0]):
            at[2][(1, 4, 9, 11, 14, 17)[n]] = item
    return at


def is_ahead(item):
    return item[0] == "x" or (item[0] in "qkv" and item[1] == 0) or item == ("m", 0)


def owner(item, b):
    return b + 1 if is_ahead(item) else b - 1 if item in OUTS else b


def order_of(kind):
    at = small_work(kind)
    return [at[g][n] for g in range(GROUPS) for n in sorted(at[g])]


BEFORE = NORM + PROJECT[0] + [("m", 0)]
PER = len(order_of("body"))


def attention_pass(nc, known, layer, x_dram, g_dram, out_dram, stack_dram, w_parts, w_out_parts, gammas, consts, small, s_qscale):
    biased = layer == 1
    passes = [(0, 0), (0, 1)] + ([(1, 0)] if len(w_parts) == 2 else [])
    HT = TILES // 2
    RP = 12
    BLKS = BANK // VW
    NE, NM = 3, 3

    with ExitStack() as ctx:
        def sb(nm, shape, dt):
            return ctx.enter_context(nc.sbuf_tensor(f"a{layer}_{nm}", shape, dt))

        def ps(nm, n):
            return ctx.enter_context(nc.psum_tensor(f"a{layer}_{nm}", [P, n, BANK], F32))

        counts = []

        def sem(nm):
            counts.append(semaphore(nc, known, f"att_{nm}"))
            return counts[-1]

        x_in = sb("x_in", [P, HT, D], F32)
        bn = sb("bn", [P, HT, 6], F32)
        mv = sb("mv", [P, HT, 2], F32)
        var_eps = sb("var_eps", [P, HT], F32)
        rstd = sb("rstd", [P, HT], F32)
        minus_half = sb("minus_half", [P, HT], F32)
        xT = [sb(f"xT{i}", [P, KI, T], F32R) for i in range(2)]
        qk = sb("qk", [P, 2, BANK], F32)
        rest = sb("rest", [P, 2, BANK], F32)
        parts = sb("parts", [P, 2, 3, T], BF16)
        q_stack = sb("q_stack", [P, HEADS, T], BF16)
        k_stack = sb("k_stack", [P, HEADS, T], BF16)
        v = sb("v", [P, TILES, HEADS, VW], F32)
        max_in = sb("max_in", [P, 2, 2, HG, TILES], F32)
        max_tmp = sb("max_tmp", [P, 2, HG, TILES], F32)
        max_parts = sb("max_parts", [P, TILES, HG, MAXROWS], BF16)
        maxT = sb("maxT", [HG * MAXROWS, T], BF16)
        junk = sb("junk", [P, NM, BANK], BF16)
        mask_add = sb("mask_add", [P, BANK], BF16)
        ident_b = sb("ident_b", [P, P], BF16)
        probs = sb("probs", [P, RP, BANK], F32)
        turned = sb("turned", [P, BLKS, VW], F32)
        inverse = sb("inverse", [P, BLKS], F32)
        pair = sb("pair", [P, 2, BLKS, 2, DH], F32)
        attn_raw = sb("attn_raw", [P, BANK], F32)
        attn = [sb(f"attn{i}", [P, KI, T], F32R) for i in range(2)]
        x_old = sb("x_old", [P, 4, D], F32)
        g_in = sb("g_in", [P, 4, D], F32)
        s_scaled = sb("s_scaled", [P, 2, 2 * D], F32)

        ps_exp = ps("ps_exp", NE)
        ps_max = ps("ps_max", NM)
        ps_small = ps("ps_small", 1)
        ps_pv = ps("ps_pv", 1)

        x_loaded, bn_done, stats_done, rstd_done, xn_done = (
            sem("x_loaded"), sem("bn_done"), sem("stats_done"), sem("rstd_done"), sem("xn_done"))
        const_set, dve_set, stood_alone = sem("const_set"), sem("dve_set"), sem("stood_alone")
        small_full = sem("small_full")
        xT_high, xT_ready = sem("xT_high"), sem("xT_ready")
        qk_ready, high_done, rest_done, mid_done, low_done = (
            sem("qk_ready"), sem("high_done"), sem("rest_done"), sem("mid_done"), sem("low_done"))
        parts_stored, stack_loaded, v_ready = sem("parts_stored"), sem("stack_loaded"), sem("v_ready")
        max_full, max_taken = sem("max_full"), sem("max_taken")
        neg_step = sem("neg_step")
        max_step, max_split, maxT_ready, maxT_loaded = sem("max_step"), sem("max_split"), sem("maxT_ready"), sem("maxT_loaded")
        masked = sem("masked")
        exp_full, exp_done, pv_done = sem("exp_full"), sem("exp_done"), sem("pv_done")
        pv_turned, inverted, pair_done, turned_back = sem("pv_turned"), sem("inverted"), sem("pair_done"), sem("turned_back")
        attn_high, attn_ready = sem("attn_high"), sem("attn_ready")
        ends_loaded = [sem("ends_loaded_even"), sem("ends_loaded_odd")]
        out_stored = [sem("out_stored_even"), sem("out_stored_odd")]
        s_done, gated, x_added = sem("s_done"), sem("gated"), sem("x_added")
        block = ctx.enter_context(nc.Block())

        ident = consts[:, C_IDENT:C_IDENT + P]
        x_half = x_dram.rearrange("(k i p) d -> k p i d", i=HT, p=P)
        x_pair = x_dram.rearrange("(k i p) d -> k p i d", i=2, p=P)
        g_pair = g_dram.rearrange("(k i p) d -> k p i d", i=2, p=P)
        out_pair = out_dram.rearrange("(k i p) d -> k p i d", i=2, p=P)

        def rows(view, k):
            return view[bass.ds(k, 1)].rearrange("o p i d -> p (o i) d")

        def pair_of(buf, i):
            return buf[:, 2 * (i % 2):2 * (i % 2) + 2]

        def flat(ap):
            return ap.rearrange("p i d -> p (i d)")

        order = {"before": BEFORE, "first": order_of("first"), "body": order_of("body"),
                 "last": order_of("last"), "behind": OUTS}

        def small_count(kind, it, key):
            n = order[kind].index(key) + 1
            if kind == "before":
                return n
            n = n + len(BEFORE)
            if kind == "first":
                return n
            n = n + len(order["first"])
            if kind == "behind":
                return n + (B - 2) * PER + len(order["last"])
            return n + (it - 1) * PER

        def group_no(b, g):
            return b * GROUPS + g

        def step_no(b, g, s):
            return group_no(b, g) * len(STEPS) + s

        def lead_tile(g, n):
            groups, tile = (1, n + LEAD) if n + LEAD < SLOTS else (2, n + LEAD - SLOTS)
            return (g + groups) // GROUPS, (g + groups) % GROUPS, tile

        def width(t, j):
            start = max(j * P, t * BANK)
            return start, (t + 1) * BANK - start

        @block.sync
        def _(sp):
            for s in counts:
                sp.sem_inc(s, BASE)

            def load_x(b, u):
                sp.wait_ge(xT_ready, BASE + (b * 2 + u) * KI)
                sp.dma_start(x_in[:], rows(x_half, b * 2 + u)).then_inc(x_loaded, 16)

            def stack(b, c):
                sp.wait_ge(low_done, BASE + (b * KI + c) * 4 + 4)
                sp.wait_ge(stack_loaded, BASE + (b * KI + c - 1) * 192)
                sp.dma_start(stack_dram[c].rearrange("q w p t -> p q w t"), parts[:]).then_inc(parts_stored, 16)
                sp.wait_ge(parts_stored, BASE + (b * KI + c + 1) * 16)
                sp.wait_ge(pv_done, BASE + step_no(b - 1, 2 * c + 1, len(STEPS) - 1) + 1)
                for s in range(SPLITS // DH):
                    for dst, w, which in ((q_stack, 0, Q_PARTS[s]), (k_stack, 1, K_PARTS[s])):
                        sp.dma_start(dst[s * DH:(s + 1) * DH, c * HC:(c + 1) * HC, :],
                                     stack_dram[c, w, which].rearrange("(h d) t -> d h t", d=DH)).then_inc(stack_loaded, 16)

            def load_max(b, g):
                if g == 0:
                    sp.wait_ge(const_set, BASE + CONSTS_SET)
                sp.wait_ge(maxT_ready, BASE + group_no(b, g) + 1)
                for h in range(HG):
                    sp.dma_start(q_stack[MAX_AT:P, g * HG + h, :],
                                 maxT[h * MAXROWS:(h + 1) * MAXROWS, :]).then_inc(maxT_loaded, 16)

            def load_ends(b, i):
                sp.wait_ge(out_stored[i % 2], BASE + (b * 2 + i // 2) * 16)
                sp.dma_start(pair_of(x_old, i), rows(x_pair, b * 4 + i)).then_inc(ends_loaded[i % 2], 16)
                sp.dma_start(pair_of(g_in, i), rows(g_pair, b * 4 + i)).then_inc(ends_loaded[i % 2], 16)

            def store_ends(b, i):
                sp.wait_ge(x_added, BASE + b * 4 + i + 1)
                sp.dma_start(rows(out_pair, b * 4 + i), pair_of(x_old, i)).then_inc(out_stored[i % 2], 16)

            def sequence(b, kind):
                more = kind != "last"
                if more:
                    load_x(b + 1, 0)
                stack(b, 1)
                if kind != "first":
                    store_ends(b - 1, 2)
                    store_ends(b - 1, 3)
                load_ends(b, 0)
                load_ends(b, 1)
                load_max(b, 1)
                if more:
                    load_x(b + 1, 1)
                load_max(b, 2)
                if more:
                    stack(b + 1, 0)
                load_max(b, 3)
                store_ends(b, 0)
                if more:
                    load_max(b + 1, 0)
                store_ends(b, 1)
                load_ends(b, 2)
                load_ends(b, 3)

            load_x(0, 0)
            load_x(0, 1)
            stack(0, 0)
            load_max(0, 0)
            sequence(0, "first")
            with sp.Fori(1, B - 1) as b:
                sequence(b, "body")
            sequence(B - 1, "last")
            store_ends(B - 1, 2)
            store_ends(B - 1, 3)
            sp.wait_ge(out_stored[0], BASE + B * 32)
            sp.wait_ge(out_stored[1], BASE + B * 32)

        @block.gpsimd
        def _(pool):
            nc.gpsimd.memset(minus_half[:], -0.5).then_inc(const_set, 1)
            pool.wait_ge(const_set, BASE + 1)

            def inverse_deviation(b, u):
                pool.wait_ge(stats_done, BASE + (b * 2 + u) * 5 + 5)
                nc.gpsimd.tensor_tensor(rstd[:], var_eps[:], minus_half[:], ALU.pow).then_inc(rstd_done, 1)

            def rest_of(b, c, n):
                no = (b * KI + c) * 4 + n
                w, cols = n // 2, slice((n % 2) * BANK, (n % 2 + 1) * BANK)
                pool.wait_ge(high_done, BASE + no + 1)
                pool.wait_ge(low_done, BASE + no - 1)
                nc.gpsimd.tensor_tensor(rest[:, n % 2], qk[:, n % 2], parts[:, w, 0, cols],
                                        ALU.subtract).then_inc(rest_done, 1)

            def low_part(b, c, n):
                no = (b * KI + c) * 4 + n
                w, cols = n // 2, slice((n % 2) * BANK, (n % 2 + 1) * BANK)
                pool.wait_ge(mid_done, BASE + no + 1)
                nc.gpsimd.tensor_tensor(parts[:, w, 2, cols], rest[:, n % 2], parts[:, w, 1, cols],
                                        ALU.subtract).then_inc(low_done, 1)

            zero = pool.to_reg(0.0)

            def mask(b, g, s):
                at = s * HG % RP
                pool.wait_ge(exp_done, BASE + step_no(b, g, s) * HG + HG)
                pool.sem_inc(stood_alone, 1)
                block_ = probs[:, at:at + HG, 0:P]
                nc.gpsimd.affine_select(block_, block_, [[0, HG], [1, P]], ALU.is_ge, zero, base=0,
                                        channel_multiplier=-1).then_inc(masked, 1)

            def split_max(b, g):
                gn = group_no(b, g)
                pool.wait_ge(max_step, BASE + gn * 4 + 1)
                pool.wait_ge(maxT_ready, BASE + gn)
                pool.sem_inc(stood_alone, 1)
                top = max_parts[:].rearrange("p i h w -> p h i w")
                nc.gpsimd.tensor_copy(top[:, :, :, 0], max_tmp[:, 0]).then_inc(max_step, 1)
                pool.wait_ge(max_step, BASE + gn * 4 + 2)
                nc.gpsimd.tensor_tensor(max_tmp[:, 1], max_tmp[:, 0], top[:, :, :, 0], ALU.subtract).then_inc(max_step, 1)
                pool.wait_ge(max_step, BASE + gn * 4 + 3)
                pool.sem_inc(stood_alone, 1)
                nc.gpsimd.tensor_copy(top[:, :, :, 1], max_tmp[:, 1]).then_inc(max_step, 1)
                pool.wait_ge(max_step, BASE + gn * 4 + 4)
                nc.gpsimd.tensor_tensor(top[:, :, :, 2], max_tmp[:, 1], top[:, :, :, 1], ALU.subtract).then_inc(max_split, 1)

            def normalise(b, g, t):
                no = group_no(b, g) * 2 + t
                pool.wait_ge(inverted, BASE + no + 1)
                pool.wait_ge(turned_back, BASE + (b * KI + g // 2) * 2 + t - 1)
                nc.gpsimd.tensor_tensor(pair[:, t, :, g % 2], turned[:, :, 0:DH],
                                        inverse[:].unsqueeze(2).broadcast_to([P, BLKS, DH]),
                                        ALU.mult).then_inc(pair_done, 1)

            def low_attention(b, c, t):
                no = (b * KI + c) * 2 + t
                pool.wait_ge(attn_high, BASE + no + 1)
                cols = slice(t * BANK, (t + 1) * BANK)
                nc.gpsimd.tensor_tensor(attn[1][:, c, cols], attn_raw[:], attn[0][:, c, cols].bitcast(F32),
                                        ALU.subtract).then_inc(attn_ready, 1)

            def add(b, i):
                no = b * 4 + i
                pool.wait_ge(ends_loaded[i % 2], BASE + (b * 2 + i // 2 + 1) * 32)
                pool.wait_ge(s_done, BASE + no + 1)
                gate, new = flat(pair_of(g_in, i)), flat(pair_of(x_old, i))
                nc.gpsimd.tensor_tensor(gate, s_scaled[:, i % 2], gate, ALU.mult).then_inc(gated, 1)
                pool.wait_ge(gated, BASE + no + 1)
                nc.gpsimd.tensor_tensor(new, gate, new, ALU.add).then_inc(x_added, 1)

            def sequence(b, kind):
                at, last = small_work(kind), kind == "last"
                for g in range(GROUPS):
                    bg, gg = (b, g - 1) if g else (b - 1, GROUPS - 1)
                    for n in range(SLOTS):
                        item = at[g].get(n, ("",))
                        if not last and LN_WORK.get((g, n), ("",))[0] == "aggregate":
                            inverse_deviation(b + 1, LN_WORK[g, n][1])
                        if n == TURN_SLOT:
                            normalise(b, g, 0)
                        if n == TURN_SLOT - BEHIND and (g or kind != "first"):
                            normalise(bg, gg, 1)
                        if item[0] in ("q", "k"):
                            what, c, u = item
                            rest_of(b + 1 - c, c, (2 if what == "k" else 0) + u)
                        if g in (0, 2) and n in PART_SLOTS[g // 2] and not (g == 2 and last):
                            low_part(b + g // 2, 1 - g // 2, PART_SLOTS[g // 2].index(n))
                        if n == HIGH_SLOT and g % 2:
                            low_attention(b, g // 2, 0)
                        if n == HIGH_SLOT - BEHIND and (g == 2 or (g == 0 and kind != "first")):
                            low_attention(bg, gg // 2, 1)
                        if n == SPLIT_MAX_SLOT and not (last and g == GROUPS - 1):
                            split_max(b + (g + 1) // GROUPS, (g + 1) % GROUPS)
                        if item[0] == "o":
                            add(owner(item, b), item[1])
                        if n % HG == HG - 1 and n // HG in DIAGONAL:
                            mask(b, g, n // HG)

            inverse_deviation(0, 0)
            nc.gpsimd.memset(v[:], 1.0).then_inc(const_set, 1)
            inverse_deviation(0, 1)
            pool.wait_ge(const_set, BASE + 2)
            pool.wait_ge(rstd_done, BASE + 2)
            nc.gpsimd.memset(q_stack[SPLITS:P], 0.0).then_inc(const_set, 1)
            nc.gpsimd.memset(k_stack[SPLITS:P], 1.0).then_inc(const_set, 1)
            pool.wait_ge(const_set, BASE + CONSTS_SET)
            for n in range(4):
                rest_of(0, 0, n)
                low_part(0, 0, n)
            split_max(0, 0)
            sequence(0, "first")
            with pool.Fori(1, B - 1) as b:
                sequence(b, "body")
            sequence(B - 1, "last")
            normalise(B - 1, GROUPS - 1, 1)
            low_attention(B - 1, 1, 1)
            for _, i in OUTS:
                add(B - 1, i)

        @block.scalar
        def _(act):
            def take_xT(sec, it, b, u, ki):
                act.wait_ge(small_full, BASE + small_count(sec, it, ("x", u, ki)))
                nc.scalar.activation(xT[0][:, ki, u * BANK:(u + 1) * BANK], ps_small[:, 0],
                                     ACT.Copy).then_inc(xT_high, 1)

            def take_qk(sec, it, b, what, c, u):
                n = (2 if what == "k" else 0) + u
                no = (b * KI + c) * 4 + n
                act.wait_ge(small_full, BASE + small_count(sec, it, (what, c, u)))
                act.wait_ge(rest_done, BASE + no - 1)
                scale, bias = 1.0, 0.0
                if what == "q":
                    scale = s_qscale if layer == 0 else DH ** -0.5
                if biased:
                    at = (S_QB if what == "q" else S_KB) + c
                    bias = small[:, at:at + 1]
                nc.scalar.activation(qk[:, n % 2], ps_small[:, 0], ACT.Identity, scale=scale, bias=bias).then_inc(qk_ready, 1)
                w, cols = n // 2, slice((n % 2) * BANK, (n % 2 + 1) * BANK)
                act.wait_ge(parts_stored, BASE + (b * KI + c) * 16)
                act.wait_ge(qk_ready, BASE + no + 1)
                nc.scalar.activation(parts[:, w, 0, cols], ps_small[:, 0], ACT.Identity, scale=scale,
                                     bias=bias).then_inc(high_done, 1)

            def middle_part(b, c, n):
                no = (b * KI + c) * 4 + n
                w, cols = n // 2, slice((n % 2) * BANK, (n % 2 + 1) * BANK)
                act.wait_ge(rest_done, BASE + no + 1)
                nc.scalar.activation(parts[:, w, 1, cols], rest[:, n % 2], ACT.Copy).then_inc(mid_done, 1)

            def take_v(sec, it, b, c, u):
                act.wait_ge(small_full, BASE + small_count(sec, it, ("v", c, u)))
                act.wait_ge(pv_done, BASE + step_no(b - 1, 2 * c + 1, len(STEPS) - 1) + 1)
                act.wait_ge(const_set, BASE + CONSTS_SET)
                dst = v[:, u * HT:(u + 1) * HT, c * HC:(c + 1) * HC, 0:DH]
                src = ps_small[:, 0].rearrange("p (i h d) -> p i h d", i=HT, d=DH)
                nc.scalar.activation(dst, src, ACT.Copy).then_inc(v_ready, 1)

            def take_max(sec, it, b, g):
                act.wait_ge(small_full, BASE + small_count(sec, it, ("m", g)))
                act.wait_ge(maxT_loaded, BASE + group_no(b, g) * 64)
                src = ps_small[0:HG * MAXROWS, 0].bitcast(BF16)
                nc.scalar.activation(maxT[:], src, ACT.Copy).then_inc(maxT_ready, 1)

            def high_attention(b, c, t):
                act.wait_ge(turned_back, BASE + (b * KI + c) * 2 + t + 1)
                act.wait_ge(s_done, BASE + b * 4)
                nc.scalar.activation(attn[0][:, c, t * BANK:(t + 1) * BANK], attn_raw[:], ACT.Copy).then_inc(attn_high, 1)

            def exponential(b, g, n):
                s, h = n // HG, n % HG
                no = step_no(b, g, s) * HG + h
                _, w = width(*STEPS[s])
                act.wait_ge(exp_full, BASE + no + 1)
                act.wait_ge(pv_done, BASE + step_no(b, g, s) + 1 - RP // HG)
                nc.scalar.activation(probs[:, n % RP, 0:w], ps_exp[:, n % NE, 0:w], ACT.Exp).then_inc(exp_done, 1)

            def sequence(b, kind):
                at, last = small_work(kind), kind == "last"
                for g in range(GROUPS):
                    for n in range(SLOTS):
                        if n in at[g]:
                            small_item(kind, b, at[g][n], owner(at[g][n], b))
                        if g in (0, 2) and n in PART_SLOTS[g // 2] and not (g == 2 and last):
                            middle_part(b + g // 2, 1 - g // 2, PART_SLOTS[g // 2].index(n))
                        exponential(b, g, n)
                        if n == HIGH_SLOT and g % 2:
                            high_attention(b, g // 2, 0)
                        if n == HIGH_SLOT - BEHIND:
                            if g == 2:
                                high_attention(b, 0, 1)
                            elif g == 0 and kind != "first":
                                high_attention(b - 1, 1, 1)

            def small_item(sec, it, key, b):
                kind = key[0]
                if kind == "x":
                    take_xT(sec, it, b, key[1], key[2])
                elif kind in "qk":
                    take_qk(sec, it, b, kind, key[1], key[2])
                elif kind == "v" and not biased:
                    take_v(sec, it, b, key[1], key[2])
                elif kind == "m":
                    take_max(sec, it, b, key[1])

            for key in BEFORE:
                small_item("before", 0, key, 0)
                if key[0] in "qk":
                    middle_part(0, 0, (2 if key[0] == "k" else 0) + key[2])
            sequence(0, "first")
            with act.Fori(1, B - 1) as b:
                sequence(b, "body")
            sequence(B - 1, "last")
            high_attention(B - 1, 1, 1)

        @block.vector
        def _(dve):
            nc.vector.memset(mask_add[:, 0:BANK - P], 0.0).then_inc(dve_set, 1)
            nc.vector.tensor_copy(mask_add[:, BANK - P:BANK], consts[:, C_MAXMASK:C_MAXMASK + P]).then_inc(dve_set, 1)
            nc.vector.tensor_copy(ident_b[:], ident).then_inc(dve_set, 1)
            nc.vector.memset(max_in[:], LOWEST).then_inc(dve_set, 1)
            dve.wait_ge(dve_set, BASE + 4)

            def statistics(b, u, i):
                if i == 0:
                    dve.wait_ge(x_loaded, BASE + (b * 2 + u + 1) * 16)
                nc.vector.bn_stats(bn[:, i], x_in[:, i]).then_inc(bn_done, 1)

            def aggregate(b, u):
                no = b * 2 + u
                dve.wait_ge(bn_done, BASE + no * 4 + 4)
                dve.sem_inc(stood_alone, 1)
                for i in range(HT):
                    nc.vector.bn_aggr(mv[:, i], bn[:, i]).then_inc(stats_done, 1)
                dve.wait_ge(stats_done, BASE + no * 5 + 4)
                nc.vector.tensor_scalar(var_eps[:], mv[:, :, 1], EPS_LN, None, ALU.add).then_inc(stats_done, 1)

            def norm(b, u, i):
                if i == 0:
                    dve.wait_ge(rstd_done, BASE + b * 2 + u + 1)
                ins = nc.vector.tensor_scalar(x_in[:, i], x_in[:, i], mv[:, i, 0:1], rstd[:, i:i + 1],
                                              ALU.subtract, ALU.mult)
                if i == HT - 1:
                    ins.then_inc(xn_done, 1)

            def low_xT(sec, it, b, u, ki):
                no = (b * 2 + u) * KI + ki
                dve.wait_ge(xT_high, BASE + no + 1)
                cols = slice(u * BANK, (u + 1) * BANK)
                nc.vector.tensor_tensor(xT[1][:, ki, cols], ps_small[:, 0], xT[0][:, ki, cols].bitcast(F32),
                                        ALU.subtract).then_inc(xT_ready, 1)

            def take_v(sec, it, b, c, u):
                dve.wait_ge(small_full, BASE + small_count(sec, it, ("v", c, u)))
                dve.wait_ge(pv_done, BASE + step_no(b - 1, 2 * c + 1, len(STEPS) - 1) + 1)
                dst = v[:, u * HT:(u + 1) * HT, c * HC:(c + 1) * HC, 0:DH]
                src = ps_small[:, 0].rearrange("p (i h d) -> p i h d", i=HT, d=DH)
                for i in range(HT):
                    bias = small[:, S_VB + c * P:S_VB + (c + 1) * P].rearrange("p (h d) -> p h d", d=DH)
                    ins = nc.vector.tensor_tensor(dst[:, i], src[:, i], bias, ALU.add)
                ins.then_inc(v_ready, 1)

            def maximum(b, g, tile):
                no = group_no(b, g) * SLOTS + tile
                h, (i, piece) = tile // 12, PIECES[tile % 12]
                w = min((i + 1) * P - piece * BANK, BANK)
                if tile == 0:
                    dve.wait_ge(neg_step, BASE + group_no(b, g) - 1)
                dve.wait_ge(max_full, BASE + no + 1)
                out = max_in[:, g % 2, piece, h, i:i + 1]
                src = ps_max[:, tile % NM, 0:w]
                if i * P < (piece + 1) * BANK:
                    dve.sem_inc(stood_alone, 1)
                    nc.vector.tensor_tensor_reduce(junk[:, tile % NM, 0:w], src, mask_add[:, BANK - w:BANK], 1.0, LOWEST,
                                                   ALU.add, ALU.max, out).then_inc(max_taken, 1)
                else:
                    nc.vector.tensor_reduce(out, src, AX.X, ALU.max).then_inc(max_taken, 1)

            def negate_max(b, g):
                gn = group_no(b, g)
                dve.wait_ge(max_taken, BASE + (gn + 1) * SLOTS)
                dve.wait_ge(max_split, BASE + gn)
                nc.vector.scalar_tensor_tensor(max_tmp[:, 1], max_in[:, g % 2, 0], 1.0, max_in[:, g % 2, 1],
                                               ALU.mult, ALU.max).then_inc(neg_step, 1)
                dve.wait_ge(neg_step, BASE + gn + 1)
                nc.vector.tensor_scalar(max_tmp[:, 0], max_tmp[:, 1], -1.0, None, ALU.mult).then_inc(max_step, 1)

            def turn(b, g, t):
                no = group_no(b, g) * 2 + t
                dve.wait_ge(pv_done, BASE + step_no(b, g, 3 if t == 0 else 11) + 1)
                dve.wait_ge(pair_done, BASE + no)
                nc.vector.transpose(turned[:].rearrange("p k c -> p (k c)"), ps_pv[:, 0]).then_inc(pv_turned, 1)
                dve.wait_ge(pv_turned, BASE + no + 1)
                nc.vector.reciprocal(inverse[:], turned[:, :, DH]).then_inc(inverted, 1)

            def turn_back(b, c, t):
                dve.wait_ge(pair_done, BASE + group_no(b, 2 * c + 1) * 2 + t + 1)
                dve.wait_ge(attn_ready, BASE + (b * KI + c) * 2 + t)
                nc.vector.transpose(attn_raw[:], pair[:, t].rearrange("p k e d -> p (k e d)")).then_inc(turned_back, 1)

            def scale_out(sec, it, b, i):
                no = b * 4 + i
                dve.wait_ge(small_full, BASE + small_count(sec, it, ("o", i)))
                dve.wait_ge(gated, BASE + no - 1)
                out = s_scaled[:, i % 2]
                if biased:
                    bias = small[:, S_PB:S_PB + D]
                    for j in range(2):
                        ins = nc.vector.tensor_tensor(out[:, j * D:(j + 1) * D], ps_small[:, 0, j * D:(j + 1) * D],
                                                      bias, ALU.add)
                    ins.then_inc(s_done, 1)
                else:
                    nc.vector.tensor_scalar(out, ps_small[:, 0], gammas[:, 5:6], None, ALU.mult).then_inc(s_done, 1)

            def small_item(sec, it, key, b):
                kind = key[0]
                if kind == "x":
                    low_xT(sec, it, b, key[1], key[2])
                elif kind == "v" and biased:
                    take_v(sec, it, b, key[1], key[2])
                elif kind == "o":
                    scale_out(sec, it, b, key[1])

            def sequence(b, kind):
                at, last = small_work(kind), kind == "last"
                for g in range(GROUPS):
                    bg, gg = (b, g - 1) if g else (b - 1, GROUPS - 1)
                    for n in range(SLOTS):
                        if n in at[g]:
                            small_item(kind, b, at[g][n], owner(at[g][n], b))
                        if not last and (g, n) in LN_WORK:
                            what, u, i = LN_WORK[g, n]
                            if what == "statistics":
                                statistics(b + 1, u, i)
                            elif what == "aggregate":
                                aggregate(b + 1, u)
                            else:
                                norm(b + 1, u, i)
                        if n == TURN_SLOT:
                            turn(b, g, 0)
                        if n == BACK_SLOT and g % 2:
                            turn_back(b, g // 2, 0)
                        if n == TURN_SLOT - BEHIND and (g or kind != "first"):
                            turn(bg, gg, 1)
                        if n == BACK_SLOT - BEHIND and (g == 2 or (g == 0 and kind != "first")):
                            turn_back(bg, gg // 2, 1)
                        ahead, mg, tile = lead_tile(g, n)
                        if last and ahead:
                            continue
                        maximum(b + ahead, mg, tile)
                        if tile == SLOTS - 1:
                            negate_max(b + ahead, mg)

            for u in range(2):
                for i in range(HT):
                    statistics(0, u, i)
                aggregate(0, u)
                for i in range(HT):
                    norm(0, u, i)
                for ki in range(KI):
                    low_xT("before", 0, 0, u, ki)
            for key in PROJECT[0]:
                small_item("before", 0, key, 0)
            for tile in range(SLOTS):
                maximum(0, 0, tile)
            negate_max(0, 0)
            for tile in range(LEAD):
                maximum(0, 1, tile)
            sequence(0, "first")
            with dve.Fori(1, B - 1) as b:
                sequence(b, "body")
            sequence(B - 1, "last")
            turn(B - 1, GROUPS - 1, 1)
            turn_back(B - 1, 1, 1)
            for _, i in OUTS:
                scale_out("behind", B - 1, B - 1, i)

        @block.tensor
        def _(pe):
            out = ps_small[:, 0]

            def taken(item, b):
                kind = item[0]
                if kind == "x":
                    return xT_ready, (b * 2 + item[1]) * KI + item[2] + 1
                if kind in "qk":
                    return high_done, (b * KI + item[1]) * 4 + (2 if kind == "k" else 0) + item[2] + 1
                if kind == "v":
                    return v_ready, (b * KI + item[1]) * 2 + item[2] + 1
                if kind == "m":
                    return maxT_ready, group_no(b, item[1]) + 1
                return s_done, b * 4 + item[1] + 1

            def project(b, what, c, u):
                pe.wait_ge(xT_ready, BASE + (b + 1) * 2 * KI)
                for ki in range(KI):
                    for n, (wp, xp) in enumerate(passes):
                        ins = nc.tensor.matmul(out, w_parts[wp][:, "qk".index(what), ki, c * P:(c + 1) * P],
                                               xT[xp][:, ki, u * BANK:(u + 1) * BANK],
                                               start=(ki == 0 and n == 0), stop=(ki == KI - 1 and n == len(passes) - 1))
                ins.then_inc(small_full, 1)

            def values(c, u):
                for i in range(HT):
                    tile = slice((u * HT + i) * P, (u * HT + i + 1) * P)
                    for ki in range(KI):
                        for n, (wp, xp) in enumerate(passes):
                            ins = nc.tensor.matmul(out[:, i * P:(i + 1) * P], xT[xp][:, ki, tile],
                                                   w_parts[wp][:, 2, ki, c * P:(c + 1) * P],
                                                   start=(ki == 0 and n == 0),
                                                   stop=(ki == KI - 1 and n == len(passes) - 1))
                ins.then_inc(small_full, 1)

            def turn_x(b, u, ki):
                pe.wait_ge(xn_done, BASE + b * 2 + u + 1)
                for i in range(HT):
                    ins = nc.tensor.transpose(out[:, i * P:(i + 1) * P], x_in[:, i, ki * P:(ki + 1) * P], ident)
                ins.then_inc(small_full, 1)

            def turn_max(b, g):
                pe.wait_ge(max_split, BASE + group_no(b, g) + 1)
                to = out[0:HG * MAXROWS].bitcast(BF16)
                for i in range(TILES):
                    ins = nc.tensor.transpose(to[:, i * P:(i + 1) * P],
                                              max_parts[:, i].rearrange("p h w -> p (h w)"), ident_b[:])
                ins.then_inc(small_full, 1)

            def project_out(b, i):
                pe.wait_ge(attn_ready, BASE + (b * KI + KI - 1) * 2 + i // 2 + 1)
                for j in range(2):
                    tile = slice((2 * i + j) * P, (2 * i + j + 1) * P)
                    for c in range(KI):
                        for n, (wp, ap) in enumerate(passes):
                            ins = nc.tensor.matmul(out[:, j * D:(j + 1) * D], attn[ap][:, c, tile], w_out_parts[wp][:, c],
                                                   start=(c == 0 and n == 0),
                                                   stop=(c == KI - 1 and n == len(passes) - 1))
                ins.then_inc(small_full, 1)

            def small_item(item, b, before):
                for it, bb in before:
                    s, count = taken(it, bb)
                    pe.wait_ge(s, BASE + count)
                kind = item[0]
                if kind == "x":
                    turn_x(b, item[1], item[2])
                elif kind in "qk":
                    project(b, kind, item[1], item[2])
                elif kind == "v":
                    values(item[1], item[2])
                elif kind == "m":
                    turn_max(b, item[1])
                else:
                    project_out(b, item[1])

            def max_tile(b, g, tile):
                no = group_no(b, g) * SLOTS + tile
                head, (i, piece) = g * HG + tile // 12, PIECES[tile % 12]
                w = min((i + 1) * P - piece * BANK, BANK)
                if tile == 0:
                    c = g // 2
                    pe.wait_ge(stack_loaded, BASE + (b * KI + c + 1) * 192)
                pe.wait_ge(max_taken, BASE + no - NM + 1)
                nc.tensor.matmul(ps_max[:, tile % NM, 0:w], q_stack[0:MAX_AT, head, i * P:(i + 1) * P],
                                 k_stack[0:MAX_AT, head, piece * BANK:piece * BANK + w],
                                 start=True, stop=True).then_inc(max_full, 1)

            def scores(b, g, n):
                s, h = n // HG, n % HG
                t, j = STEPS[s]
                head = g * HG + h
                q0, w = width(t, j)
                no = step_no(b, g, s) * HG + h
                if n == 0:
                    pe.wait_ge(maxT_loaded, BASE + (group_no(b, g) + 1) * 64)
                pe.wait_ge(exp_done, BASE + no - NE + 1)
                nc.tensor.matmul(ps_exp[:, n % NE, 0:w], k_stack[:, head, j * P:(j + 1) * P],
                                 q_stack[:, head, q0:q0 + w], start=True, stop=True).then_inc(exp_full, 1)

            def weigh(b, g, s):
                t, j = STEPS[s]
                q0, w = width(t, j)
                first, last = s in (0, 4), s in (3, len(STEPS) - 1)
                if s in DIAGONAL:
                    pe.wait_ge(masked, BASE + group_no(b, g) * len(DIAGONAL) + DIAGONAL.index(s) + 1)
                else:
                    pe.wait_ge(exp_done, BASE + step_no(b, g, s) * HG + HG)
                if first:
                    pe.wait_ge(pv_turned, BASE + group_no(b, g) * 2 + t)
                    if t == 0:
                        pe.wait_ge(v_ready, BASE + (b * KI + g // 2 + 1) * 2)
                for h in range(HG):
                    ins = nc.tensor.matmul(ps_pv[h * VW:(h + 1) * VW, 0, q0 - t * BANK:q0 - t * BANK + w],
                                           v[:, j, g * HG + h], probs[:, (s * HG + h) % RP, 0:w],
                                           start=first, stop=last)
                ins.then_inc(pv_done, 1)

            def sequence(b, kind):
                at, last = small_work(kind), kind == "last"
                before = [(("m", 0), b)]
                for g in range(GROUPS):
                    for n in range(SLOTS):
                        if n in at[g]:
                            item = at[g][n]
                            small_item(item, owner(item, b), before)
                            before = [(item, owner(item, b))]
                        scores(b, g, n)
                        behind = n - WEIGH_LAG - (HG - 1)
                        if behind % HG == 0:
                            if behind >= 0:
                                weigh(b, g, behind // HG)
                            elif g:
                                weigh(b, g - 1, len(STEPS) + behind // HG)
                            elif kind != "first":
                                weigh(b - 1, GROUPS - 1, len(STEPS) + behind // HG)
                        ahead, mg, tile = lead_tile(g, n)
                        if not (last and ahead):
                            max_tile(b + ahead, mg, tile)

            pe.wait_ge(dve_set, BASE + 4)
            before = []
            for item in BEFORE[:-1]:
                small_item(item, 0, before)
                before = [(item, 0)]
            pe.wait_ge(const_set, BASE + CONSTS_SET)
            for tile in range(SLOTS):
                max_tile(0, 0, tile)
            small_item(BEFORE[-1], 0, before)
            for tile in range(LEAD):
                max_tile(0, 1, tile)
            sequence(0, "first")
            with pe.Fori(1, B - 1) as b:
                sequence(b, "body")
            sequence(B - 1, "last")
            for n in range(WEIGH_LAG // HG, -1, -1):
                weigh(B - 1, GROUPS - 1, len(STEPS) - 1 - n)
            before = [(("o", 1), B - 1)]
            for item in OUTS:
                small_item(item, B - 1, before)
                before = [(item, B - 1)]


def build(nc, x, consts_dram, small_dram, a0_w, a0_wo, f0_up, f0_down, a1_w, a1_wo, f1_up, f1_down, out):
    known = {}
    g_dram = nc.dram_tensor("gate", [B * T, D], F32).ap()
    x1_dram = nc.dram_tensor("x_after_layer_0", [B * T, D], F32).ap()
    stack_dram = nc.dram_tensor("qk_parts", [KI, 2, 3, P, T], BF16).ap()
    with ExitStack() as ctx:
        consts = ctx.enter_context(nc.sbuf_tensor("consts", [P, C_END], F32))
        small = ctx.enter_context(nc.sbuf_tensor("small", [P, S_END], F32))
        gammas = ctx.enter_context(nc.sbuf_tensor("gammas", [P, 8], F32))
        with ExitStack() as c0:
            loaded = nc.alloc_semaphore("consts_loaded")
            bias_scaled = nc.alloc_semaphore("bias_scaled")
            block = c0.enter_context(nc.Block())

            @block.sync
            def _(sp):
                sp.dma_start(consts[:], consts_dram).then_inc(loaded, 16)
                sp.dma_start(small[:], small_dram).then_inc(loaded, 16)

            @block.vector
            def _(dve):
                dve.wait_ge(loaded, 32)
                q_bias = small[:, S_QB:S_QB + KI]
                nc.vector.tensor_scalar(q_bias, q_bias, DH ** -0.5, None, ALU.mult).then_inc(bias_scaled, 1)
                dve.wait_ge(bias_scaled, 1)

        with ExitStack() as c0:
            up = c0.enter_context(nc.sbuf_tensor("f0_up", [P, 2, KI, 6, P], F32R))
            down = c0.enter_context(nc.sbuf_tensor("f0_down", [P, 6, D], F32R))
            wide = KI * 6 * P
            count = HID[0] * D
            ternary_weights(nc, "f0u", f0_up, 2 * wide, up[:].rearrange("p w k c m -> p (w k c m)"),
                         [(0, wide, 6), (wide, wide, 7)], 0.0, 1e-8, count, gammas)
            ternary_weights(nc, "f0d", f0_down, 6 * D, down[:].rearrange("p c d -> p (c d)"),
                         [(0, 6 * D, 6)], 0.0, 1e-8, count, gammas)
            ffn_pass(nc, known, 0, x, g_dram, [up], [down], gammas, consts)
        with ExitStack() as c0:
            w = c0.enter_context(nc.sbuf_tensor("a0_w", [P, 3, KI, D], F32R))
            wo = c0.enter_context(nc.sbuf_tensor("a0_wo", [P, KI, D], F32R))
            wide = KI * D
            ternary_weights(nc, "a0w", a0_w, 3 * wide, w[:].rearrange("p w k m -> p (w k m)"),
                         [(i * wide, wide, i) for i in range(3)], 1e-5, 0.0, D * D, gammas)
            ternary_weights(nc, "a0o", a0_wo, wide, wo[:].rearrange("p c d -> p (c d)"),
                         [(0, wide, 3)], 1e-5, 0.0, D * D, gammas)
            scales(nc, gammas)
            attention_pass(nc, known, 0, x, g_dram, x1_dram, stack_dram, [w], [wo], gammas, consts, small, gammas[:, 4:5])
        with nc.Block() as block:
            @block.sync
            def _(sp):
                for s in known.values():
                    sp.sem_clear(s)

        with ExitStack() as c0:
            up = [c0.enter_context(nc.sbuf_tensor(f"f1_up{i}", [P, 2, KI, 8, P], F32R)) for i in range(2)]
            down = [c0.enter_context(nc.sbuf_tensor(f"f1_down{i}", [P, 8, D], F32R)) for i in range(2)]
            flat_up = [u[:].rearrange("p w k c m -> p (w k c m)") for u in up]
            flat_down = [d[:].rearrange("p c d -> p (c d)") for d in down]
            split_weights(nc, "f1u", f1_up, 2 * KI * 8 * P, *flat_up)
            split_weights(nc, "f1d", f1_down, 8 * D, *flat_down)
            ffn_pass(nc, known, 1, x1_dram, g_dram, up, down, gammas, consts)
        with ExitStack() as c0:
            w = [c0.enter_context(nc.sbuf_tensor(f"a1_w{i}", [P, 3, KI, D], F32R)) for i in range(2)]
            wo = [c0.enter_context(nc.sbuf_tensor(f"a1_wo{i}", [P, KI, D], F32R)) for i in range(2)]
            flat_w = [u[:].rearrange("p w k m -> p (w k m)") for u in w]
            split_weights(nc, "a1w", a1_w, 3 * KI * D, *flat_w)
            split_weights(nc, "a1o", a1_wo, KI * D, *[u[:].rearrange("p c d -> p (c d)") for u in wo])
            attention_pass(nc, known, 1, x1_dram, g_dram, out, stack_dram, w, wo, gammas, consts, small, None)


def scales(nc, gammas):
    with ExitStack() as ctx:
        made = nc.alloc_semaphore("scales_made")
        block = ctx.enter_context(nc.Block())

        @block.vector
        def _(dve):
            nc.vector.tensor_scalar(gammas[:, 4:5], gammas[:, 0:1], gammas[:, 1:2], DH ** -0.5,
                                    ALU.mult, ALU.mult).then_inc(made, 1)
            nc.vector.tensor_scalar(gammas[:, 5:6], gammas[:, 2:3], gammas[:, 3:4], None,
                                    ALU.mult).then_inc(made, 1)
            dve.wait_ge(made, 2)


def laid_out(inputs):
    import numpy as np

    f = {k: np.asarray(v) for k, v in inputs.items()}

    def by_row(w):
        return w.reshape(-1, P, w.shape[1]).transpose(1, 0, 2)

    def out_rows(w):
        return w.reshape(KI, 2, HG, DH, D).transpose(2, 1, 3, 0, 4)

    def thirds(ws):
        return np.stack([by_row(w) for w in ws], 1)

    pad = 6 * P - HID[0]
    f0 = np.stack([by_row(np.pad(f[n].T, ((0, 0), (0, pad)))) for n in ("L0_ffn_w1", "L0_ffn_w2")], 1)
    f0d = by_row(np.pad(f["L0_ffn_w3"].T, ((0, pad), (0, 0))))

    def fours(w):
        k = by_row(w)
        return k.reshape(P, KI, 2, P, 4).transpose(0, 1, 2, 4, 3).reshape(P, KI, 8 * P)

    f1 = np.stack([fours(f[n]) for n in ("L1_ffn_w_gate", "L1_ffn_w_up")], 1)
    f1d = f["L1_ffn_w_down"].reshape(2, P, 4, D).transpose(1, 0, 2, 3)
    wa, ba = f["L1_attn_W_attn"], f["L1_attn_b_attn"]

    consts = np.zeros((P, C_END), np.float32)
    p, c = np.arange(P)[:, None], np.arange(P)[None, :]
    consts[:, C_IDENT:C_IDENT + P] = p == c
    consts[:, C_MAXMASK:C_END] = np.where(c > p, NEG, 0.0)
    small = np.zeros((P, S_END), ba.dtype)
    small[:, S_QB:S_QB + KI] = ba[0:D].reshape(KI, P).T
    small[:, S_KB:S_KB + KI] = ba[D:2 * D].reshape(KI, P).T
    small[:, S_VB:S_VB + D] = ba[None, 2 * D:]
    small[:, S_PB:S_PB + D] = f["L1_attn_b_proj"][None]

    def rows(a):
        return np.ascontiguousarray(a.reshape(P, -1))

    return {
        "x": f["L0_attn_x"].reshape(B * T, D), "consts": consts, "small": small,
        "a0_w": rows(thirds([f[f"L0_attn_w{n}"].T for n in "qkv"])), "a0_wo": rows(out_rows(f["L0_attn_wo"].T)),
        "f0_up": rows(f0), "f0_down": rows(f0d),
        "a1_w": rows(thirds([wa[:, i * D:(i + 1) * D] for i in range(3)])), "a1_wo": rows(out_rows(f["L1_attn_W_proj"])),
        "f1_up": rows(f1), "f1_down": rows(f1d),
    }


def kernel(**inputs):
    import numpy as _np
    import concourse.bacc as _bacc
    from concourse import mybir as _mybir
    from concourse.bass_utils import run_bass_kernel_spmd as _run

    nc = _bacc.Bacc("TRN2", target_bir_lowering=False, num_devices=1)
    arrays, args = {}, []
    for name, a in laid_out(inputs).items():
        a = _np.ascontiguousarray(a)
        arrays[f"in_{name}"] = a
        args.append(nc.dram_tensor(f"in_{name}", a.shape, _mybir.dt.from_np(a.dtype), kind="ExternalInput").ap())
    out = nc.dram_tensor("out_x", (B * T, D), F32, kind="ExternalOutput").ap()
    build(nc, *args, out)
    r = _run(nc, [arrays], core_ids=[0])
    return r.results[0]["out_x"].reshape(B, T, D)
```

```python
from contextlib import ExitStack

import concourse.bass as bass
from concourse import mybir

F32 = mybir.dt.float32
F32R = mybir.dt.float32r
BF16 = mybir.dt.bfloat16
ALU = mybir.AluOpType
ACT = mybir.ActivationFunctionType
AX = mybir.AxisListType

P = 128
BANK = 512
B, T, D = 4, 1024, 256
HEADS, DH = 16, 16
KI = D // P
TILES = T // P
HG = 4
GROUPS = HEADS // HG
HC = P // DH
VW = 32
HID = (704, 1024)
EPS_LN = 1e-5
NEG = -1e30
LOWEST = -3e38
SPLITS = 96
MAXROWS = 3
MAX_AT = P - MAXROWS
Q_PARTS = (0, 0, 0, 1, 1, 2)
K_PARTS = (0, 1, 2, 0, 1, 0)
C_IDENT, C_MAXMASK = 0, 128
C_END = C_MAXMASK + P
S_QB, S_KB, S_VB, S_PB = 0, KI, 2 * KI, 2 * KI + D
S_END = 2 * KI + 2 * D


BASE = 512


def semaphore(nc, known, name):
    if name not in known:
        known[name] = nc.alloc_semaphore(name)
    return known[name]


class SplitWeights:

    def __init__(self, nc, name, matrices):
        step = 1024
        starts = [sum(m[1] for m in matrices[:n]) for n in range(len(matrices))]
        self.nc, self.columns = nc, sum(m[1] for m in matrices)
        self.pieces = [[a[:, c0:min(c0 + step, m[1])] for a in (m[0], m[2], m[3])] + [start + c0, min(step, m[1] - c0)]
                       for m, start in zip(matrices, starts) for c0 in range(0, m[1], step)]
        self.loaded = [nc.alloc_semaphore(f"{name}_loaded{n}") for n in range(len(self.pieces))]
        self.high_done = nc.alloc_semaphore(f"{name}_high_done")
        self.low_done = nc.alloc_semaphore(f"{name}_low_done")

    def load(self, sp):
        for (dram, _, _, at, w), s in zip(self.pieces, self.loaded):
            sp.dma_start(self.raw[:, at:at + w], dram).then_inc(s, 16)

    def scalar(self, act):
        for (_, high, _, at, w), s in zip(self.pieces, self.loaded):
            act.wait_ge(s, 16)
            self.nc.scalar.activation(high, self.raw[:, at:at + w], ACT.Copy).then_inc(self.high_done, 1)

    def tensor(self, pe):
        pass

    def vector_begin(self, dve):
        pass

    def ones(self, dve):
        pass

    def vector(self, dve, i):
        _, high, low, at, w = self.pieces[i]
        dve.wait_ge(self.high_done, i + 1)
        self.nc.vector.tensor_tensor(low, self.raw[:, at:at + w], high.bitcast(F32),
                                     ALU.subtract).then_inc(self.low_done, 1)

    def ready(self, engine):
        engine.wait_ge(self.low_done, len(self.pieces))


class TernaryWeights:

    def __init__(self, nc, name, matrices, floor, eps, count, gammas, g0, scaled=False):
        starts = [sum(w for _, w, _ in matrices[:n]) for n in range(len(matrices))]
        self.nc, self.gammas, self.g0, self.n, self.scaled = nc, gammas, g0, len(matrices), scaled
        self.floor, self.eps, self.count = floor, eps, count
        self.pieces = [(dram, out, at, w) for at, (dram, w, out) in zip(starts, matrices)]
        self.width = sum(w for _, w, _ in matrices)
        self.columns = 2 * self.width + P + 3 * self.n
        self.loaded = [nc.alloc_semaphore(f"{name}_loaded{i}") for i in range(self.n)]
        self.summed = nc.alloc_semaphore(f"{name}_summed")
        self.totalled = nc.alloc_semaphore(f"{name}_totalled")
        self.gamma_step = nc.alloc_semaphore(f"{name}_gamma_step")
        self.below_done = nc.alloc_semaphore(f"{name}_below_done")
        self.parts_done = nc.alloc_semaphore(f"{name}_parts_done")

    def areas(self):
        w, n = self.width, self.n
        ones = 2 * w
        sums = ones + P
        return (self.raw[:, 0:w], self.raw[:, w:2 * w], self.raw[:, ones:sums], self.raw[:, sums:sums + n],
                self.raw[:, sums + n:sums + 2 * n], self.raw[:, sums + 2 * n:sums + 3 * n])

    def load(self, sp):
        raw = self.areas()[0]
        for (dram, _, at, w), s in zip(self.pieces, self.loaded):
            sp.dma_start(raw[:, at:at + w], dram).then_inc(s, 16)

    def scalar(self, act):
        raw, second, _, sums, _, _ = self.areas()
        for i, (_, _, at, w) in enumerate(self.pieces):
            act.wait_ge(self.loaded[i], 16)
            self.nc.scalar.activation(second[:, at:at + w], raw[:, at:at + w], ACT.Abs,
                                      accum_out=sums[:, i:i + 1]).then_inc(self.summed, 1)
        if self.scaled:
            act.wait_ge(self.gamma_step, 5)

    def tensor(self, pe):
        _, _, ones, sums, _, _ = self.areas()
        pe.wait_ge(self.summed, self.n + 1)
        self.nc.tensor.matmul(self.total[:, 0:self.n], ones, sums, start=True, stop=True).then_inc(self.totalled, 1)

    def vector_begin(self, dve):
        _, _, _, _, above, below = self.areas()
        gamma = self.gammas[:, self.g0:self.g0 + self.n]
        dve.wait_ge(self.totalled, 1)
        self.nc.vector.tensor_scalar(gamma, self.total[:, 0:self.n], 1.0 / self.count, self.floor,
                                     ALU.mult, ALU.max).then_inc(self.gamma_step, 1)
        dve.wait_ge(self.gamma_step, 1)
        self.nc.vector.tensor_scalar(above, gamma, self.eps, 0.5, ALU.add, ALU.mult).then_inc(self.gamma_step, 1)
        self.nc.vector.tensor_scalar(below, gamma, self.eps, -0.5, ALU.add, ALU.mult).then_inc(self.gamma_step, 1)
        if self.scaled:
            g = self.gammas
            self.nc.vector.tensor_scalar(g[:, 4:5], g[:, 0:1], g[:, 1:2], DH ** -0.5, ALU.mult,
                                         ALU.mult).then_inc(self.gamma_step, 1)
            self.nc.vector.tensor_scalar(g[:, 5:6], g[:, 2:3], g[:, 3:4], None, ALU.mult).then_inc(self.gamma_step, 1)
        dve.wait_ge(self.gamma_step, 5 if self.scaled else 3)

    def ones(self, dve):
        self.nc.vector.memset(self.areas()[2], 1.0).then_inc(self.summed, 1)

    def vector(self, dve, i):
        raw, second, _, _, above, below = self.areas()
        _, out, at, w = self.pieces[i]
        cols = slice(at, at + w)
        self.nc.vector.tensor_scalar(second[:, cols], raw[:, cols], below[:, i:i + 1], None,
                                     ALU.is_lt).then_inc(self.below_done, 1)
        dve.wait_ge(self.below_done, i + 1)
        self.nc.vector.scalar_tensor_tensor(out, raw[:, cols], above[:, i:i + 1], second[:, cols],
                                            ALU.is_gt, ALU.subtract).then_inc(self.parts_done, 1)

    def ready(self, engine):
        engine.wait_ge(self.parts_done, self.n)


def layer_norm(nc, dve, k, section, sems, bufs):
    x_loaded, bn_done, stats_done, rstd_done, xn_done, stood_alone, turned = sems
    x_in, xn, bn, mv, var_eps, rstd = bufs
    if section == 0:
        dve.wait_ge(x_loaded, BASE + (k + 1) * 16)
    if section < 2:
        for i in (2 * section, 2 * section + 1):
            nc.vector.bn_stats(bn[:, i], x_in[:, i]).then_inc(bn_done, 1)
    if section == 1:
        dve.wait_ge(bn_done, BASE + k * 4 + 4)
        dve.sem_inc(stood_alone, 1)
        for i in range(4):
            nc.vector.bn_aggr(mv[:, i], bn[:, i]).then_inc(stats_done, 1)
        dve.wait_ge(stats_done, BASE + k * 5 + 4)
        nc.vector.tensor_scalar(var_eps[:], mv[:, :, 1], EPS_LN, None, ALU.add).then_inc(stats_done, 1)
    if section == 2:
        dve.wait_ge(rstd_done, BASE + k + 1)
        dve.wait_ge(turned, BASE + k * KI)
    if section >= 2:
        for i in (2 * section - 4, 2 * section - 3):
            ins = nc.vector.tensor_scalar(xn[:, i], x_in[:, i], mv[:, i, 0:1], rstd[:, i:i + 1],
                                          ALU.subtract, ALU.mult)
        if section == 3:
            ins.then_inc(xn_done, 1)


def ffn_pass(nc, known, layer, x_dram, g_dram, weights, w_up_parts, w_down_parts, consts):
    sparse = layer == 1
    NCH = 4 if sparse else 3
    BLOCKS = B * T // BANK
    BT = BANK // P
    MEMB = [P] * 8 if sparse else [P] * 5 + [HID[0] - 5 * P]
    NW = len(w_up_parts)
    passes = [(0, 0), (0, 1)] + ([(1, 0)] if NW == 2 else [])

    with ExitStack() as ctx:
        def sb(nm, shape, dt):
            return ctx.enter_context(nc.sbuf_tensor(f"f{layer}_{nm}", shape, dt))

        counts = []

        def sem(nm):
            counts.append(semaphore(nc, known, f"ffn_{nm}"))
            return counts[-1]

        x_in = sb("x_in", [P, BT, D], F32)
        xn = sb("xn", [P, BT, D], F32)
        bn = sb("bn", [P, BT, 6], F32)
        mv = sb("mv", [P, BT, 2], F32)
        var_eps = sb("var_eps", [P, BT], F32)
        rstd = sb("rstd", [P, BT], F32)
        minus_half = sb("minus_half", [P, BT], F32)
        xT = [sb(f"xT{i}", [P, 2, KI, BANK], F32R) for i in range(2)]
        act_gate = sb("act_gate", [P, 2, BANK], F32)
        hid = sb("hid", [P, 2, NCH, BANK], F32)
        hT = [sb(f"hT{i}", [P, 2, NCH, BANK], F32R) for i in range(2)]
        sig = sb("sig", [P, 2, BANK], F32)
        g_out = sb("g_out", [P, BT, D], F32)
        if sparse:
            mag = sb("mag", [P, NCH, BANK], F32)
            beats = sb("beats", [P, 6, BANK], BF16)
            votes = sb("votes", [P, 4, BANK], BF16)
            half_votes = sb("half_votes", [P, 4, BANK], BF16)
        ps_up = ctx.enter_context(nc.psum_tensor(f"f{layer}_ps_up", [P, 4, BANK], F32))
        ps_xT = ctx.enter_context(nc.psum_tensor(f"f{layer}_ps_xT", [P, KI, BANK], F32))
        ps_down = ctx.enter_context(nc.psum_tensor(f"f{layer}_ps_down", [P, 2, BANK], F32))
        weights.raw = sb("raw", [P, weights.columns], F32)[:]
        weights.total = ps_down[:, 0]

        x_loaded, bn_done, stats_done, rstd_done, xn_done = (
            sem("x_loaded"), sem("bn_done"), sem("stats_done"), sem("rstd_done"), sem("xn_done"))
        half_set, stood_alone = sem("half_set"), sem("stood_alone")
        turned, xT_high, xT_ready = sem("turned"), sem("xT_high"), sem("xT_ready")
        gate_full, up_full, gate_taken, hid_done = sem("gate_full"), sem("up_full"), sem("gate_taken"), sem("hid_done")
        mag_done, beats_done, votes_done, kept = sem("mag_done"), sem("beats_done"), sem("votes_done"), sem("kept")
        high_done, low_done = sem("high_done"), sem("low_done")
        down_done, sig_done, g_done, g_stored = sem("down_done"), sem("sig_done"), sem("g_done"), sem("g_stored")
        block = ctx.enter_context(nc.Block())
        ident = consts[:, C_IDENT:C_IDENT + P]

        def n_par(half, m):
            return (half * NCH + m) % 2

        x_v = x_dram.rearrange("(k i p) d -> k p i d", i=BT, p=P)
        g_v = g_dram.rearrange("(k i p) d -> k p i d", i=BT, p=P)

        def rows(v, k):
            return v[bass.ds(k, 1)].rearrange("o p i d -> p (o i) d")

        def over_blocks(engine, periods):
            periods(0, 0, "first")
            with engine.Fori(0, BLOCKS // 2 - 1) as i:
                periods(i * 2 + 1, 1, "body")
                periods(i * 2 + 2, 0, "body")
            periods(BLOCKS - 1, 1, "last")

        @block.sync
        def _(sp):
            sp.dma_start(x_in[:], rows(x_v, 0)).then_inc(x_loaded, 16)
            weights.load(sp)
            for s in counts:
                sp.sem_inc(s, BASE)

            def body(k):
                sp.wait_ge(xn_done, BASE + k)
                sp.dma_start(x_in[:], rows(x_v, k)).then_inc(x_loaded, 16)

            def store(k):
                sp.wait_ge(g_done, BASE + k * 2 + 2)
                sp.dma_start(rows(g_v, k), g_out[:]).then_inc(g_stored, 16)

            body(1)
            body(2)
            with sp.Fori(3, BLOCKS) as k:
                body(k)
                store(k - 3)
            store(BLOCKS - 3)
            store(BLOCKS - 2)
            store(BLOCKS - 1)
            sp.wait_ge(g_stored, BASE + 16 * BLOCKS)

        @block.gpsimd
        def _(pool):
            nc.gpsimd.memset(minus_half[:], -0.5).then_inc(half_set, 1)
            pool.wait_ge(half_set, BASE + 1)

            def inverse_deviation(k):
                pool.wait_ge(stats_done, BASE + k * 5 + 5)
                nc.gpsimd.tensor_tensor(rstd[:], var_eps[:], minus_half[:], ALU.pow).then_inc(rstd_done, 1)

            def low_parts(k, half):
                for m in range(NCH):
                    n = k * 2 * NCH + half * NCH + m
                    w = MEMB[half * NCH + m]
                    pool.wait_ge(high_done, BASE + n + 1)
                    nc.gpsimd.tensor_tensor(hT[1][0:w, half, m], hid[0:w, half, m], hT[0][0:w, half, m].bitcast(F32),
                                            ALU.subtract).then_inc(low_done, 1)

            def periods(k, odd, kind):
                if kind != "last":
                    inverse_deviation(k + 1)
                if kind != "first":
                    low_parts(k - 1, 1)
                low_parts(k, 0)

            inverse_deviation(0)
            over_blocks(pool, periods)
            low_parts(BLOCKS - 1, 1)

        @block.scalar
        def _(act):
            def take_xT(k, odd):
                for ki in range(KI):
                    act.wait_ge(turned, BASE + k * KI + ki + 1)
                    if ki == 0:
                        act.wait_ge(up_full, BASE + (k - 1) * 2 * NCH)
                    nc.scalar.activation(xT[0][:, odd, ki], ps_xT[:, ki], ACT.Copy).then_inc(xT_high, 1)

            def chunk_gate(k, half, m):
                n = k * 2 * NCH + half * NCH + m
                w = MEMB[half * NCH + m]
                act.wait_ge(gate_full, BASE + n + 1)
                act.wait_ge(hid_done, BASE + n - 1)
                func = ACT.Silu if sparse else ACT.Sigmoid
                nc.scalar.activation(act_gate[0:w, n_par(half, m)], ps_up[0:w, 2 * n_par(half, m)],
                                     func).then_inc(gate_taken, 1)

            def magnitude(k, half, m):
                n = k * 2 * NCH + half * NCH + m
                act.wait_ge(hid_done, BASE + n + 1)
                if m == 0:
                    act.wait_ge(beats_done, BASE + (k * 2 + half) * 6)
                nc.scalar.activation(mag[:, m], hid[:, half, m], ACT.Abs).then_inc(mag_done, 1)

            def high_part(k, half, m):
                n = k * 2 * NCH + half * NCH + m
                w = MEMB[half * NCH + m]
                act.wait_ge(kept if sparse else hid_done, BASE + n + 1)
                if m == 0:
                    act.wait_ge(down_done, BASE + k * 2 + half - 1)
                nc.scalar.activation(hT[0][0:w, half, m], hid[0:w, half, m], ACT.Copy).then_inc(high_done, 1)

            def out_sigmoid(k):
                act.wait_ge(down_done, BASE + k * 2 + 2)
                act.wait_ge(g_done, BASE + k * 2)
                for t in range(2):
                    func = ACT.Silu if sparse else ACT.Sigmoid
                    if sparse and t == 0:
                        act.wait_ge(g_stored, BASE + k * 16)
                    out = g_out[:, 2 * t:2 * t + 2].rearrange("p i d -> p (i d)") if sparse else sig[:, t]
                    ins = nc.scalar.activation(out, ps_down[:, t], func)
                    ins.then_inc(g_done if sparse else sig_done, 1)

            def periods(k, odd, kind):
                for half in range(2):
                    before = (k, 0) if half else (k - 1, 1)
                    for m in range(NCH):
                        chunk_gate(k, half, m)
                        if sparse and m:
                            magnitude(k, half, m - 1)
                        if not sparse and (half or kind != "first"):
                            high_part(*before, m)
                        if m == NCH - 2 and half and kind != "last":
                            take_xT(k + 1, 1 - odd)
                    if sparse:
                        magnitude(k, half, NCH - 1)
                        for m in range(NCH):
                            if half or kind != "first":
                                high_part(*before, m)
                    if half and kind != "first":
                        out_sigmoid(k - 1)

            weights.scalar(act)
            take_xT(0, 0)
            over_blocks(act, periods)
            for m in range(NCH):
                high_part(BLOCKS - 1, 1, m)
            out_sigmoid(BLOCKS - 1)

        ln_sems = (x_loaded, bn_done, stats_done, rstd_done, xn_done, stood_alone, turned)
        ln_bufs = (x_in, xn, bn, mv, var_eps, rstd)

        @block.vector
        def _(dve):
            def low_xT(k, odd):
                for ki in range(KI):
                    dve.wait_ge(xT_high, BASE + k * KI + ki + 1)
                    nc.vector.tensor_tensor(xT[1][:, odd, ki], ps_xT[:, ki], xT[0][:, odd, ki].bitcast(F32),
                                            ALU.subtract).then_inc(xT_ready, 1)

            def hidden(k, half, m):
                n = k * 2 * NCH + half * NCH + m
                w = MEMB[half * NCH + m]
                dve.wait_ge(gate_taken, BASE + n + 1)
                dve.wait_ge(up_full, BASE + n + 1)
                dve.wait_ge(low_done, BASE + (k * 2 + half - 2) * NCH + m + 1)
                nc.vector.tensor_tensor(hid[0:w, half, m], ps_up[0:w, 2 * n_par(half, m) + 1],
                                        act_gate[0:w, n_par(half, m)], ALU.mult).then_inc(hid_done, 1)

            def two_of_four(k, half, section):
                q = k * 2 + half
                pairs = [(0, 1), (0, 2), (0, 3), (1, 2), (1, 3), (2, 3)]
                if section == 0:
                    dve.wait_ge(mag_done, BASE + (q + 1) * NCH)
                    dve.wait_ge(kept, BASE + q * NCH)
                for c, (i, j) in enumerate(pairs):
                    if section == c // 4:
                        nc.vector.tensor_tensor(beats[:, c], mag[:, i], mag[:, j], ALU.is_ge).then_inc(beats_done, 1)
                if section == 1:
                    dve.wait_ge(beats_done, BASE + q * 6 + 6)
                    first = [(0, 1, ALU.add), (3, 0, ALU.subtract), (5, 1, ALU.subtract), (2, 4, ALU.add)]
                    for c, (i, j, op) in enumerate(first):
                        nc.vector.tensor_tensor(half_votes[:, c], beats[:, i], beats[:, j], op).then_inc(votes_done, 1)
                if section == 2:
                    second = [(2, ALU.add), (4, ALU.add), (3, ALU.subtract), (5, ALU.add)]
                    dve.wait_ge(votes_done, BASE + q * 8 + 4)
                    for c, (j, op) in enumerate(second):
                        nc.vector.tensor_tensor(votes[:, c], half_votes[:, c], beats[:, j], op).then_inc(votes_done, 1)
                if section == 3:
                    keep = [(2.0, ALU.is_ge), (1.0, ALU.is_ge), (0.0, ALU.is_ge), (1.0, ALU.is_le)]
                    dve.wait_ge(votes_done, BASE + q * 8 + 8)
                    for m, (bound, op) in enumerate(keep):
                        nc.vector.scalar_tensor_tensor(hid[:, half, m], votes[:, m], bound, hid[:, half, m],
                                                       op, ALU.mult).then_inc(kept, 1)

            def out_gate(k):
                for t in range(2):
                    dve.wait_ge(sig_done, BASE + k * 2 + t + 1)
                    if t == 0:
                        dve.wait_ge(g_stored, BASE + k * 16)
                    nc.vector.tensor_tensor(g_out[:, 2 * t:2 * t + 2].rearrange("p i d -> p (i d)"), ps_down[:, t],
                                            sig[:, t], ALU.mult).then_inc(g_done, 1)

            def periods(k, odd, kind):
                for half in range(2):
                    before = (k, 0) if half else (k - 1, 1)
                    for m in range(NCH):
                        if sparse and (half or kind != "first"):
                            two_of_four(*before, m)
                        if half == 0 and kind != "last":
                            layer_norm(nc, dve, k + 1, m, ln_sems, ln_bufs)
                        if half and kind != "last" and m == NCH - 1:
                            low_xT(k + 1, 1 - odd)
                        hidden(k, half, m)
                    if half == 0 and kind != "last" and NCH == 3:
                        layer_norm(nc, dve, k + 1, 3, ln_sems, ln_bufs)
                    if half and kind != "first" and not sparse:
                        out_gate(k - 1)

            weights.ones(dve)
            for m in range(4):
                layer_norm(nc, dve, 0, m, ln_sems, ln_bufs)
            weights.vector_begin(dve)
            low_xT(0, 0)
            for i in range(len(weights.pieces)):
                weights.vector(dve, i)
            over_blocks(dve, periods)
            if sparse:
                for section in range(4):
                    two_of_four(BLOCKS - 1, 1, section)
            else:
                out_gate(BLOCKS - 1)

        @block.tensor
        def _(pe):
            def turn(k):
                for ki in range(KI):
                    if ki == 0:
                        pe.wait_ge(xn_done, BASE + k + 1)
                    pe.wait_ge(xT_ready, BASE + (k - 1) * KI + ki + 1)
                    for i in range(BT):
                        ins = nc.tensor.transpose(ps_xT[:, ki, i * P:(i + 1) * P], xn[:, i, ki * P:(ki + 1) * P], ident)
                    ins.then_inc(turned, 1)

            def up(k, odd, half, m):
                n = k * 2 * NCH + half * NCH + m
                w = MEMB[half * NCH + m]
                if half == 0 and m == 0:
                    pe.wait_ge(xT_ready, BASE + k * KI + KI)
                for which, taken, full in ((0, gate_taken, gate_full), (1, hid_done, up_full)):
                    pe.wait_ge(taken, BASE + n - 1)
                    out = ps_up[0:w, 2 * n_par(half, m) + which]
                    for ki in range(KI):
                        for c, (wp, xp) in enumerate(passes):
                            ins = nc.tensor.matmul(out, w_up_parts[wp][:, which, ki, half * NCH + m, 0:w],
                                                   xT[xp][:, odd, ki], start=(ki == 0 and c == 0),
                                                   stop=(ki == KI - 1 and c == len(passes) - 1))
                    ins.then_inc(full, 1)

            def down(k, half):
                q = k * 2 + half
                pe.wait_ge(low_done, BASE + (q + 1) * NCH)
                if half == 0:
                    pe.wait_ge(g_done, BASE + k * 2)
                for i in range(BT):
                    for m in range(NCH):
                        w = MEMB[half * NCH + m]
                        for c, (wp, hp) in enumerate(passes):
                            ins = nc.tensor.matmul(
                                ps_down[:, i // 2, (i % 2) * D:(i % 2 + 1) * D], hT[hp][0:w, half, m, i * P:(i + 1) * P],
                                w_down_parts[wp][0:w, half * NCH + m],
                                start=(half == 0 and m == 0 and c == 0 and i % 2 == 0),
                                stop=(half == 1 and m == NCH - 1 and c == len(passes) - 1),
                                skip_group_check=True)
                ins.then_inc(down_done, 1)

            def periods(k, odd, kind):
                for half in range(2):
                    for m in range(NCH):
                        up(k, odd, half, m)
                        if m == 1 and half and kind != "last":
                            turn(k + 1)
                        if m == NCH - 2 and kind != "first":
                            down(k - 1, half)

            weights.tensor(pe)
            turn(0)
            weights.ready(pe)
            over_blocks(pe, periods)
            down(BLOCKS - 1, 0)
            down(BLOCKS - 1, 1)



SLOTS = 48
LEAD = 18
LN_WORK = {(0, 19): ("aggregate", 0, 0), (1, 4): ("aggregate", 1, 0)}
for _i in range(4):
    LN_WORK[0, (11, 13, 15, 17)[_i]] = ("statistics", 0, _i)
    LN_WORK[0, (22, 24, 28, 30)[_i]] = ("norm", 0, _i)
    LN_WORK[(0, 0, 0, 1)[_i], (42, 44, 46, 1)[_i]] = ("statistics", 1, _i)
    LN_WORK[1, 7 + 2 * _i] = ("norm", 1, _i)
CONSTS_SET = 4
STEPS = [(0, j) for j in (0, 3, 1, 2)] + [(1, j) for j in (0, 7, 1, 6, 2, 5, 3, 4)]
DIAGONAL = [s for s, (t, j) in enumerate(STEPS) if j * P >= t * BANK]
PIECES = [(0, 0), (4, 0), (1, 0), (5, 0), (2, 0), (6, 0), (4, 1), (7, 0), (5, 1), (3, 0), (6, 1), (7, 1)]


PROJECT = [[("q", c, 0), ("q", c, 1), ("k", c, 0), ("k", c, 1)] for c in range(KI)]
VALUES = [[("v", c, 0), ("v", c, 1)] for c in range(KI)]
NORM = [("x", u, ki) for u in range(2) for ki in range(KI)]
OUTS = [("o", 2), ("o", 3)]
TURN_SLOT, BACK_SLOT, HIGH_SLOT = 21, 25, 30
BEHIND = 16
WEIGH_LAG = 5
SPLIT_MAX_SLOT = 33
QK_SLOTS = ((20, 24, 28, 32), (15, 18, 22, 26))
PART_SLOTS = ((23, 27, 31, 35), (18, 21, 25, 29))


def step_width(s):
    t, j = STEPS[s]
    return (t + 1) * BANK - max(j * P, t * BANK)


def tile_width(tile):
    i, piece = PIECES[tile % len(PIECES)]
    return min((i + 1) * P - piece * BANK, BANK)


def weighed_at(n):
    behind = n - WEIGH_LAG - (HG - 1)
    return behind // HG if behind % HG == 0 else None


def paced():
    v_cost = 4.4
    shares = []
    for n in range(SLOTS):
        s = weighed_at(n)
        shares.append((step_width(n // HG), 0 if s is None else v_cost * step_width(s % len(STEPS))))
    load = [tile_width(tile) + 64 for tile in range(SLOTS)]
    scale = sum(load) / sum(map(sum, shares))
    beside, tile, done, share = [], 0, 0, 0
    for own, v_own in shares:
        here = []
        for upto in (share + own + v_own / 2, share + own + v_own):
            here.append([])
            while tile < SLOTS and done + load[(tile + LEAD) % SLOTS] / 2 <= upto * scale:
                done += load[(tile + LEAD) % SLOTS]
                here[-1].append(tile + LEAD)
                tile += 1
        share += own + v_own
        beside.append(here)
    beside[-1][1] += range(tile + LEAD, SLOTS + LEAD)
    return beside


PACED = paced()


def lead_tiles(g, n, part):
    at = [(g + 1 + tile // SLOTS, tile % SLOTS) for tile in PACED[n][part]]
    return [(group // GROUPS, group % GROUPS, tile) for group, tile in at]


def small_work(kind):
    last = kind == "last"
    at = [dict() for _ in range(GROUPS)]
    for g in range(GROUPS):
        if g < GROUPS - 1 or not last:
            at[g][38] = ("m", (g + 1) % GROUPS)
    at[0].update(zip((7, 10), VALUES[1]))
    at[GROUPS - 1].update({36: ("o", 0), 45: ("o", 1)})
    if kind != "first":
        at[0].update({20: ("o", 2), 26: ("o", 3)})
    if not last:
        for n, item in enumerate(NORM):
            at[n // 2][(34, 37, 16, 18)[n]] = item
        for c in range(KI):
            at[1 + c].update(zip(QK_SLOTS[c], PROJECT[c]))
        at[2].update(zip((8, 11), VALUES[0]))
    return at


def is_ahead(item):
    return item[0] in "xqk" or item in VALUES[0] or item == ("m", 0)


def owner(item, b):
    return b + 1 if is_ahead(item) else b - 1 if item in OUTS else b


def order_of(kind):
    at = small_work(kind)
    return [at[g][n] for g in range(GROUPS) for n in sorted(at[g])]


BEFORE = NORM + PROJECT[0] + PROJECT[1] + VALUES[0] + [("m", 0)]
PER = len(order_of("body"))


def attention_pass(nc, known, layer, x_dram, g_dram, out_dram, stack_dram, weights, w_parts, w_out_parts, gammas, consts,
                   small, s_qscale):
    biased = layer == 1
    passes = [(0, 0), (0, 1)] + ([(1, 0)] if len(w_parts) == 2 else [])
    HT = TILES // 2
    RP = 12
    BLKS = BANK // VW
    NE, NM = 3, 3

    with ExitStack() as ctx:
        def sb(nm, shape, dt):
            return ctx.enter_context(nc.sbuf_tensor(f"a{layer}_{nm}", shape, dt))

        def ps(nm, n):
            return ctx.enter_context(nc.psum_tensor(f"a{layer}_{nm}", [P, n, BANK], F32))

        counts = []

        def sem(nm):
            counts.append(semaphore(nc, known, f"att_{nm}"))
            return counts[-1]

        x_in = sb("x_in", [P, HT, D], F32)
        bn = sb("bn", [P, HT, 6], F32)
        mv = sb("mv", [P, HT, 2], F32)
        var_eps = sb("var_eps", [P, HT], F32)
        rstd = sb("rstd", [P, HT], F32)
        minus_half = sb("minus_half", [P, HT], F32)
        xT = [sb(f"xT{i}", [P, KI, T], F32R) for i in range(2)]
        qk = sb("qk", [P, 2, BANK], F32)
        rest = sb("rest", [P, 2, BANK], F32)
        parts = sb("parts", [P, 2, 3, T], BF16)
        q_stack = sb("q_stack", [P, HEADS, T], BF16)
        k_stack = sb("k_stack", [P, HEADS, T], BF16)
        v = sb("v", [P, TILES, HEADS, VW], F32)
        max_in = sb("max_in", [P, 2, 2, HG, TILES], F32)
        max_tmp = sb("max_tmp", [P, 2, HG, TILES], F32)
        max_parts = sb("max_parts", [P, TILES, HG, MAXROWS], BF16)
        maxT = sb("maxT", [HG * MAXROWS, T], BF16)
        junk = sb("junk", [P, NM, BANK], BF16)
        mask_add = sb("mask_add", [P, BANK], BF16)
        ident_b = sb("ident_b", [P, P], BF16)
        probs = sb("probs", [P, RP, BANK], F32)
        turned = sb("turned", [P, BLKS, VW], F32)
        inverse = sb("inverse", [P, BLKS], F32)
        pair = sb("pair", [P, 2, BLKS, 2, DH], F32)
        attn_raw = sb("attn_raw", [P, BANK], F32)
        attn = [sb(f"attn{i}", [P, KI, T], F32R) for i in range(2)]
        x_old = sb("x_old", [P, 4, D], F32)
        g_in = sb("g_in", [P, 4, D], F32)
        s_scaled = sb("s_scaled", [P, 2, 2 * D], F32)

        ps_exp = ps("ps_exp", NE)
        ps_max = ps("ps_max", NM)
        ps_small = ps("ps_small", 1)
        ps_pv = ps("ps_pv", 1)
        weights.raw = probs[:].rearrange("p n w -> p (n w)")[:, 0:weights.columns]
        weights.total = ps_exp[:, 0]

        x_loaded, bn_done, stats_done, rstd_done, xn_done = (
            sem("x_loaded"), sem("bn_done"), sem("stats_done"), sem("rstd_done"), sem("xn_done"))
        x_1_loaded = sem("x_1_loaded")
        const_set, dve_set, stood_alone = sem("const_set"), sem("dve_set"), sem("stood_alone")
        small_full = sem("small_full")
        xT_high, xT_ready = sem("xT_high"), sem("xT_ready")
        qk_ready, high_done, rest_done, mid_done, low_done = (
            sem("qk_ready"), sem("high_done"), sem("rest_done"), sem("mid_done"), sem("low_done"))
        parts_stored, v_ready = sem("parts_stored"), sem("v_ready")
        stack_loaded = [sem(f"stack_{c}_loaded") for c in range(KI)]
        max_full, max_taken = sem("max_full"), sem("max_taken")
        neg_step = sem("neg_step")
        max_step, max_split, maxT_ready, maxT_loaded = sem("max_step"), sem("max_split"), sem("maxT_ready"), sem("maxT_loaded")
        masked = sem("masked")
        exp_full, exp_done, pv_done = sem("exp_full"), sem("exp_done"), sem("pv_done")
        pv_turned, inverted, pair_done, turned_back = sem("pv_turned"), sem("inverted"), sem("pair_done"), sem("turned_back")
        attn_high, attn_ready = sem("attn_high"), sem("attn_ready")
        ends_loaded = [sem("ends_loaded_even"), sem("ends_loaded_odd")]
        out_stored = [sem("out_stored_even"), sem("out_stored_odd")]
        s_done, gated, x_added = sem("s_done"), sem("gated"), sem("x_added")
        block = ctx.enter_context(nc.Block())

        ident = consts[:, C_IDENT:C_IDENT + P]
        x_half = x_dram.rearrange("(k i p) d -> k p i d", i=HT, p=P)
        x_pair = x_dram.rearrange("(k i p) d -> k p i d", i=2, p=P)
        g_pair = g_dram.rearrange("(k i p) d -> k p i d", i=2, p=P)
        out_pair = out_dram.rearrange("(k i p) d -> k p i d", i=2, p=P)

        def rows(view, k):
            return view[bass.ds(k, 1)].rearrange("o p i d -> p (o i) d")

        def pair_of(buf, i):
            return buf[:, 2 * (i % 2):2 * (i % 2) + 2]

        def flat(ap):
            return ap.rearrange("p i d -> p (i d)")

        order = {"before": BEFORE, "first": order_of("first"), "body": order_of("body"),
                 "last": order_of("last"), "behind": OUTS}

        def small_count(kind, it, key):
            n = order[kind].index(key) + 1
            if kind == "before":
                return n
            n = n + len(BEFORE)
            if kind == "first":
                return n
            n = n + len(order["first"])
            if kind == "behind":
                return n + (B - 2) * PER + len(order["last"])
            return n + (it - 1) * PER

        def small_bank(kind, item):
            return (ps_pv if kind == "before" and BEFORE.index(item) % 2 else ps_small)[:, 0]

        def group_no(b, g):
            return b * GROUPS + g

        def step_no(b, g, s):
            return group_no(b, g) * len(STEPS) + s

        def width(t, j):
            start = max(j * P, t * BANK)
            return start, (t + 1) * BANK - start

        @block.sync
        def _(sp):
            sp.dma_start(x_in[:], rows(x_half, 0)).then_inc(x_loaded, 16)
            sp.dma_start(x_old[:], rows(x_half, 1)).then_inc(x_1_loaded, 16)
            weights.load(sp)
            for s in counts:
                sp.sem_inc(s, BASE)

            def load_x(b, u):
                sp.wait_ge(xT_ready, BASE + (b * 2 + u) * KI)
                sp.dma_start(x_in[:], rows(x_half, b * 2 + u)).then_inc(x_loaded, 16)

            def store_parts(b, c):
                sp.wait_ge(low_done, BASE + (b * KI + c) * 4 + 4)
                sp.wait_ge(stack_loaded[c], BASE + b * 192)
                sp.dma_start(stack_dram[c].rearrange("q w p t -> p q w t"), parts[:]).then_inc(parts_stored, 16)

            def load_stack(b, c):
                sp.wait_ge(parts_stored, BASE + (b * KI + c + 1) * 16)
                sp.wait_ge(pv_done, BASE + step_no(b - 1, 2 * c + 1, len(STEPS) - 1) + 1)
                for s in range(SPLITS // DH):
                    for dst, w, which in ((q_stack, 0, Q_PARTS[s]), (k_stack, 1, K_PARTS[s])):
                        sp.dma_start(dst[s * DH:(s + 1) * DH, c * HC:(c + 1) * HC, :],
                                     stack_dram[c, w, which].rearrange("(h d) t -> d h t", d=DH)).then_inc(stack_loaded[c], 16)

            def load_max(b, g):
                if g == 0:
                    sp.wait_ge(const_set, BASE + CONSTS_SET)
                sp.wait_ge(maxT_ready, BASE + group_no(b, g) + 1)
                for h in range(HG):
                    sp.dma_start(q_stack[MAX_AT:P, g * HG + h, :],
                                 maxT[h * MAXROWS:(h + 1) * MAXROWS, :]).then_inc(maxT_loaded, 16)

            def load_ends(b, i):
                sp.wait_ge(out_stored[i % 2], BASE + (b * 2 + i // 2) * 16)
                sp.dma_start(pair_of(x_old, i), rows(x_pair, b * 4 + i)).then_inc(ends_loaded[i % 2], 16)
                sp.dma_start(pair_of(g_in, i), rows(g_pair, b * 4 + i)).then_inc(ends_loaded[i % 2], 16)

            def store_ends(b, i):
                sp.wait_ge(x_added, BASE + b * 4 + i + 1)
                sp.dma_start(rows(out_pair, b * 4 + i), pair_of(x_old, i)).then_inc(out_stored[i % 2], 16)

            def sequence(b, kind):
                more = kind != "last"
                if more:
                    load_x(b + 1, 0)
                if kind != "first":
                    load_stack(b, 1)
                    store_ends(b - 1, 2)
                    store_ends(b - 1, 3)
                else:
                    sp.wait_ge(xT_ready, BASE + 2 * KI)
                load_ends(b, 0)
                load_ends(b, 1)
                if more:
                    load_x(b + 1, 1)
                load_max(b, 1)
                if more:
                    store_parts(b + 1, 0)
                load_max(b, 2)
                if more:
                    load_stack(b + 1, 0)
                    store_parts(b + 1, 1)
                load_max(b, 3)
                store_ends(b, 0)
                if more:
                    load_max(b + 1, 0)
                store_ends(b, 1)
                load_ends(b, 2)
                load_ends(b, 3)

            for c in range(KI):
                store_parts(0, c)
                load_stack(0, c)
            load_max(0, 0)
            sequence(0, "first")
            with sp.Fori(1, B - 1) as b:
                sequence(b, "body")
            sequence(B - 1, "last")
            store_ends(B - 1, 2)
            store_ends(B - 1, 3)
            sp.wait_ge(out_stored[0], BASE + B * 32)
            sp.wait_ge(out_stored[1], BASE + B * 32)

        def rest_of(engine, b, c, n):
            no = (b * KI + c) * 4 + n
            w, cols = n // 2, slice((n % 2) * BANK, (n % 2 + 1) * BANK)
            engine.wait_ge(high_done, BASE + no + 1)
            engine.wait_ge(low_done, BASE + no - 1)
            engine.tensor_tensor(rest[:, n % 2], qk[:, n % 2], parts[:, w, 0, cols], ALU.subtract).then_inc(rest_done, 1)

        def low_part(engine, b, c, n):
            no = (b * KI + c) * 4 + n
            w, cols = n // 2, slice((n % 2) * BANK, (n % 2 + 1) * BANK)
            engine.wait_ge(mid_done, BASE + no + 1)
            engine.tensor_tensor(parts[:, w, 2, cols], rest[:, n % 2], parts[:, w, 1, cols],
                                 ALU.subtract).then_inc(low_done, 1)

        @block.gpsimd
        def _(pool):
            nc.gpsimd.memset(minus_half[:], -0.5).then_inc(const_set, 1)
            pool.wait_ge(const_set, BASE + 1)

            def inverse_deviation(b, u):
                pool.wait_ge(stats_done, BASE + (b * 2 + u) * 5 + 5)
                nc.gpsimd.tensor_tensor(rstd[:], var_eps[:], minus_half[:], ALU.pow).then_inc(rstd_done, 1)

            zero = pool.to_reg(0.0)

            def mask(b, g, s):
                at = s * HG % RP
                pool.wait_ge(exp_done, BASE + step_no(b, g, s) * HG + HG)
                pool.sem_inc(stood_alone, 1)
                block_ = probs[:, at:at + HG, 0:P]
                nc.gpsimd.affine_select(block_, block_, [[0, HG], [1, P]], ALU.is_ge, zero, base=0,
                                        channel_multiplier=-1).then_inc(masked, 1)

            def split_max(b, g):
                gn = group_no(b, g)
                pool.wait_ge(max_step, BASE + gn * 4 + 1)
                pool.wait_ge(maxT_ready, BASE + gn)
                pool.sem_inc(stood_alone, 1)
                top = max_parts[:].rearrange("p i h w -> p h i w")
                nc.gpsimd.tensor_copy(top[:, :, :, 0], max_tmp[:, 0]).then_inc(max_step, 1)
                pool.wait_ge(max_step, BASE + gn * 4 + 2)
                nc.gpsimd.tensor_tensor(max_tmp[:, 1], max_tmp[:, 0], top[:, :, :, 0], ALU.subtract).then_inc(max_step, 1)
                pool.wait_ge(max_step, BASE + gn * 4 + 3)
                pool.sem_inc(stood_alone, 1)
                nc.gpsimd.tensor_copy(top[:, :, :, 1], max_tmp[:, 1]).then_inc(max_step, 1)
                pool.wait_ge(max_step, BASE + gn * 4 + 4)
                nc.gpsimd.tensor_tensor(top[:, :, :, 2], max_tmp[:, 1], top[:, :, :, 1], ALU.subtract).then_inc(max_split, 1)

            def normalise(b, g, t):
                no = group_no(b, g) * 2 + t
                pool.wait_ge(inverted, BASE + no + 1)
                pool.wait_ge(turned_back, BASE + (b * KI + g // 2) * 2 + t - 1)
                nc.gpsimd.tensor_tensor(pair[:, t, :, g % 2], turned[:, :, 0:DH],
                                        inverse[:].unsqueeze(2).broadcast_to([P, BLKS, DH]),
                                        ALU.mult).then_inc(pair_done, 1)

            def low_attention(b, c, t):
                no = (b * KI + c) * 2 + t
                pool.wait_ge(attn_high, BASE + no + 1)
                cols = slice(t * BANK, (t + 1) * BANK)
                nc.gpsimd.tensor_tensor(attn[1][:, c, cols], attn_raw[:], attn[0][:, c, cols].bitcast(F32),
                                        ALU.subtract).then_inc(attn_ready, 1)

            def add(b, i):
                no = b * 4 + i
                pool.wait_ge(ends_loaded[i % 2], BASE + (b * 2 + i // 2 + 1) * 32)
                pool.wait_ge(s_done, BASE + no + 1)
                gate, new = flat(pair_of(g_in, i)), flat(pair_of(x_old, i))
                nc.gpsimd.tensor_tensor(gate, s_scaled[:, i % 2], gate, ALU.mult).then_inc(gated, 1)
                pool.wait_ge(gated, BASE + no + 1)
                nc.gpsimd.tensor_tensor(new, gate, new, ALU.add).then_inc(x_added, 1)

            def sequence(b, kind):
                at, last = small_work(kind), kind == "last"
                for g in range(GROUPS):
                    bg, gg = (b, g - 1) if g else (b - 1, GROUPS - 1)
                    for n in range(SLOTS):
                        item = at[g].get(n, ("",))
                        if not last and LN_WORK.get((g, n), ("",))[0] == "aggregate":
                            inverse_deviation(b + 1, LN_WORK[g, n][1])
                        if n == TURN_SLOT:
                            normalise(b, g, 0)
                        if n == TURN_SLOT - BEHIND and (g or kind != "first"):
                            normalise(bg, gg, 1)
                        if item[0] in ("q", "k"):
                            what, c, u = item
                            rest_of(pool, b + 1, c, (2 if what == "k" else 0) + u)
                        if g in (1, 2) and n in PART_SLOTS[g - 1] and not last:
                            low_part(pool, b + 1, g - 1, PART_SLOTS[g - 1].index(n))
                        if n == HIGH_SLOT and g % 2:
                            low_attention(b, g // 2, 0)
                        if n == HIGH_SLOT - BEHIND and (g == 2 or (g == 0 and kind != "first")):
                            low_attention(bg, gg // 2, 1)
                        if n == SPLIT_MAX_SLOT and not (last and g == GROUPS - 1):
                            split_max(b + (g + 1) // GROUPS, (g + 1) % GROUPS)
                        if item[0] == "o":
                            add(owner(item, b), item[1])
                        if n % HG == HG - 1 and n // HG in DIAGONAL:
                            mask(b, g, n // HG)

            inverse_deviation(0, 0)
            inverse_deviation(0, 1)
            nc.gpsimd.memset(v[:], 1.0).then_inc(const_set, 1)
            pool.wait_ge(rstd_done, BASE + 2)
            pool.wait_ge(const_set, BASE + 2)
            nc.gpsimd.memset(q_stack[SPLITS:P].bitcast(F32), 0.0).then_inc(const_set, 1)
            nc.gpsimd.memset(k_stack[SPLITS:P], 1.0).then_inc(const_set, 1)
            pool.wait_ge(const_set, BASE + 4)
            split_max(0, 0)
            sequence(0, "first")
            with pool.Fori(1, B - 1) as b:
                sequence(b, "body")
            sequence(B - 1, "last")
            normalise(B - 1, GROUPS - 1, 1)
            low_attention(B - 1, 1, 1)
            for _, i in OUTS:
                add(B - 1, i)

        @block.scalar
        def _(act):
            def take_xT(sec, it, b, u, ki):
                act.wait_ge(small_full, BASE + small_count(sec, it, ("x", u, ki)))
                nc.scalar.activation(xT[0][:, ki, u * BANK:(u + 1) * BANK], small_bank(sec, ("x", u, ki)),
                                     ACT.Copy).then_inc(xT_high, 1)

            def take_qk(sec, it, b, what, c, u):
                n = (2 if what == "k" else 0) + u
                no = (b * KI + c) * 4 + n
                act.wait_ge(small_full, BASE + small_count(sec, it, (what, c, u)))
                act.wait_ge(rest_done, BASE + no - 1)
                scale, bias = 1.0, 0.0
                if what == "q":
                    scale = s_qscale if layer == 0 else DH ** -0.5
                if biased:
                    at = (S_QB if what == "q" else S_KB) + c
                    bias = small[:, at:at + 1]
                src = small_bank(sec, (what, c, u))
                nc.scalar.activation(qk[:, n % 2], src, ACT.Identity, scale=scale, bias=bias).then_inc(qk_ready, 1)
                w, cols = n // 2, slice((n % 2) * BANK, (n % 2 + 1) * BANK)
                act.wait_ge(parts_stored, BASE + (b * KI + c) * 16)
                act.wait_ge(qk_ready, BASE + no + 1)
                nc.scalar.activation(parts[:, w, 0, cols], src, ACT.Identity, scale=scale,
                                     bias=bias).then_inc(high_done, 1)

            def middle_part(b, c, n):
                no = (b * KI + c) * 4 + n
                w, cols = n // 2, slice((n % 2) * BANK, (n % 2 + 1) * BANK)
                act.wait_ge(rest_done, BASE + no + 1)
                nc.scalar.activation(parts[:, w, 1, cols], rest[:, n % 2], ACT.Copy).then_inc(mid_done, 1)

            def take_v(sec, it, b, c, u):
                act.wait_ge(small_full, BASE + small_count(sec, it, ("v", c, u)))
                act.wait_ge(pv_done, BASE + step_no(b - 1, 2 * c + 1, len(STEPS) - 1) + 1)
                act.wait_ge(const_set, BASE + 2)
                dst = v[:, u * HT:(u + 1) * HT, c * HC:(c + 1) * HC, 0:DH]
                src = small_bank(sec, ("v", c, u)).rearrange("p (i h d) -> p i h d", i=HT, d=DH)
                nc.scalar.activation(dst, src, ACT.Copy).then_inc(v_ready, 1)

            def take_max(sec, it, b, g):
                act.wait_ge(small_full, BASE + small_count(sec, it, ("m", g)))
                act.wait_ge(maxT_loaded, BASE + group_no(b, g) * 64)
                src = ps_small[0:HG * MAXROWS, 0].bitcast(BF16)
                nc.scalar.activation(maxT[:], src, ACT.Copy).then_inc(maxT_ready, 1)

            def high_attention(b, c, t):
                act.wait_ge(turned_back, BASE + (b * KI + c) * 2 + t + 1)
                act.wait_ge(s_done, BASE + b * 4)
                nc.scalar.activation(attn[0][:, c, t * BANK:(t + 1) * BANK], attn_raw[:], ACT.Copy).then_inc(attn_high, 1)

            def exponential(b, g, n):
                s, h = n // HG, n % HG
                no = step_no(b, g, s) * HG + h
                _, w = width(*STEPS[s])
                act.wait_ge(exp_full, BASE + no + 1)
                act.wait_ge(pv_done, BASE + step_no(b, g, s) + 1 - RP // HG)
                nc.scalar.activation(probs[:, n % RP, 0:w], ps_exp[:, n % NE, 0:w], ACT.Exp).then_inc(exp_done, 1)

            def sequence(b, kind):
                at, last = small_work(kind), kind == "last"
                for g in range(GROUPS):
                    for n in range(SLOTS):
                        if n in at[g]:
                            small_item(kind, b, at[g][n], owner(at[g][n], b))
                        exponential(b, g, n)
                        if g in (1, 2) and n in PART_SLOTS[g - 1] and not last:
                            middle_part(b + 1, g - 1, PART_SLOTS[g - 1].index(n))
                        if n == HIGH_SLOT and g % 2:
                            high_attention(b, g // 2, 0)
                        if n == HIGH_SLOT - BEHIND:
                            if g == 2:
                                high_attention(b, 0, 1)
                            elif g == 0 and kind != "first":
                                high_attention(b - 1, 1, 1)

            def small_item(sec, it, key, b):
                kind = key[0]
                if kind == "x":
                    take_xT(sec, it, b, key[1], key[2])
                elif kind in "qk":
                    take_qk(sec, it, b, kind, key[1], key[2])
                elif kind == "v" and not biased:
                    take_v(sec, it, b, key[1], key[2])
                elif kind == "m":
                    take_max(sec, it, b, key[1])

            weights.scalar(act)
            for key in BEFORE:
                small_item("before", 0, key, 0)
                if key[0] in "qk":
                    middle_part(0, key[1], (2 if key[0] == "k" else 0) + key[2])
            sequence(0, "first")
            with act.Fori(1, B - 1) as b:
                sequence(b, "body")
            sequence(B - 1, "last")
            high_attention(B - 1, 1, 1)

        @block.vector
        def _(dve):
            nc.vector.memset(mask_add[:, 0:BANK - P], 0.0).then_inc(dve_set, 1)
            nc.vector.tensor_copy(mask_add[:, BANK - P:BANK], consts[:, C_MAXMASK:C_MAXMASK + P]).then_inc(dve_set, 1)
            nc.vector.tensor_copy(ident_b[:], ident).then_inc(dve_set, 1)
            nc.vector.memset(max_in[:], LOWEST).then_inc(dve_set, 1)
            dve.wait_ge(dve_set, BASE + 4)
            weights.ones(dve)

            def statistics(b, u, i, x_half=x_in, loaded=None):
                if i == 0:
                    dve.wait_ge(*(loaded or (x_loaded, BASE + (b * 2 + u) * 16)))
                nc.vector.bn_stats(bn[:, i], x_half[:, i]).then_inc(bn_done, 1)

            def aggregate(b, u):
                no = b * 2 + u
                dve.wait_ge(bn_done, BASE + no * 4 + 4)
                dve.sem_inc(stood_alone, 1)
                for i in range(HT):
                    nc.vector.bn_aggr(mv[:, i], bn[:, i]).then_inc(stats_done, 1)
                dve.wait_ge(stats_done, BASE + no * 5 + 4)
                nc.vector.tensor_scalar(var_eps[:], mv[:, :, 1], EPS_LN, None, ALU.add).then_inc(stats_done, 1)

            def norm(b, u, i, x_half=x_in):
                if i == 0:
                    dve.wait_ge(rstd_done, BASE + b * 2 + u + 1)
                ins = nc.vector.tensor_scalar(x_half[:, i], x_half[:, i], mv[:, i, 0:1], rstd[:, i:i + 1],
                                              ALU.subtract, ALU.mult)
                if i == HT - 1:
                    ins.then_inc(xn_done, 1)

            def low_xT(sec, it, b, u, ki):
                no = (b * 2 + u) * KI + ki
                dve.wait_ge(xT_high, BASE + no + 1)
                cols = slice(u * BANK, (u + 1) * BANK)
                nc.vector.tensor_tensor(xT[1][:, ki, cols], small_bank(sec, ("x", u, ki)), xT[0][:, ki, cols].bitcast(F32),
                                        ALU.subtract).then_inc(xT_ready, 1)

            def take_v(sec, it, b, c, u):
                dve.wait_ge(small_full, BASE + small_count(sec, it, ("v", c, u)))
                dve.wait_ge(pv_done, BASE + step_no(b - 1, 2 * c + 1, len(STEPS) - 1) + 1)
                dst = v[:, u * HT:(u + 1) * HT, c * HC:(c + 1) * HC, 0:DH]
                src = small_bank(sec, ("v", c, u)).rearrange("p (i h d) -> p i h d", i=HT, d=DH)
                for i in range(HT):
                    bias = small[:, S_VB + c * P:S_VB + (c + 1) * P].rearrange("p (h d) -> p h d", d=DH)
                    ins = nc.vector.tensor_tensor(dst[:, i], src[:, i], bias, ALU.add)
                ins.then_inc(v_ready, 1)

            def maximum(b, g, tile):
                no = group_no(b, g) * SLOTS + tile
                h, (i, piece) = tile // 12, PIECES[tile % 12]
                w = min((i + 1) * P - piece * BANK, BANK)
                if tile == 0:
                    dve.wait_ge(neg_step, BASE + group_no(b, g) - 1)
                dve.wait_ge(max_full, BASE + no + 1)
                out = max_in[:, g % 2, piece, h, i:i + 1]
                src = ps_max[:, tile % NM, 0:w]
                if i * P < (piece + 1) * BANK:
                    dve.sem_inc(stood_alone, 1)
                    nc.vector.tensor_tensor_reduce(junk[:, tile % NM, 0:w], src, mask_add[:, BANK - w:BANK], 1.0, LOWEST,
                                                   ALU.add, ALU.max, out).then_inc(max_taken, 1)
                else:
                    nc.vector.tensor_reduce(out, src, AX.X, ALU.max).then_inc(max_taken, 1)

            def negate_max(b, g):
                gn = group_no(b, g)
                dve.wait_ge(max_taken, BASE + (gn + 1) * SLOTS)
                dve.wait_ge(max_split, BASE + gn)
                nc.vector.scalar_tensor_tensor(max_tmp[:, 1], max_in[:, g % 2, 0], 1.0, max_in[:, g % 2, 1],
                                               ALU.mult, ALU.max).then_inc(neg_step, 1)
                dve.wait_ge(neg_step, BASE + gn + 1)
                nc.vector.tensor_scalar(max_tmp[:, 0], max_tmp[:, 1], -1.0, None, ALU.mult).then_inc(max_step, 1)

            def turn(b, g, t):
                no = group_no(b, g) * 2 + t
                dve.wait_ge(pv_done, BASE + step_no(b, g, 3 if t == 0 else 11) + 1)
                dve.wait_ge(pair_done, BASE + no)
                nc.vector.transpose(turned[:].rearrange("p k c -> p (k c)"), ps_pv[:, 0]).then_inc(pv_turned, 1)
                dve.wait_ge(pv_turned, BASE + no + 1)
                nc.vector.reciprocal(inverse[:], turned[:, :, DH]).then_inc(inverted, 1)

            def turn_back(b, c, t):
                dve.wait_ge(pair_done, BASE + group_no(b, 2 * c + 1) * 2 + t + 1)
                dve.wait_ge(attn_ready, BASE + (b * KI + c) * 2 + t)
                nc.vector.transpose(attn_raw[:], pair[:, t].rearrange("p k e d -> p (k e d)")).then_inc(turned_back, 1)

            def scale_out(sec, it, b, i):
                no = b * 4 + i
                dve.wait_ge(small_full, BASE + small_count(sec, it, ("o", i)))
                dve.wait_ge(gated, BASE + no - 1)
                out = s_scaled[:, i % 2]
                if biased:
                    bias = small[:, S_PB:S_PB + D]
                    for j in range(2):
                        ins = nc.vector.tensor_tensor(out[:, j * D:(j + 1) * D], ps_small[:, 0, j * D:(j + 1) * D],
                                                      bias, ALU.add)
                    ins.then_inc(s_done, 1)
                else:
                    nc.vector.tensor_scalar(out, ps_small[:, 0], gammas[:, 5:6], None, ALU.mult).then_inc(s_done, 1)

            def small_item(sec, it, key, b):
                kind = key[0]
                if kind == "x":
                    low_xT(sec, it, b, key[1], key[2])
                elif kind == "v" and biased:
                    take_v(sec, it, b, key[1], key[2])
                elif kind == "o":
                    scale_out(sec, it, b, key[1])

            def sequence(b, kind):
                at, last = small_work(kind), kind == "last"
                for g in range(GROUPS):
                    bg, gg = (b, g - 1) if g else (b - 1, GROUPS - 1)
                    for n in range(SLOTS):
                        if n in at[g]:
                            small_item(kind, b, at[g][n], owner(at[g][n], b))
                        if not last and (g, n) in LN_WORK:
                            what, u, i = LN_WORK[g, n]
                            if what == "statistics":
                                statistics(b + 1, u, i)
                            elif what == "aggregate":
                                aggregate(b + 1, u)
                            else:
                                norm(b + 1, u, i)
                        if n == TURN_SLOT:
                            turn(b, g, 0)
                        if n == BACK_SLOT and g % 2:
                            turn_back(b, g // 2, 0)
                        if n == TURN_SLOT - BEHIND and (g or kind != "first"):
                            turn(bg, gg, 1)
                        if n == BACK_SLOT - BEHIND and (g == 2 or (g == 0 and kind != "first")):
                            turn_back(bg, gg // 2, 1)
                        for ahead, mg, tile in lead_tiles(g, n, 0) + lead_tiles(g, n, 1):
                            if last and ahead:
                                continue
                            maximum(b + ahead, mg, tile)
                            if tile == SLOTS - 1:
                                negate_max(b + ahead, mg)

            for u, x_half in enumerate((x_in, x_old)):
                for i in range(HT):
                    statistics(0, u, i, x_half, ((x_loaded, x_1_loaded)[u], BASE + 16))
                aggregate(0, u)
                for i in range(HT):
                    norm(0, u, i, x_half)
            weights.vector_begin(dve)
            for n, (_, u, ki) in enumerate(NORM):
                low_xT("before", 0, 0, u, ki)
                if n < len(weights.pieces):
                    weights.vector(dve, n)
            for n in range(2 * 4):
                rest_of(dve, 0, n // 4, n % 4)
                low_part(dve, 0, n // 4, n % 4)
            dve.wait_ge(const_set, BASE + 2)
            for key in VALUES[0]:
                small_item("before", 0, key, 0)
            for tile in range(SLOTS):
                maximum(0, 0, tile)
            negate_max(0, 0)
            for tile in range(LEAD):
                maximum(0, 1, tile)
            sequence(0, "first")
            with dve.Fori(1, B - 1) as b:
                sequence(b, "body")
            sequence(B - 1, "last")
            turn(B - 1, GROUPS - 1, 1)
            turn_back(B - 1, 1, 1)
            for _, i in OUTS:
                scale_out("behind", B - 1, B - 1, i)

        @block.tensor
        def _(pe):
            def taken(item, b):
                kind = item[0]
                if kind == "x":
                    return xT_ready, (b * 2 + item[1]) * KI + item[2] + 1
                if kind in "qk":
                    return high_done, (b * KI + item[1]) * 4 + (2 if kind == "k" else 0) + item[2] + 1
                if kind == "v":
                    return v_ready, (b * KI + item[1]) * 2 + item[2] + 1
                if kind == "m":
                    return maxT_ready, group_no(b, item[1]) + 1
                return s_done, b * 4 + item[1] + 1

            def project(out, b, what, c, u):
                pe.wait_ge(xT_ready, BASE + (b + 1) * 2 * KI)
                for ki in range(KI):
                    for n, (wp, xp) in enumerate(passes):
                        ins = nc.tensor.matmul(out, w_parts[wp][:, "qk".index(what), ki, c * P:(c + 1) * P],
                                               xT[xp][:, ki, u * BANK:(u + 1) * BANK],
                                               start=(ki == 0 and n == 0), stop=(ki == KI - 1 and n == len(passes) - 1))
                ins.then_inc(small_full, 1)

            def values(out, c, u):
                for i in range(HT):
                    tile = slice((u * HT + i) * P, (u * HT + i + 1) * P)
                    for ki in range(KI):
                        for n, (wp, xp) in enumerate(passes):
                            ins = nc.tensor.matmul(out[:, i * P:(i + 1) * P], xT[xp][:, ki, tile],
                                                   w_parts[wp][:, 2, ki, c * P:(c + 1) * P],
                                                   start=(ki == 0 and n == 0),
                                                   stop=(ki == KI - 1 and n == len(passes) - 1))
                ins.then_inc(small_full, 1)

            def turn_x(out, b, u, ki, x_half=x_in):
                pe.wait_ge(xn_done, BASE + b * 2 + u + 1)
                for i in range(HT):
                    ins = nc.tensor.transpose(out[:, i * P:(i + 1) * P], x_half[:, i, ki * P:(ki + 1) * P], ident)
                ins.then_inc(small_full, 1)

            def turn_max(out, b, g):
                pe.wait_ge(max_split, BASE + group_no(b, g) + 1)
                to = out[0:HG * MAXROWS].bitcast(BF16)
                for i in range(TILES):
                    ins = nc.tensor.transpose(to[:, i * P:(i + 1) * P],
                                              max_parts[:, i].rearrange("p h w -> p (h w)"), ident_b[:])
                ins.then_inc(small_full, 1)

            def project_out(out, b, i):
                pe.wait_ge(attn_ready, BASE + (b * KI + KI - 1) * 2 + i // 2 + 1)
                for j in range(2):
                    tile = slice((2 * i + j) * P, (2 * i + j + 1) * P)
                    for c in range(KI):
                        for n, (wp, ap) in enumerate(passes):
                            ins = nc.tensor.matmul(out[:, j * D:(j + 1) * D], attn[ap][:, c, tile], w_out_parts[wp][:, c],
                                                   start=(c == 0 and n == 0),
                                                   stop=(c == KI - 1 and n == len(passes) - 1))
                ins.then_inc(small_full, 1)

            def small_item(item, b, before, section="body"):
                for it, bb in before:
                    s, count = taken(it, bb)
                    pe.wait_ge(s, BASE + count)
                out = small_bank(section, item)
                kind = item[0]
                if kind == "x":
                    turn_x(out, b, item[1], item[2], x_old if item[1] and section == "before" else x_in)
                elif kind in "qk":
                    project(out, b, kind, item[1], item[2])
                elif kind == "v":
                    values(out, item[1], item[2])
                elif kind == "m":
                    turn_max(out, b, item[1])
                else:
                    project_out(out, b, item[1])

            def max_tile(b, g, tile):
                no = group_no(b, g) * SLOTS + tile
                head, (i, piece) = g * HG + tile // 12, PIECES[tile % 12]
                w = min((i + 1) * P - piece * BANK, BANK)
                if tile == 0:
                    c = g // 2
                    pe.wait_ge(stack_loaded[c], BASE + (b + 1) * 192)
                pe.wait_ge(max_taken, BASE + no - NM + 1)
                nc.tensor.matmul(ps_max[:, tile % NM, 0:w], q_stack[0:MAX_AT, head, i * P:(i + 1) * P],
                                 k_stack[0:MAX_AT, head, piece * BANK:piece * BANK + w],
                                 start=True, stop=True).then_inc(max_full, 1)

            def scores(b, g, n):
                s, h = n // HG, n % HG
                t, j = STEPS[s]
                head = g * HG + h
                q0, w = width(t, j)
                no = step_no(b, g, s) * HG + h
                if n == 0:
                    pe.wait_ge(maxT_loaded, BASE + (group_no(b, g) + 1) * 64)
                pe.wait_ge(exp_done, BASE + no - NE + 1)
                nc.tensor.matmul(ps_exp[:, n % NE, 0:w], k_stack[:, head, j * P:(j + 1) * P],
                                 q_stack[:, head, q0:q0 + w], start=True, stop=True).then_inc(exp_full, 1)

            def weigh(b, g, s):
                t, j = STEPS[s]
                q0, w = width(t, j)
                first, last = s in (0, 4), s in (3, len(STEPS) - 1)
                if s in DIAGONAL:
                    pe.wait_ge(masked, BASE + group_no(b, g) * len(DIAGONAL) + DIAGONAL.index(s) + 1)
                else:
                    pe.wait_ge(exp_done, BASE + step_no(b, g, s) * HG + HG)
                if first:
                    pe.wait_ge(pv_turned, BASE + group_no(b, g) * 2 + t)
                    if t == 0:
                        pe.wait_ge(v_ready, BASE + (b * KI + g // 2 + 1) * 2)
                for h in range(HG):
                    ins = nc.tensor.matmul(ps_pv[h * VW:(h + 1) * VW, 0, q0 - t * BANK:q0 - t * BANK + w],
                                           v[:, j, g * HG + h], probs[:, (s * HG + h) % RP, 0:w],
                                           start=first, stop=last)
                ins.then_inc(pv_done, 1)

            def sequence(b, kind):
                at, last = small_work(kind), kind == "last"
                before = [(("m", 0), b)]
                for g in range(GROUPS):
                    for n in range(SLOTS):
                        if n in at[g]:
                            item = at[g][n]
                            small_item(item, owner(item, b), before)
                            before = [(item, owner(item, b))]
                        scores(b, g, n)
                        for part in range(2):
                            if part and weighed_at(n) is not None:
                                s = weighed_at(n)
                                if s >= 0:
                                    weigh(b, g, s)
                                elif g:
                                    weigh(b, g - 1, len(STEPS) + s)
                                elif kind != "first":
                                    weigh(b - 1, GROUPS - 1, len(STEPS) + s)
                            for ahead, mg, tile in lead_tiles(g, n, part):
                                if not (last and ahead):
                                    max_tile(b + ahead, mg, tile)

            pe.wait_ge(dve_set, BASE + 4)
            weights.tensor(pe)
            for n, item in enumerate(BEFORE[:-1]):
                if n == len(NORM):
                    weights.ready(pe)
                small_item(item, 0, [(BEFORE[n - 2], 0)] if n >= 2 else [], "before")
            pe.wait_ge(const_set, BASE + CONSTS_SET)
            for tile in range(SLOTS):
                max_tile(0, 0, tile)
            small_item(BEFORE[-1], 0, [(BEFORE[-3], 0)], "before")
            for tile in range(LEAD):
                max_tile(0, 1, tile)
            sequence(0, "first")
            with pe.Fori(1, B - 1) as b:
                sequence(b, "body")
            sequence(B - 1, "last")
            for n in range(WEIGH_LAG // HG, -1, -1):
                weigh(B - 1, GROUPS - 1, len(STEPS) - 1 - n)
            before = [(("o", 1), B - 1)]
            for item in OUTS:
                small_item(item, B - 1, before)
                before = [(item, B - 1)]


def build(nc, x, consts_dram, small_dram, a0_w, a0_wo, f0_up, f0_down, a1_w, a1_wo, f1_up, f1_down, out):
    known = {}
    g_dram = nc.dram_tensor("gate", [B * T, D], F32).ap()
    x1_dram = nc.dram_tensor("x_after_layer_0", [B * T, D], F32).ap()
    stack_dram = nc.dram_tensor("qk_parts", [KI, 2, 3, P, T], BF16).ap()
    with ExitStack() as ctx:
        consts = ctx.enter_context(nc.sbuf_tensor("consts", [P, C_END], F32))
        small = ctx.enter_context(nc.sbuf_tensor("small", [P, S_END], F32))
        gammas = ctx.enter_context(nc.sbuf_tensor("gammas", [P, 9], F32))
        with ExitStack() as c0:
            loaded = nc.alloc_semaphore("consts_loaded")
            bias_scaled = nc.alloc_semaphore("bias_scaled")
            block = c0.enter_context(nc.Block())

            @block.sync
            def _(sp):
                sp.dma_start(consts[:], consts_dram).then_inc(loaded, 16)
                sp.dma_start(small[:], small_dram).then_inc(loaded, 16)

            @block.vector
            def _(dve):
                dve.wait_ge(loaded, 32)
                q_bias = small[:, S_QB:S_QB + KI]
                nc.vector.tensor_scalar(q_bias, q_bias, DH ** -0.5, None, ALU.mult).then_inc(bias_scaled, 1)
                dve.wait_ge(bias_scaled, 1)

        with ExitStack() as c0:
            up = c0.enter_context(nc.sbuf_tensor("f0_up", [P, 2, KI, 6, P], F32R))
            down = c0.enter_context(nc.sbuf_tensor("f0_down", [P, 6, D], F32R))
            wide = KI * 6 * P
            count = HID[0] * D
            flat_up = up[:].rearrange("p w k c m -> p w (k c m)")
            weights = TernaryWeights(nc, "f0w", [(f0_up[:, 0:wide], wide, flat_up[:, 0]),
                                                 (f0_up[:, wide:2 * wide], wide, flat_up[:, 1]),
                                                 (f0_down, 6 * D, down[:].rearrange("p c d -> p (c d)"))],
                                     0.0, 1e-8, count, gammas, 6)
            ffn_pass(nc, known, 0, x, g_dram, weights, [up], [down], consts)
        with ExitStack() as c0:
            w = c0.enter_context(nc.sbuf_tensor("a0_w", [P, 3, KI, D], F32R))
            wo = c0.enter_context(nc.sbuf_tensor("a0_wo", [P, KI, D], F32R))
            wide = KI * D
            flat_w = w[:].rearrange("p w k m -> p w (k m)")
            weights = TernaryWeights(nc, "a0w", [(a0_w[:, i * wide:(i + 1) * wide], wide, flat_w[:, i]) for i in range(3)]
                                     + [(a0_wo, wide, wo[:].rearrange("p c d -> p (c d)"))],
                                     1e-5, 0.0, D * D, gammas, 0, scaled=True)
            attention_pass(nc, known, 0, x, g_dram, x1_dram, stack_dram, weights, [w], [wo], gammas, consts, small,
                           gammas[:, 4:5])
        with nc.Block() as block:
            @block.sync
            def _(sp):
                for s in known.values():
                    sp.sem_clear(s)

        with ExitStack() as c0:
            up = [c0.enter_context(nc.sbuf_tensor(f"f1_up{i}", [P, 2, KI, 8, P], F32R)) for i in range(2)]
            down = [c0.enter_context(nc.sbuf_tensor(f"f1_down{i}", [P, 8, D], F32R)) for i in range(2)]
            flat_up = [u[:].rearrange("p w k c m -> p (w k c m)") for u in up]
            flat_down = [d[:].rearrange("p c d -> p (c d)") for d in down]
            weights = SplitWeights(nc, "f1w", [(f1_up, 2 * KI * 8 * P, *flat_up), (f1_down, 8 * D, *flat_down)])
            ffn_pass(nc, known, 1, x1_dram, g_dram, weights, up, down, consts)
        with ExitStack() as c0:
            w = [c0.enter_context(nc.sbuf_tensor(f"a1_w{i}", [P, 3, KI, D], F32R)) for i in range(2)]
            wo = [c0.enter_context(nc.sbuf_tensor(f"a1_wo{i}", [P, KI, D], F32R)) for i in range(2)]
            flat_w = [u[:].rearrange("p w k m -> p (w k m)") for u in w]
            flat_wo = [u[:].rearrange("p c d -> p (c d)") for u in wo]
            weights = SplitWeights(nc, "a1w", [(a1_w, 3 * KI * D, *flat_w), (a1_wo, KI * D, *flat_wo)])
            attention_pass(nc, known, 1, x1_dram, g_dram, out, stack_dram, weights, w, wo, gammas, consts, small, None)


def laid_out(inputs):
    import numpy as np

    f = {k: np.asarray(v) for k, v in inputs.items()}

    def by_row(w):
        return w.reshape(-1, P, w.shape[1]).transpose(1, 0, 2)

    def out_rows(w):
        return w.reshape(KI, 2, HG, DH, D).transpose(2, 1, 3, 0, 4)

    def thirds(ws):
        return np.stack([by_row(w) for w in ws], 1)

    pad = 6 * P - HID[0]
    f0 = np.stack([by_row(np.pad(f[n].T, ((0, 0), (0, pad)))) for n in ("L0_ffn_w1", "L0_ffn_w2")], 1)
    f0d = by_row(np.pad(f["L0_ffn_w3"].T, ((0, pad), (0, 0))))

    def fours(w):
        k = by_row(w)
        return k.reshape(P, KI, 2, P, 4).transpose(0, 1, 2, 4, 3).reshape(P, KI, 8 * P)

    f1 = np.stack([fours(f[n]) for n in ("L1_ffn_w_gate", "L1_ffn_w_up")], 1)
    f1d = f["L1_ffn_w_down"].reshape(2, P, 4, D).transpose(1, 0, 2, 3)
    wa, ba = f["L1_attn_W_attn"], f["L1_attn_b_attn"]

    consts = np.zeros((P, C_END), np.float32)
    p, c = np.arange(P)[:, None], np.arange(P)[None, :]
    consts[:, C_IDENT:C_IDENT + P] = p == c
    consts[:, C_MAXMASK:C_END] = np.where(c > p, NEG, 0.0)
    small = np.zeros((P, S_END), ba.dtype)
    small[:, S_QB:S_QB + KI] = ba[0:D].reshape(KI, P).T
    small[:, S_KB:S_KB + KI] = ba[D:2 * D].reshape(KI, P).T
    small[:, S_VB:S_VB + D] = ba[None, 2 * D:]
    small[:, S_PB:S_PB + D] = f["L1_attn_b_proj"][None]

    def rows(a):
        return np.ascontiguousarray(a.reshape(P, -1))

    return {
        "x": f["L0_attn_x"].reshape(B * T, D), "consts": consts, "small": small,
        "a0_w": rows(thirds([f[f"L0_attn_w{n}"].T for n in "qkv"])), "a0_wo": rows(out_rows(f["L0_attn_wo"].T)),
        "f0_up": rows(f0), "f0_down": rows(f0d),
        "a1_w": rows(thirds([wa[:, i * D:(i + 1) * D] for i in range(3)])), "a1_wo": rows(out_rows(f["L1_attn_W_proj"])),
        "f1_up": rows(f1), "f1_down": rows(f1d),
    }


def kernel(**inputs):
    import numpy as _np
    import concourse.bacc as _bacc
    from concourse import mybir as _mybir
    from concourse.bass_utils import run_bass_kernel_spmd as _run

    nc = _bacc.Bacc("TRN2", target_bir_lowering=False, num_devices=1)
    arrays, args = {}, []
    for name, a in laid_out(inputs).items():
        a = _np.ascontiguousarray(a)
        arrays[f"in_{name}"] = a
        args.append(nc.dram_tensor(f"in_{name}", a.shape, _mybir.dt.from_np(a.dtype), kind="ExternalInput").ap())
    out = nc.dram_tensor("out_x", (B * T, D), F32, kind="ExternalOutput").ap()
    build(nc, *args, out)
    r = _run(nc, [arrays], core_ids=[0])
    return r.results[0]["out_x"].reshape(B, T, D)
```
